# Optimizing a Trainium2 kernel written in Bass

```python
import numpy as np
import jax
import jax.numpy as jnp

def _softmax(x, axis=-1):
    return jax.nn.softmax(x, axis=axis)
def _gelu(x):
    return jax.nn.gelu(x, approximate=True)
def _silu(x):
    return jax.nn.silu(x)
def _sigmoid(x):
    return jax.nn.sigmoid(x)
def _layernorm(x, axis=-1, eps=1e-5):
    m = jnp.mean(x, axis=axis, keepdims=True)
    v = jnp.var(x, axis=axis, keepdims=True)
    return (x - m) / jnp.sqrt(v + eps)
def _scatter_add(tgt, idx, src, axis=0):
    return tgt.at[idx].add(src)
def _segment_sum(src, seg, n):
    return jax.ops.segment_sum(src, seg, n)

kernel_name = 'mk_conv_attn_hybrid_d4_conv_nchw128_4106bd'

def setup_inputs(seed: int = 0):
    np.random.seed(seed)
    _w = jnp.asarray
    def _rec_inputs():
        import jax
        import jax.numpy as jnp
        _gk = jax.random.key(seed)
        x = -0.000929 + 1 * jax.random.normal(jax.random.fold_in(_gk, 1), (2, 128, 64, 64), jnp.float32)
        return x
    x = _rec_inputs()
    def _L0_conv_setup():
        import jax, jax.numpy as jnp
        import numpy as np
        NUM_HEADS = 4
        KERNEL = 7
        EPS = 1e-05

        def _na2d(x, w_qkv, b_qkv, rpb, w_p, b_p):
            B, H, W, C = x.shape
            h, k = (NUM_HEADS, KERNEL)
            d = C // h
            qkv = (x @ w_qkv.T + b_qkv).reshape(B, H, W, 3, h, d)
            q = qkv[..., 0, :, :] * d ** (-0.5)
            kk = qkv[..., 1, :, :]
            v = qkv[..., 2, :, :]
            si = jnp.clip(jnp.arange(H) - k // 2, 0, H - k)
            sj = jnp.clip(jnp.arange(W) - k // 2, 0, W - k)
            idx_i = si[:, None] + jnp.arange(k)
            idx_j = sj[:, None] + jnp.arange(k)

            def win(t):
                t = t[:, idx_i]
                t = t[:, :, :, idx_j]
                return jnp.transpose(t, (0, 1, 3, 2, 4, 5, 6))
            kw = win(kk)
            vw = win(v)
            attn = jnp.einsum('bijhd,bijpqhd->bijhpq', q, kw)
            bi = jnp.arange(k)[None, :] + (k - 1) - (jnp.arange(H) - si)[:, None]
            bj = jnp.arange(k)[None, :] + (k - 1) - (jnp.arange(W) - sj)[:, None]
            bias = rpb[:, bi[:, None, :, None], bj[None, :, None, :]]
            attn = attn + jnp.transpose(bias, (1, 2, 0, 3, 4))[None]
            attn = jax.nn.softmax(attn.reshape(B, H, W, h, k * k), axis=-1).reshape(B, H, W, h, k, k)
            out = jnp.einsum('bijhpq,bijpqhd->bijhd', attn, vw).reshape(B, H, W, C)
            return out @ w_p.T + b_p
        key = jax.random.key(seed)
        ks = jax.random.split(key, 6)
        C, depth = (128, 2)
        x = jax.random.normal(ks[0], (2, C, 64, 64), jnp.float32)
        qkv_w = jax.random.normal(ks[1], (depth, 3 * C, C), jnp.float32) * 0.05
        qkv_b = jnp.zeros((depth, 3 * C), jnp.float32)
        rpb = jax.random.normal(ks[2], (depth, NUM_HEADS, 2 * KERNEL - 1, 2 * KERNEL - 1), jnp.float32) * 0.02
        proj_w = jax.random.normal(ks[3], (depth, C, C), jnp.float32) * 0.05
        proj_b = jnp.zeros((depth, C), jnp.float32)
        ln_g = jnp.ones((C,), jnp.float32)
        ln_b = jnp.zeros((C,), jnp.float32)
        return dict(x=x, qkv_w=qkv_w, qkv_b=qkv_b, rpb=rpb, proj_w=proj_w, proj_b=proj_b, ln_g=ln_g, ln_b=ln_b)
    _L0_conv_all = _L0_conv_setup()
    _L0_conv_in = {k: v for k, v in _L0_conv_all.items() if k in ('qkv_w', 'qkv_b', 'rpb', 'proj_w', 'proj_b', 'ln_g', 'ln_b', )}
    del _L0_conv_all

    def _L1_conv_setup():
        import jax, jax.numpy as jnp
        import numpy as np
        NUM_HEADS = 4
        K = 3
        K2 = K * K
        PAD = K // 2

        def _unfold(x, H, W):
            xp = jnp.pad(x, ((0, 0), (0, 0), (PAD, PAD), (PAD, PAD)))
            return jnp.stack([xp[:, :, i:i + H, j:j + W] for i in range(K) for j in range(K)], axis=2)
        key = jax.random.key(seed)
        ks = jax.random.split(key, 5)
        B, C, H, W = (8, 128, 64, 64)
        x = jax.random.normal(ks[0], (B, C, H, W), jnp.float32)
        w_qkv = jax.random.normal(ks[1], (3 * C, C), jnp.float32) * 0.05
        w_kernel = jax.random.normal(ks[2], (NUM_HEADS * K2, 3 * C // NUM_HEADS), jnp.float32) * 0.05
        b_kernel = jnp.zeros((NUM_HEADS * K2,), jnp.float32)
        w_proj = jax.random.normal(ks[3], (C, C), jnp.float32) * 0.05
        alpha = jnp.asarray(0.5, jnp.float32)
        beta = jnp.asarray(0.5, jnp.float32)
        return {'x': x, 'w_qkv': w_qkv, 'w_kernel': w_kernel, 'b_kernel': b_kernel, 'w_proj': w_proj, 'alpha': alpha, 'beta': beta}
    _L1_conv_all = _L1_conv_setup()
    _L1_conv_in = {k: v for k, v in _L1_conv_all.items() if k in ('w_qkv', 'w_kernel', 'b_kernel', 'w_proj', 'alpha', 'beta', )}
    del _L1_conv_all

    def _L2_attn_setup():
        import jax, jax.numpy as jnp
        import numpy as np
        B, N, D = (4, 1024, 128)
        key = jax.random.key(seed)
        ks = jax.random.split(key, 4)
        scale = 1.0 / np.sqrt(D)
        return {'inputs': jax.random.normal(ks[0], (B, N, D), dtype=jnp.float32), 'Wq': jax.random.normal(ks[1], (D, D), dtype=jnp.float32) * scale, 'bq': jnp.zeros((D,), dtype=jnp.float32), 'Wk': jax.random.normal(ks[2], (D, D), dtype=jnp.float32) * scale, 'bk': jnp.zeros((D,), dtype=jnp.float32), 'Wv': jax.random.normal(ks[3], (D, D), dtype=jnp.float32) * scale, 'bv': jnp.zeros((D,), dtype=jnp.float32)}
    _L2_attn_all = _L2_attn_setup()
    _L2_attn_in = {k: v for k, v in _L2_attn_all.items() if k in ('Wq', 'bq', 'Wk', 'bk', 'Wv', 'bv', )}
    del _L2_attn_all

    def _L2_ffn_setup():
        import jax, jax.numpy as jnp
        import numpy as np
        PADDED_SL = 8192
        TEMPERATURE = 1.0
        SIGMA_POW = 0.25

        def _stu_conv(phi, u, n):
            b, sl, d = u.shape
            sgn = jnp.where(jnp.arange(sl) % 2 == 0, 1.0, -1.0).astype(u.dtype)
            sgn3 = sgn[None, :, None]
            Vf = jnp.fft.rfft(phi, n=n, axis=0)
            Uf_p = jnp.fft.rfft(u, n=n, axis=1)
            Uf_m = jnp.fft.rfft(u * sgn3, n=n, axis=1)
            U_plus = jnp.fft.irfft(Vf[None, :, :, None] * Uf_p[:, :, None, :], n=n, axis=1)[:, :sl]
            U_minus = jnp.fft.irfft(Vf[None, :, :, None] * Uf_m[:, :, None, :], n=n, axis=1)[:, :sl]
            U_minus = U_minus * sgn[None, :, None, None]
            return (U_plus, U_minus)

        def _compute_spectral(u, sigma, phi, Mpp, Mpm):
            U_plus, U_minus = _stu_conv(phi, u, PADDED_SL)
            s = sigma ** SIGMA_POW
            out = jnp.einsum('btkd,k,kde->bte', U_plus, s, Mpp)
            out = out + jnp.einsum('btkd,k,kde->bte', U_minus, s, Mpm)
            return out

        def _compute_ar_u(Mu, u):
            sl = u.shape[1]
            out = jnp.zeros(u.shape[:2] + (Mu.shape[-1],), dtype=u.dtype)
            for i in range(Mu.shape[0]):
                ui = jnp.pad(u, ((0, 0), (i, 0), (0, 0)))[:, :sl]
                out = out + jnp.einsum('btd,de->bte', ui, Mu[i])
            return out

        def _stu(u, sigma, phi, Mu, Mpp, Mpm):
            return _compute_spectral(u, sigma, phi, Mpp, Mpm) + _compute_ar_u(Mu, u)
        key = jax.random.key(seed)
        ks = jax.random.split(key, 8)
        b, sl, d, K, k_u = (2, 4096, 128, 16, 3)
        x = jax.random.normal(ks[0], (b, sl, d), dtype=jnp.float32)
        sigma = jax.random.uniform(ks[1], (K,), dtype=jnp.float32, minval=0.001, maxval=1.0)
        phi = jax.random.normal(ks[2], (sl, K), dtype=jnp.float32) / np.sqrt(sl)
        M_u = jax.random.normal(ks[3], (4, k_u, d, d), dtype=jnp.float32) * 0.02
        M_phi_plus = jax.random.normal(ks[4], (4, K, d, d), dtype=jnp.float32) * 0.02
        M_phi_minus = jax.random.normal(ks[5], (4, K, d, d), dtype=jnp.float32) * 0.02
        log_weights = jnp.ones((4,), dtype=jnp.float32)
        u01 = jax.random.uniform(ks[6], (4,), dtype=jnp.float32, minval=1e-06, maxval=1.0 - 1e-06)
        gumbel = -jnp.log(-jnp.log(u01))
        return {'x': x, 'sigma': sigma, 'phi': phi, 'M_u': M_u, 'M_phi_plus': M_phi_plus, 'M_phi_minus': M_phi_minus, 'log_weights': log_weights, 'gumbel': gumbel}
    _L2_ffn_all = _L2_ffn_setup()
    _L2_ffn_in = {k: v for k, v in _L2_ffn_all.items() if k in ('sigma', 'phi', 'M_u', 'M_phi_plus', 'M_phi_minus', 'log_weights', 'gumbel', )}
    del _L2_ffn_all

    def _L3_attn_setup():
        import jax, jax.numpy as jnp
        import numpy as np
        B, T, C = (16, 2048, 128)
        HEAD_SIZE = 128
        key = jax.random.key(seed)
        k1, k2, k3, k4 = jax.random.split(key, 4)
        x = jax.random.normal(k1, (B, T, C), dtype=jnp.float32)
        scale = (1.0 / np.sqrt(C)).astype(np.float32)
        Wq = jax.random.normal(k2, (HEAD_SIZE, C), dtype=jnp.float32) * scale
        Wk = jax.random.normal(k3, (HEAD_SIZE, C), dtype=jnp.float32) * scale
        Wv = jax.random.normal(k4, (HEAD_SIZE, C), dtype=jnp.float32) * scale
        return {'x': x, 'Wq': Wq, 'Wk': Wk, 'Wv': Wv}
    _L3_attn_all = _L3_attn_setup()
    _L3_attn_in = {k: v for k, v in _L3_attn_all.items() if k in ('Wq', 'Wk', 'Wv', )}
    del _L3_attn_all

    def _L3_ffn_setup():
        import jax, jax.numpy as jnp
        import numpy as np
        B, N, D, C, E, K = (8, 8192, 128, 128, 8, 2)
        key = jax.random.key(seed)
        k0, k1, k2 = jax.random.split(key, 3)
        x = jax.random.normal(k0, (B, N, D), dtype=jnp.float32)
        router_w = jax.random.normal(k1, (D, E), dtype=jnp.float32) * 0.05
        router_b = jnp.zeros((E,), dtype=jnp.float32)
        expert_w = jax.random.normal(k2, (E, D, C), dtype=jnp.float32) * (1.0 / np.sqrt(D))
        expert_b = jnp.zeros((E, C), dtype=jnp.float32)
        return {'x': x, 'router_w': router_w, 'router_b': router_b, 'expert_w': expert_w, 'expert_b': expert_b}
    _L3_ffn_all = _L3_ffn_setup()
    _L3_ffn_in = {k: v for k, v in _L3_ffn_all.items() if k in ('router_w', 'router_b', 'expert_w', 'expert_b', )}
    del _L3_ffn_all

    return {
        "x": x,
        "L0_conv_qkv_w": _L0_conv_in["qkv_w"],
        "L0_conv_qkv_b": _L0_conv_in["qkv_b"],
        "L0_conv_rpb": _L0_conv_in["rpb"],
        "L0_conv_proj_w": _L0_conv_in["proj_w"],
        "L0_conv_proj_b": _L0_conv_in["proj_b"],
        "L0_conv_ln_g": _L0_conv_in["ln_g"],
        "L0_conv_ln_b": _L0_conv_in["ln_b"],
        "L1_conv_w_qkv": _L1_conv_in["w_qkv"],
        "L1_conv_w_kernel": _L1_conv_in["w_kernel"],
        "L1_conv_b_kernel": _L1_conv_in["b_kernel"],
        "L1_conv_w_proj": _L1_conv_in["w_proj"],
        "L1_conv_alpha": _L1_conv_in["alpha"],
        "L1_conv_beta": _L1_conv_in["beta"],
        "L2_attn_Wq": _L2_attn_in["Wq"],
        "L2_attn_bq": _L2_attn_in["bq"],
        "L2_attn_Wk": _L2_attn_in["Wk"],
        "L2_attn_bk": _L2_attn_in["bk"],
        "L2_attn_Wv": _L2_attn_in["Wv"],
        "L2_attn_bv": _L2_attn_in["bv"],
        "L2_ffn_sigma": _L2_ffn_in["sigma"],
        "L2_ffn_phi": _L2_ffn_in["phi"],
        "L2_ffn_M_u": _L2_ffn_in["M_u"],
        "L2_ffn_M_phi_plus": _L2_ffn_in["M_phi_plus"],
        "L2_ffn_M_phi_minus": _L2_ffn_in["M_phi_minus"],
        "L2_ffn_log_weights": _L2_ffn_in["log_weights"],
        "L2_ffn_gumbel": _L2_ffn_in["gumbel"],
        "L3_attn_Wq": _L3_attn_in["Wq"],
        "L3_attn_Wk": _L3_attn_in["Wk"],
        "L3_attn_Wv": _L3_attn_in["Wv"],
        "L3_ffn_router_w": _L3_ffn_in["router_w"],
        "L3_ffn_router_b": _L3_ffn_in["router_b"],
        "L3_ffn_expert_w": _L3_ffn_in["expert_w"],
        "L3_ffn_expert_b": _L3_ffn_in["expert_b"],
    }

def reference(x, L0_conv_qkv_w, L0_conv_qkv_b, L0_conv_rpb, L0_conv_proj_w, L0_conv_proj_b, L0_conv_ln_g, L0_conv_ln_b, L1_conv_w_qkv, L1_conv_w_kernel, L1_conv_b_kernel, L1_conv_w_proj, L1_conv_alpha, L1_conv_beta, L2_attn_Wq, L2_attn_bq, L2_attn_Wk, L2_attn_bk, L2_attn_Wv, L2_attn_bv, L2_ffn_sigma, L2_ffn_phi, L2_ffn_M_u, L2_ffn_M_phi_plus, L2_ffn_M_phi_minus, L2_ffn_log_weights, L2_ffn_gumbel, L3_attn_Wq, L3_attn_Wk, L3_attn_Wv, L3_ffn_router_w, L3_ffn_router_b, L3_ffn_expert_w, L3_ffn_expert_b):
    import jax
    import jax.numpy as jnp
    def _L0_conv_ref(x, qkv_w, qkv_b, rpb, proj_w, proj_b, ln_g, ln_b):
        import jax, jax.numpy as jnp
        import numpy as np
        NUM_HEADS = 4
        KERNEL = 7
        EPS = 1e-05

        def _na2d(x, w_qkv, b_qkv, rpb, w_p, b_p):
            B, H, W, C = x.shape
            h, k = (NUM_HEADS, KERNEL)
            d = C // h
            qkv = (x @ w_qkv.T + b_qkv).reshape(B, H, W, 3, h, d)
            q = qkv[..., 0, :, :] * d ** (-0.5)
            kk = qkv[..., 1, :, :]
            v = qkv[..., 2, :, :]
            si = jnp.clip(jnp.arange(H) - k // 2, 0, H - k)
            sj = jnp.clip(jnp.arange(W) - k // 2, 0, W - k)
            idx_i = si[:, None] + jnp.arange(k)
            idx_j = sj[:, None] + jnp.arange(k)

            def win(t):
                t = t[:, idx_i]
                t = t[:, :, :, idx_j]
                return jnp.transpose(t, (0, 1, 3, 2, 4, 5, 6))
            kw = win(kk)
            vw = win(v)
            attn = jnp.einsum('bijhd,bijpqhd->bijhpq', q, kw)
            bi = jnp.arange(k)[None, :] + (k - 1) - (jnp.arange(H) - si)[:, None]
            bj = jnp.arange(k)[None, :] + (k - 1) - (jnp.arange(W) - sj)[:, None]
            bias = rpb[:, bi[:, None, :, None], bj[None, :, None, :]]
            attn = attn + jnp.transpose(bias, (1, 2, 0, 3, 4))[None]
            attn = jax.nn.softmax(attn.reshape(B, H, W, h, k * k), axis=-1).reshape(B, H, W, h, k, k)
            out = jnp.einsum('bijhpq,bijpqhd->bijhd', attn, vw).reshape(B, H, W, C)
            return out @ w_p.T + b_p
        y = jnp.transpose(x, (0, 2, 3, 1))
        for l in range(qkv_w.shape[0]):
            y = _na2d(y, qkv_w[l], qkv_b[l], rpb[l], proj_w[l], proj_b[l])
        mu = y.mean(-1, keepdims=True)
        var = y.var(-1, keepdims=True)
        y = (y - mu) / jnp.sqrt(var + EPS) * ln_g + ln_b
        return jnp.transpose(y, (0, 3, 1, 2))

    def _L1_conv_ref(x, w_qkv, w_kernel, b_kernel, w_proj, alpha, beta):
        import jax, jax.numpy as jnp
        import numpy as np
        NUM_HEADS = 4
        K = 3
        K2 = K * K
        PAD = K // 2

        def _unfold(x, H, W):
            xp = jnp.pad(x, ((0, 0), (0, 0), (PAD, PAD), (PAD, PAD)))
            return jnp.stack([xp[:, :, i:i + H, j:j + W] for i in range(K) for j in range(K)], axis=2)
        B, C, H, W = x.shape
        L = H * W
        hd = C // NUM_HEADS
        qkv = jnp.einsum('oc,bchw->bohw', w_qkv, x)
        q, k, v = jnp.split(qkv, 3, axis=1)
        q_flat = q.reshape(B, NUM_HEADS, hd, L)
        k_patch = _unfold(k, H, W).reshape(B, NUM_HEADS, hd, K2, L)
        v_patch = _unfold(v, H, W).reshape(B, NUM_HEADS, hd, K2, L)
        logits = jnp.einsum('bhdl,bhdkl->bhkl', q_flat, k_patch)
        attn = jax.nn.softmax(logits, axis=2)
        attn_out = jnp.einsum('bhkl,bhdkl->bhdl', attn, v_patch).reshape(B, C, H, W)
        G = NUM_HEADS
        cg = 3 * C // G
        qkv_g = qkv.reshape(B, G, cg, L)
        wk = w_kernel.reshape(G, K2, cg)
        kernel = jnp.einsum('bgcl,gkc->bgkl', qkv_g, wk) + b_kernel.reshape(1, G, K2, 1)
        conv_out = jnp.einsum('bhkl,bhdkl->bhdl', kernel, v_patch).reshape(B, C, H, W)
        out = alpha * attn_out + beta * conv_out
        out = jnp.einsum('oc,bchw->bohw', w_proj, out)
        return out

    def _L2_attn_ref(inputs, Wq, bq, Wk, bk, Wv, bv):
        import jax, jax.numpy as jnp
        import numpy as np
        B, N, D = (4, 1024, 128)
        q = inputs @ Wq + bq
        k = inputs @ Wk + bk
        v = inputs @ Wv + bv
        kv = jnp.sum(k * v, axis=1, keepdims=True)
        return q * kv

    def _L2_ffn_ref(x, sigma, phi, M_u, M_phi_plus, M_phi_minus, log_weights, gumbel):
        import jax, jax.numpy as jnp
        import numpy as np
        PADDED_SL = 8192
        TEMPERATURE = 1.0
        SIGMA_POW = 0.25

        def _stu_conv(phi, u, n):
            b, sl, d = u.shape
            sgn = jnp.where(jnp.arange(sl) % 2 == 0, 1.0, -1.0).astype(u.dtype)
            sgn3 = sgn[None, :, None]
            Vf = jnp.fft.rfft(phi, n=n, axis=0)
            Uf_p = jnp.fft.rfft(u, n=n, axis=1)
            Uf_m = jnp.fft.rfft(u * sgn3, n=n, axis=1)
            U_plus = jnp.fft.irfft(Vf[None, :, :, None] * Uf_p[:, :, None, :], n=n, axis=1)[:, :sl]
            U_minus = jnp.fft.irfft(Vf[None, :, :, None] * Uf_m[:, :, None, :], n=n, axis=1)[:, :sl]
            U_minus = U_minus * sgn[None, :, None, None]
            return (U_plus, U_minus)

        def _compute_spectral(u, sigma, phi, Mpp, Mpm):
            U_plus, U_minus = _stu_conv(phi, u, PADDED_SL)
            s = sigma ** SIGMA_POW
            out = jnp.einsum('btkd,k,kde->bte', U_plus, s, Mpp)
            out = out + jnp.einsum('btkd,k,kde->bte', U_minus, s, Mpm)
            return out

        def _compute_ar_u(Mu, u):
            sl = u.shape[1]
            out = jnp.zeros(u.shape[:2] + (Mu.shape[-1],), dtype=u.dtype)
            for i in range(Mu.shape[0]):
                ui = jnp.pad(u, ((0, 0), (i, 0), (0, 0)))[:, :sl]
                out = out + jnp.einsum('btd,de->bte', ui, Mu[i])
            return out

        def _stu(u, sigma, phi, Mu, Mpp, Mpm):
            return _compute_spectral(u, sigma, phi, Mpp, Mpm) + _compute_ar_u(Mu, u)
        T = x.shape[1]
        outs = []
        for i, frac in enumerate((1, 2, 4, 8)):
            xi = x[:, :T // frac]
            si = _stu(xi, sigma, phi, M_u[i], M_phi_plus[i], M_phi_minus[i])
            si = jnp.pad(si, ((0, 0), (0, T - si.shape[1]), (0, 0)))
            outs.append(si)
        y_soft = jax.nn.softmax((log_weights + gumbel) / TEMPERATURE)
        y_hard = jax.nn.one_hot(jnp.argmax(y_soft), 4, dtype=y_soft.dtype)
        weights = y_hard - jax.lax.stop_gradient(y_soft) + y_soft
        stacked = jnp.stack(outs, axis=-1)
        return jnp.sum(stacked * weights, axis=-1)

    def _L3_attn_ref(x, Wq, Wk, Wv):
        import jax, jax.numpy as jnp
        import numpy as np
        B, T, C = (16, 2048, 128)
        HEAD_SIZE = 128
        Bd, Td, Cd = x.shape
        q = jnp.einsum('btc,hc->bth', x, Wq)
        k = jnp.einsum('btc,hc->bth', x, Wk)
        v = jnp.einsum('btc,hc->bth', x, Wv)
        scores = jnp.einsum('bth,bsh->bts', q, k) * Cd ** (-0.5)
        causal = jnp.tril(jnp.ones((Td, Td), dtype=bool))
        scores = jnp.where(causal, scores, -jnp.inf)
        attn = jax.nn.softmax(scores, axis=-1)
        out = jnp.einsum('bts,bsh->bth', attn, v)
        return out

    def _L3_ffn_ref(x, router_w, router_b, expert_w, expert_b):
        import jax, jax.numpy as jnp
        import numpy as np
        B, N, D, C, E, K = (8, 8192, 128, 128, 8, 2)
        router_probs = jax.nn.softmax(x @ router_w + router_b, axis=-1)
        top_p, top_i = jax.lax.top_k(router_probs, K)
        top_p = top_p / jnp.sum(top_p, axis=-1, keepdims=True)
        expert_out = jnp.einsum('bnd,edc->bnec', x, expert_w) + expert_b
        gathered = jnp.take_along_axis(expert_out, top_i[..., None], axis=2)
        return jnp.einsum('bnk,bnkc->bnc', top_p, gathered)

    def _gn(v, G=32, eps=1e-5):
        B_, C_, H_, W_ = v.shape
        g = v.reshape(B_, G, C_ // G, H_, W_)
        m = jnp.mean(g, axis=(2, 3, 4), keepdims=True)
        s = jnp.var(g, axis=(2, 3, 4), keepdims=True)
        return ((g - m) / jnp.sqrt(s + eps)).reshape(v.shape)

    def _ln_c(v, eps=1e-6):
        m = jnp.mean(v, axis=1, keepdims=True)
        s = jnp.var(v, axis=1, keepdims=True)
        return (v - m) / jnp.sqrt(s + eps)

    def _ln_t(v, eps=1e-5):
        m = jnp.mean(v, axis=-1, keepdims=True)
        s = jnp.var(v, axis=-1, keepdims=True)
        return (v - m) / jnp.sqrt(s + eps)

    def _to_tokens(v):
        B_, C_, H_, W_ = v.shape
        return v.reshape(B_, C_, H_ * W_).transpose(0, 2, 1)
    def _from_tokens(t, like):
        B_, C_, H_, W_ = like.shape
        return t.transpose(0, 2, 1).reshape(B_, C_, H_, W_)

    x = x + _L0_conv_ref(_gn(x), L0_conv_qkv_w, L0_conv_qkv_b, L0_conv_rpb, L0_conv_proj_w, L0_conv_proj_b, L0_conv_ln_g, L0_conv_ln_b)
    x = x + _L1_conv_ref(_gn(x), L1_conv_w_qkv, L1_conv_w_kernel, L1_conv_b_kernel, L1_conv_w_proj, L1_conv_alpha, L1_conv_beta)
    t = _to_tokens(x)
    t = t + _L2_attn_ref(_ln_t(t), L2_attn_Wq, L2_attn_bq, L2_attn_Wk, L2_attn_bk, L2_attn_Wv, L2_attn_bv)
    t = t + _L2_ffn_ref(_ln_t(t), L2_ffn_sigma, L2_ffn_phi, L2_ffn_M_u, L2_ffn_M_phi_plus, L2_ffn_M_phi_minus, L2_ffn_log_weights, L2_ffn_gumbel)
    t = t + _L3_attn_ref(_ln_t(t), L3_attn_Wq, L3_attn_Wk, L3_attn_Wv)
    t = t + _L3_ffn_ref(_ln_t(t), L3_ffn_router_w, L3_ffn_router_b, L3_ffn_expert_w, L3_ffn_expert_b)
    x = _from_tokens(t, x)
    return x


_drawn_inputs = setup_inputs


def setup_inputs(seed=0):
    import zlib

    import numpy as np

    out = dict(_drawn_inputs(seed))
    spreads = {'L0_conv_qkv_b': (0.0, 0.1),
     'L0_conv_proj_b': (0.0, 0.1),
     'L0_conv_ln_g': (1.0, 0.2),
     'L0_conv_ln_b': (0.0, 0.1),
     'L1_conv_b_kernel': (0.0, 0.1),
     'L2_attn_bq': (0.0, 0.1),
     'L2_attn_bk': (0.0, 0.1),
     'L2_attn_bv': (0.0, 0.1),
     'L2_ffn_log_weights': (1.0, 0.2),
     'L3_ffn_router_b': (0.0, 2.0),
     'L3_ffn_expert_b': (0.0, 2.0)}
    factors = {'L0_conv_rpb': 64.0,
     'L2_ffn_sigma': 33.472,
     'L2_ffn_phi': 8.0,
     'L2_ffn_M_u': 194.634,
     'L2_ffn_M_phi_plus': 8.0,
     'L2_ffn_M_phi_minus': 8.0,
     'L2_ffn_gumbel': 8.0,
     'L3_attn_Wq': 64.0,
     'L3_attn_Wk': 64.0,
     'L3_attn_Wv': 64.0,
     'L3_ffn_router_w': 64.0,
     'L3_ffn_expert_w': 64.0}
    for name, (base, spread) in spreads.items():
        noise = np.random.default_rng([zlib.crc32(name.encode()), seed]).standard_normal(out[name].shape)
        drawn = base * np.exp(spread * noise) if base else spread * noise
        out[name] = jnp.asarray(drawn.astype(out[name].dtype))
    for name, factor in factors.items():
        out[name] = (out[name] * factor).astype(out[name].dtype)
    return out
```

```python
from contextlib import ExitStack, contextmanager

import numpy as np
import concourse.bass as bass
from concourse import mybir

F32 = mybir.dt.float32
F32R = mybir.dt.float32r
ALU = mybir.AluOpType
ACT = mybir.ActivationFunctionType
AX = mybir.AxisListType
ds = bass.ds

B, C, H, W = 2, 128, 64, 64
L = H * W
N = B * L
CH = 512
NCH = L // CH
TPC = CH // 128
HEADS, HD = 4, 32
GN_GROUP = 4
KW = 7
QR, QC = 8, 16
RR, RC = QR + KW - 1, QC + KW - 1
NKEY = RR * RC
KROWS = (5, 5, 4)
KOFF = (0, 5 * RC, 10 * RC)
CT = W // QC
COLSTART = [min(max(c * QC - KW // 2, 0), W - RC) for c in range(CT)]
K2, PW = 9, W + 2
NF = 16
R = 64
NB = L // R
SLOTS = NB
SPB = 8
MOE = 8
BIG = 1.0e30


class Stage:

    def __init__(self, nc, stack, names):
        self.nc, self.sems, numbers = nc, {}, []
        for name in names:
            name, n = name if isinstance(name, tuple) else (name, 1)
            made = [stack.enter_context(nc.semaphore(f"{name}{k}" if n > 1 else name)) for k in range(n)]
            self.sems[name] = made if n > 1 else made[0]
            numbers += [sem.num for sem in made]
        self.own = range(min(numbers), max(numbers) + 1)

    def __getitem__(self, name):
        return self.sems[name]

    @contextmanager
    def block(self):
        with self.nc.Block() as block:
            yield block
        self.nc.all_engine_barrier(sems_to_clear=self.own)


def allocator(nc, ctx, tag):
    sb = lambda n, s, dtype=F32: ctx.enter_context(nc.sbuf_tensor(n + tag, s, dtype))
    pb = lambda n, s: ctx.enter_context(nc.psum_tensor(n + tag, s, F32))
    return sb, pb


def product(e, out, left, right, start, stop):
    (lh, ll), (rh, rl) = left, right
    e.matmul(out, lh, rl, start=start, stop=False)
    e.matmul(out, ll, rh, start=False, stop=False)
    return e.matmul(out, lh, rh, start=False, stop=stop)


def load_and_group_norm(nc, T, first):
    X, Y = T["X"], T["Y"]
    with ExitStack() as ctx:
        sb, pb = allocator(nc, ctx, "_0" if first else "_1")
        stats = sb("gn_stats", [128, B, NCH, 6])
        mv = sb("gn_mv", [128, B, 2])
        mom = sb("gn_mom", [128, B, 2])
        grp = sb("gn_grp", [128, B, 2])
        var = sb("gn_var", [128, B])
        rstd = sb("gn_rstd", [128, B])
        ps = pb("gn_ps", [128, CH])
        S = Stage(nc, ctx, [("x_loaded", B * NCH // 2), "const_loaded", "stats_done", "aggr_done", "sq_done", "mom_done",
                            "grp_in_psum", "grp_done", "gvar_a", "gvar_b", "sd_done", "rstd_done"])
        with S.block() as block:
            @block.sync
            def _(e):
                if first:
                    for b in range(B):
                        for c in range(NCH // 2):
                            e.dma_start(X[:, b * L + c * 1024:b * L + (c + 1) * 1024],
                                        T["x"][b, :, c * 1024:(c + 1) * 1024]).then_inc(S["x_loaded"][b * NCH // 2 + c], 16)
                    for piece in S["x_loaded"]:
                        e.wait_ge(piece, 16)

            @block.scalar
            def _(e):
                if first:
                    loads = [(T["ident"], T["c_ident"]), (T["gmat"], T["c_gmat"]), (T["eps"], T["c_eps"])]
                    for dst, src in loads:
                        e.dma_start(dst[:, :], src).then_inc(S["const_loaded"], 16)
                    e.wait_ge(S["const_loaded"], 16 * len(loads))
                e.wait_ge(S["gvar_b"], 1)
                e.activation(var[:, :], var[:, :], ACT.Sqrt, bias=T["eps"][:, 0:1]).then_inc(S["sd_done"], 1)

            @block.tensor
            def _(e):
                if first:
                    e.wait_ge(S["const_loaded"], 48)
                e.wait_ge(S["mom_done"], 1)
                e.matmul(ps[:, 0:2 * B], T["gmat"][:, :], mom[:, :, :].rearrange("p b m -> p (b m)"),
                         start=True, stop=True).then_inc(S["grp_in_psum"], 1)

            @block.vector
            def _(e):
                for b in range(B):
                    for c in range(NCH):
                        if first and c % 2 == 0:
                            e.wait_ge(S["x_loaded"][(b * NCH + c) // 2], 16)
                        at = b * L + c * CH
                        e.bn_stats(stats[:, b, c, :], X[:, at:at + CH]).then_inc(S["stats_done"], 1)
                e.wait_ge(S["stats_done"], B * NCH)
                for b in range(B):
                    e.bn_aggr(mv[:, b, :], stats[:, b, :, :].rearrange("p c s -> p (c s)")).then_inc(S["aggr_done"], 1)
                e.wait_ge(S["aggr_done"], B)
                e.tensor_tensor(mom[:, :, 1], mv[:, :, 0], mv[:, :, 0], ALU.mult).then_inc(S["sq_done"], 1)
                e.wait_ge(S["sq_done"], 1)
                e.tensor_tensor(mom[:, :, 1], mom[:, :, 1], mv[:, :, 1], ALU.add)
                e.tensor_copy(mom[:, :, 0], mv[:, :, 0]).then_inc(S["mom_done"], 1)
                e.wait_ge(S["grp_in_psum"], 1)
                e.tensor_copy(grp[:, :, :].rearrange("p b m -> p (b m)"), ps[:, 0:2 * B]).then_inc(S["grp_done"], 1)
                e.wait_ge(S["grp_done"], 1)
                e.tensor_tensor(var[:, :], grp[:, :, 0], grp[:, :, 0], ALU.mult).then_inc(S["gvar_a"], 1)
                e.wait_ge(S["gvar_a"], 1)
                e.tensor_tensor(var[:, :], grp[:, :, 1], var[:, :], ALU.subtract).then_inc(S["gvar_b"], 1)
                e.wait_ge(S["sd_done"], 1)
                e.reciprocal(rstd[:, :], var[:, :]).then_inc(S["rstd_done"], 1)
                e.wait_ge(S["rstd_done"], 1)
                for b in range(B):
                    e.tensor_scalar(Y[:, b * L:(b + 1) * L], X[:, b * L:(b + 1) * L], grp[:, b, 0:1],
                                    rstd[:, b:b + 1], ALU.subtract, ALU.mult)


def na_keys_values(nc, T, K_img, w, layer):
    Y, U = T["Y"], 4
    with ExitStack() as ctx:
        sb, pb = allocator(nc, ctx, f"_{layer}")
        y_in = [sb(f"nkv_y{u}", [128, CH]) for u in range(U)]
        v_out = [sb(f"nkv_v{u}", [128, TPC, 128]) for u in range(U)]
        psK = [pb(f"nkv_pk{i}", [128, CH]) for i in range(2)]
        psV = [pb(f"nkv_pv{i}", [128, TPC, 128]) for i in range(2)]
        S = Stage(nc, ctx, ["y_staged", "k_in_psum", "v_in_psum", "k_out", "v_out", "v_stored"])
        with nc.Fori(0, N // (CH * U)) as it:
            with S.block() as block:
                @block.gpsimd
                def _(e):
                    for u in range(U):
                        e.tensor_copy(y_in[u][:, :], Y[:, ds(it * (CH * U) + u * CH, CH)]).then_inc(S["y_staged"], 1)

                @block.tensor
                def _(e):
                    for u in range(U):
                        e.wait_ge(S["y_staged"], u + 1)
                        if u >= 2:
                            e.wait_ge(S["k_out"], u - 1)
                            e.wait_ge(S["v_out"], u - 1)
                        e.matmul(psK[u % 2][:, :], w["k"][:, :], y_in[u][:, :], start=True, stop=True)\
                            .then_inc(S["k_in_psum"], 1)
                        for j in range(TPC):
                            mm = e.matmul(psV[u % 2][:, j, :], y_in[u][:, j * 128:(j + 1) * 128], w["v"][:, :],
                                          start=True, stop=True)
                        mm.then_inc(S["v_in_psum"], 1)

                @block.scalar
                def _(e):
                    for u in range(U):
                        e.wait_ge(S["k_in_psum"], u + 1)
                        e.activation(K_img[:, ds(it * (CH * U) + u * CH, CH)], psK[u % 2][:, :], ACT.Identity,
                                     bias=w["bk"][:, 0:1]).then_inc(S["k_out"], 1)

                @block.vector
                def _(e):
                    for u in range(U):
                        e.wait_ge(S["v_in_psum"], u + 1)
                        e.tensor_tensor(v_out[u][:, :, :], psV[u % 2][:, :, :],
                                        w["bv"][:, :].unsqueeze(1).to_broadcast([128, TPC, 128]), ALU.add)\
                            .then_inc(S["v_out"], 1)

                @block.sync
                def _(e):
                    for u in range(U):
                        e.wait_ge(S["v_out"], u + 1)
                        e.dma_start(T["v_dram"][ds(it * (CH * U) + u * CH, CH), :].rearrange("(j p) c -> p j c", p=128),
                                    v_out[u][:, :, :]).then_inc(S["v_stored"], 16)
                    e.wait_ge(S["v_stored"], 16 * U)


def na_attend(nc, T, K_img, w, bias, layer):
    Y = T["Y"]
    Yrows = Y[:, :].rearrange("p (r c) -> p r c", c=W)
    Krows = K_img[:, :].rearrange("p (r c) -> p r c", c=W)
    Vrows = T["v_dram"].rearrange("(r c) d -> r c d", c=W)
    NT = 2 * CT
    NU = NT * HEADS
    scale = -float(HD) ** -0.5
    with ExitStack() as ctx:
        sb, pb = allocator(nc, ctx, f"_{layer}")
        v_in = sb("na_v", [128, NT, 3, 128])
        q_sb = [sb(f"na_q{i}", [128, 128]) for i in range(2)]
        q_masked = [sb(f"na_qm{i}", [128, HEADS, 128]) for i in range(2)]
        s_sb = [sb(f"na_s{i}", [128, NKEY]) for i in range(2)]
        p_sb = [sb(f"na_p{i}", [128, NKEY]) for i in range(2)]
        pt_sb = [sb(f"na_pt{i}", [128, 3 * 128]) for i in range(2)]
        nmax = sb("na_nmax", [128, 2])
        rsum = sb("na_rsum", [128, NT, HEADS])
        rinv = sb("na_rinv", [128, NT, HEADS])
        o_sb = [sb(f"na_o{i}", [128, 128]) for i in range(2)]
        ot_sb = [sb(f"na_ot{i}", [128, 128]) for i in range(2)]
        psQ = pb("na_psQ", [128, CH])
        psS = [pb(f"na_psS{i}", [128, CH]) for i in range(2)]
        psT = [pb(f"na_psT{i}", [128, CH]) for i in range(2)]
        psO = [pb(f"na_psO{i}", [128, CH]) for i in range(2)]
        psF = pb("na_psF", [128, CH])
        S = Stage(nc, ctx, [("v_loaded", 2 * CT), "q_in_psum", "q_copied", "q_masked", "s_in_psum", "s_biased",
                            "p_done", "pt_in_psum", "pt_copied", "o_in_psum", "rinv_done", "o_scaled",
                            "ot_in_psum", "ot_copied", "proj_in_psum", "y_written"])
        with S.block() as block:
            @block.vector
            def _(e):
                for i in range(2):
                    e.memset(psT[i][:, :], 0.0)

        def body(rows):
            with S.block() as block:
                @block.sync
                def _(e):
                    for t in range(NT):
                        _, k0, _ = rows[t // CT]
                        c0 = COLSTART[t % CT]
                        for j, (n, off) in enumerate(zip(KROWS, (0, 5, 10))):
                            e.dma_start(v_in[0:n * RC, t, j, :], Vrows[ds(k0 + off, n), c0:c0 + RC, :])\
                                .then_inc(S["v_loaded"][t], 16)
                    for t in range(NT):
                        e.wait_ge(S["v_loaded"][t], 16 * 3)

                @block.tensor
                def _(e):
                    def queries(t):
                        q0 = rows[t // CT][0]
                        if t >= 1:
                            e.wait_ge(S["q_copied"], t)
                        e.matmul(psQ[:, 0:128], w["q"][:, :], Yrows[:, ds(q0, QR), (t % CT) * QC:(t % CT + 1) * QC],
                                 start=True, stop=True).then_inc(S["q_in_psum"], 1)

                    def scores(n):
                        t, h = divmod(n, HEADS)
                        k0, c0 = rows[t // CT][1], COLSTART[t % CT]
                        e.wait_ge(S["q_masked"], t + 1)
                        if n >= 2:
                            e.wait_ge(S["s_biased"], n - 1)
                        e.matmul(psS[n % 2][:, 0:NKEY], q_masked[t % 2][:, h, :], Krows[:, ds(k0, RR), c0:c0 + RC],
                                 start=True, stop=True).then_inc(S["s_in_psum"], 1)

                    def transposes(n):
                        e.wait_ge(S["p_done"], n + 1)
                        if n >= 2:
                            e.wait_ge(S["pt_copied"], n - 1)
                        for j in range(3):
                            k = KROWS[j] * RC
                            tr = e.transpose(psT[n % 2][0:k, j * 128:(j + 1) * 128],
                                             p_sb[n % 2][:, KOFF[j]:KOFF[j] + k], T["ident"][:, :])
                        tr.then_inc(S["pt_in_psum"], 1)

                    def values(n):
                        t, h = divmod(n, HEADS)
                        e.wait_ge(S["pt_copied"], n + 1)
                        if h == 0:
                            e.wait_ge(S["v_loaded"][t], 16 * 3)
                            if t >= 2:
                                e.wait_ge(S["o_scaled"], t - 1)
                        for j in range(3):
                            k = KROWS[j] * RC
                            mm = e.matmul(psO[t % 2][:, h * 128:(h + 1) * 128],
                                          pt_sb[n % 2][0:k, j * 128:(j + 1) * 128], v_in[0:k, t, j, :],
                                          start=(j == 0), stop=(j == 2))
                        mm.then_inc(S["o_in_psum"], 1)

                    def turn_output(t):
                        e.wait_ge(S["o_scaled"], t + 1)
                        if t >= 1:
                            e.wait_ge(S["y_written"], t)
                        e.transpose(psF[:, 0:128], o_sb[t % 2][:, :], T["ident"][:, :]).then_inc(S["ot_in_psum"], 1)

                    def project(t):
                        e.wait_ge(S["ot_copied"], t + 1)
                        e.matmul(psF[:, 128:256], w["p"][:, :], ot_sb[t % 2][:, :], start=True, stop=True)\
                            .then_inc(S["proj_in_psum"], 1)

                    queries(0)
                    scores(0)
                    for n in range(NU):
                        t, h = divmod(n, HEADS)
                        if h == 1 and t + 1 < NT:
                            queries(t + 1)
                        if n + 1 < NU:
                            scores(n + 1)
                        transposes(n)
                        if n >= 1:
                            values(n - 1)
                        if t >= 1 and h == 2:
                            turn_output(t - 1)
                        if t >= 1 and h == 3:
                            project(t - 1)
                    values(NU - 1)
                    turn_output(NT - 1)
                    project(NT - 1)

                @block.gpsimd
                def _(e):
                    for t in range(NT):
                        e.wait_ge(S["q_copied"], t + 1)
                        if t >= 2:
                            e.wait_ge(S["s_in_psum"], HEADS * (t - 1))
                        e.tensor_tensor(q_masked[t % 2][:, :, :],
                                        q_sb[t % 2][:, :].unsqueeze(1).to_broadcast([128, HEADS, 128]),
                                        T["headmask"][:, :].unsqueeze(2).to_broadcast([128, HEADS, 128]),
                                        ALU.mult).then_inc(S["q_masked"], 1)

                @block.vector
                def _(e):
                    def normalise(t):
                        e.wait_ge(S["p_done"], HEADS * (t + 1))
                        e.reciprocal(rinv[:, t, :], rsum[:, t, :]).then_inc(S["rinv_done"], 1)
                        e.wait_ge(S["rinv_done"], t + 1)
                        e.wait_ge(S["o_in_psum"], HEADS * (t + 1))
                        if t >= 2:
                            e.wait_ge(S["ot_in_psum"], t - 1)
                        own = bass.AP(psO[t % 2], 0, [[CH, 128], [128 + HD, HEADS], [1, HD]])
                        e.tensor_tensor(o_sb[t % 2][:, :].rearrange("p (h d) -> p h d", h=HEADS), own,
                                        rinv[:, t, :].unsqueeze(2).to_broadcast([128, HEADS, HD]), ALU.mult)\
                            .then_inc(S["o_scaled"], 1)

                    for n in range(NU):
                        t, h = divmod(n, HEADS)
                        kind = 3 * rows[t // CT][2] + (0 if t % CT == 0 else 2 if t % CT == CT - 1 else 1)
                        e.wait_ge(S["s_in_psum"], n + 1)
                        if n >= 2:
                            e.wait_ge(S["p_done"], n - 1)
                        e.tensor_tensor_reduce(out=s_sb[n % 2][:, :], in0=psS[n % 2][:, 0:NKEY],
                                               in1=bias[:, kind, h, :], scale=1.0, scalar=2 * BIG, op0=ALU.add,
                                               op1=ALU.min, accum_out=nmax[:, n % 2:n % 2 + 1]).then_inc(S["s_biased"], 1)
                        if h == 1 and t >= 1:
                            normalise(t - 1)
                    normalise(NT - 1)

                @block.scalar
                def _(e):
                    def queries(t):
                        e.wait_ge(S["q_in_psum"], t + 1)
                        if t >= 2:
                            e.wait_ge(S["q_masked"], t - 1)
                        e.activation(q_sb[t % 2][:, :], psQ[:, 0:128], ACT.Identity, bias=w["bq"][:, 0:1],
                                     scale=scale).then_inc(S["q_copied"], 1)

                    def copy_turned(n):
                        e.wait_ge(S["pt_in_psum"], n + 1)
                        if n >= 2:
                            e.wait_ge(S["o_in_psum"], n - 1)
                        e.activation(pt_sb[n % 2][:, :], psT[n % 2][:, 0:3 * 128], ACT.Copy).then_inc(S["pt_copied"], 1)

                    def copy_output(t):
                        e.wait_ge(S["ot_in_psum"], t + 1)
                        if t >= 2:
                            e.wait_ge(S["proj_in_psum"], t - 1)
                        e.activation(ot_sb[t % 2][:, :], psF[:, 0:128], ACT.Copy).then_inc(S["ot_copied"], 1)

                    def write(t):
                        e.wait_ge(S["proj_in_psum"], t + 1)
                        q0 = rows[t // CT][0]
                        e.activation(Yrows[:, ds(q0, QR), (t % CT) * QC:(t % CT + 1) * QC],
                                     psF[:, 128:256].rearrange("p (r c) -> p r c", r=QR), ACT.Identity,
                                     bias=w["bp"][:, 0:1]).then_inc(S["y_written"], 1)

                    queries(0)
                    for n in range(NU):
                        t, h = divmod(n, HEADS)
                        if h == 1 and t + 1 < NT:
                            queries(t + 1)
                        e.wait_ge(S["s_biased"], n + 1)
                        if n >= 2:
                            e.wait_ge(S["pt_in_psum"], n - 1)
                        e.activation(p_sb[n % 2][:, :], s_sb[n % 2][:, :], ACT.Exp, scale=-1.0,
                                     bias=nmax[:, n % 2:n % 2 + 1], accum_out=rsum[:, t, h:h + 1]).then_inc(S["p_done"], 1)
                        if n >= 1:
                            copy_turned(n - 1)
                        if t >= 1 and h == 3:
                            copy_output(t - 1)
                        if t >= 2 and h == 0:
                            write(t - 2)
                    copy_turned(NU - 1)
                    write(NT - 2)
                    copy_output(NT - 1)
                    write(NT - 1)

        last_k0 = H - RR
        with nc.Fori(0, B) as b:
            body([(b * H, b * H, 0), (b * H + H - QR, b * H + last_k0, 2)])
            with nc.Fori(0, (H // QR - 2) // 2) as r:
                q0 = b * H + r * (2 * QR) + QR
                body([(q0, q0 - KW // 2, 1), (q0 + QR, q0 + (QR - KW // 2), 1)])


def neighbourhood_attention(nc, T):
    for layer in range(2):
        with ExitStack() as ctx:
            sb, _ = allocator(nc, ctx, f"_{layer}")
            K_img = sb("na_K", [128, N])
            bias = sb("na_bias", [128, 9, HEADS, NKEY])
            w = {k: sb("na_w" + k, [128, 128]) for k in "qkvp"}
            w["bv"] = sb("na_bv", [128, 128])
            for k in ("bq", "bk", "bp"):
                w[k] = sb("na_" + k, [128, 1])
            T["headmask"] = sb("na_headmask", [128, HEADS])
            msk = sb("na_msk", [128, 9, NKEY])
            S = Stage(nc, ctx, ["w_loaded", "bias_loaded", "bq_done"])
            with S.block() as block:
                @block.sync
                def _(e):
                    loads = [(w[k][:, :], T["na_w"][layer, i, :, :]) for i, k in enumerate("qkvp")]
                    loads += [(w[k][:, :], T["na_b"][layer, i, :].unsqueeze(1)) for i, k in enumerate(("bq", "bk"))]
                    loads += [(w["bv"][:, :], T["na_b"][layer, 2, :].partition_broadcast(128)),
                              (w["bp"][:, :], T["na_b"][layer, 3, :].unsqueeze(1)),
                              (T["headmask"][:, :], T["c_headmask"])]
                    for dst, src in loads:
                        e.dma_start(dst, src).then_inc(S["w_loaded"], 16)
                    e.wait_ge(S["w_loaded"], 16 * len(loads))

                @block.scalar
                def _(e):
                    e.dma_start(msk[:, :, :], T["c_namask"]).then_inc(S["bias_loaded"], 16)
                    for k in range(9):
                        e.dma_start(bias[:, k, :, :], T["na_bias"][layer, k, :, :, :]).then_inc(S["bias_loaded"], 16)
                    e.wait_ge(S["bias_loaded"], 160)

                @block.vector
                def _(e):
                    e.wait_ge(S["w_loaded"], 144)
                    e.tensor_scalar(w["bq"][:, :], w["bq"][:, :], -float(HD) ** -0.5, None, ALU.mult)
                    e.wait_ge(S["bias_loaded"], 160)
                    for h in range(HEADS):
                        e.tensor_tensor(bias[:, :, h, :], msk[:, :, :], bias[:, :, h, :], ALU.subtract)
            na_keys_values(nc, T, K_img, w, layer)
            na_attend(nc, T, K_img, w, bias, layer)


def layer_norm_tokens(nc, T, src, dst, tag, affine=None):
    X, U = T["X"], 4
    with ExitStack() as ctx:
        sb, pb = allocator(nc, ctx, "_" + tag)
        x_in = [sb(f"ln_x{u}", [128, CH]) for u in range(U)]
        stats = sb("ln_stats", [128, U, TPC, 6])
        mv = sb("ln_mv", [128, U, TPC, 2])
        sd = sb("ln_sd", [128, U, TPC])
        rstd = sb("ln_rstd", [128, U, TPC])
        z = [sb(f"ln_z{i}", [128, TPC, 128]) for i in range(2)]
        zg = [sb(f"ln_zg{i}", [128, CH]) for i in range(2)] if affine else None
        psA = [pb(f"ln_psA{i}", [128, TPC, 128]) for i in range(3)]
        psB = [pb(f"ln_psB{i}", [128, CH]) for i in range(2)]
        S = Stage(nc, ctx, ["x_staged", "xt_in_psum", "stats_done", "aggr_done", "sd_done", "rstd_done",
                            "z_done", "zt_in_psum", "z_out", "added"])

        def skewed(first, second):
            first(0)
            for u in range(U):
                if u + 1 < U:
                    first(u + 1)
                second(u)

        with nc.Fori(0, B) as b, nc.Fori(0, NCH // U) as half:
            at = lambda u: ds(b * L + half * (U * CH) + u * CH, CH)
            with S.block() as block:
                @block.gpsimd
                def _(e):
                    for u in range(U):
                        e.tensor_copy(x_in[u][:, :], src[:, at(u)]).then_inc(S["x_staged"], 1)
                    if affine:
                        for u in range(U):
                            e.wait_ge(S["z_out"], u + 1)
                            e.tensor_tensor(X[:, at(u)], X[:, at(u)], zg[u % 2][:, :], ALU.add).then_inc(S["added"], 1)

                @block.tensor
                def _(e):
                    def to_tokens(u):
                        e.wait_ge(S["x_staged"], u + 1)
                        if u >= 3:
                            e.wait_ge(S["z_done"], u - 2)
                        for j in range(TPC):
                            tr = e.transpose(psA[u % 3][:, j, :], x_in[u][:, j * 128:(j + 1) * 128], T["ident"][:, :])
                        tr.then_inc(S["xt_in_psum"], 1)

                    def back(u):
                        e.wait_ge(S["z_done"], u + 1)
                        if u >= 2:
                            e.wait_ge(S["z_out"], u - 1)
                        for j in range(TPC):
                            tr = e.transpose(psB[u % 2][:, j * 128:(j + 1) * 128], z[u % 2][:, j, :], T["ident"][:, :])
                        tr.then_inc(S["zt_in_psum"], 1)

                    skewed(to_tokens, back)

                @block.vector
                def _(e):
                    def statistics(u):
                        e.wait_ge(S["xt_in_psum"], u + 1)
                        for j in range(TPC):
                            e.bn_stats(stats[:, u, j, :], psA[u % 3][:, j, :]).then_inc(S["stats_done"], 1)
                        for j in range(TPC):
                            e.wait_ge(S["stats_done"], u * TPC + j + 1)
                            e.bn_aggr(mv[:, u, j, :], stats[:, u, j, :]).then_inc(S["aggr_done"], 1)

                    def normalise(u):
                        e.wait_ge(S["sd_done"], u + 1)
                        e.reciprocal(rstd[:, u, :], sd[:, u, :]).then_inc(S["rstd_done"], 1)
                        e.wait_ge(S["rstd_done"], u + 1)
                        if u >= 2:
                            e.wait_ge(S["zt_in_psum"], u - 1)
                        for j in range(TPC):
                            op = e.tensor_scalar(z[u % 2][:, j, :], psA[u % 3][:, j, :], mv[:, u, j, 0:1],
                                                 rstd[:, u, j:j + 1], ALU.subtract, ALU.mult)
                        op.then_inc(S["z_done"], 1)

                    skewed(statistics, normalise)

                @block.scalar
                def _(e):
                    def deviation(u):
                        e.wait_ge(S["aggr_done"], TPC * (u + 1))
                        e.activation(sd[:, u, :], mv[:, u, :, 1], ACT.Sqrt, bias=T["eps"][:, 0:1]).then_inc(S["sd_done"], 1)

                    def out(u):
                        e.wait_ge(S["zt_in_psum"], u + 1)
                        if affine:
                            if u >= 2:
                                e.wait_ge(S["added"], u - 1)
                            e.activation(zg[u % 2][:, :], psB[u % 2][:, :], ACT.Identity, bias=affine[1][:, 0:1],
                                         scale=affine[0][:, 0:1]).then_inc(S["z_out"], 1)
                        else:
                            e.activation(dst(b, half, u), psB[u % 2][:, :], ACT.Copy).then_inc(S["z_out"], 1)

                    skewed(deviation, out)


def norm_into_residual(nc, T):
    with ExitStack() as ctx:
        sb, _ = allocator(nc, ctx, "_l0")
        gain, bias = sb("ln_g", [128, 1]), sb("ln_b", [128, 1])
        S = Stage(nc, ctx, ["ln_loaded"])
        with S.block() as block:
            @block.sync
            def _(e):
                e.dma_start(gain[:, :], T["ln_g"].unsqueeze(1)).then_inc(S["ln_loaded"], 16)
                e.dma_start(bias[:, :], T["ln_b"].unsqueeze(1)).then_inc(S["ln_loaded"], 16)
                e.wait_ge(S["ln_loaded"], 32)
        layer_norm_tokens(nc, T, T["Y"], None, "l0", affine=(gain, bias))


def conv_attention(nc, T):
    X, Y = T["X"], T["Y"]
    KH = K2 * HEADS
    with ExitStack() as ctx:
        sb, pb = allocator(nc, ctx, "_c3")
        Kp, Vp = sb("c3_K", [128, B * PW, PW]), sb("c3_V", [128, B * PW, PW])
        wqkv, wker = sb("c3_wqkv", [128, 3, 128]), sb("c3_wker", [128, 3, 128])
        wproj = sb("c3_wproj", [128, 128])
        hsum, hspread = sb("c3_hsum", [128, K2, 128]), sb("c3_hspread", [128, K2, 128])
        bker, alpha, beta = sb("c3_bker", [128, 1]), sb("c3_alpha", [128, 1]), sb("c3_beta", [128, 1])
        with ExitStack() as inner:
            _, pbi = allocator(nc, inner, "_c3p")
            S = Stage(nc, inner, ["c3_loaded", "borders_zeroed"])
            with S.block() as block:
                @block.sync
                def _(e):
                    loads = [(wqkv[:, :, :], T["c3_wqkv"]), (wker[:, :, :], T["c3_wker"]),
                             (wproj[:, :], T["c3_wproj"]), (hsum[:, :, :], T["c_hsum"]),
                             (hspread[:, :, :], T["c_hspread"]), (bker[:, :], T["c3_bker"]),
                             (alpha[:, :], T["alpha"][0, :].partition_broadcast(128)),
                             (beta[:, :], T["beta"][0, :].partition_broadcast(128))]
                    for dst, src in loads:
                        e.dma_start(dst, src).then_inc(S["c3_loaded"], 16)
                    e.wait_ge(S["c3_loaded"], 16 * len(loads))

                @block.vector
                def _(e):
                    e.memset(Vp[:, :, :], 0.0)
                    e.wait_ge(S["c3_loaded"], 128)
                    e.tensor_scalar(wker[:, :, :], wker[:, :, :], beta[:, 0:1], None, ALU.mult)
                    e.tensor_scalar(bker[:, :], bker[:, :], beta[:, 0:1], None, ALU.mult)

                @block.gpsimd
                def _(e):
                    e.memset(Kp[:, :, :], 0.0)

            P = Stage(nc, inner, ["qkv_in_psum", "q_out", "k_out3", "v_out3"])
            ps = [[pbi(f"c3_ps{p}{i}", [128, CH]) for i in range(2)] for p in range(3)]
            with nc.Fori(0, B) as b:
                with P.block() as block:
                    inside = lambda img, u: img[:, ds(b * PW + (1 + 8 * u), 8), 1:1 + W]
                    grid = lambda p: p[:, :].rearrange("p (r c) -> p r c", c=W)

                    @block.tensor
                    def _(e):
                        for u in range(NCH):
                            if u >= 2:
                                e.wait_ge(P["q_out"], u - 1)
                                e.wait_ge(P["k_out3"], u - 1)
                                e.wait_ge(P["v_out3"], u - 1)
                            for p in range(3):
                                mm = e.matmul(ps[p][u % 2][:, :], wqkv[:, p, :], Y[:, ds(b * L + u * CH, CH)],
                                              start=True, stop=True)
                            mm.then_inc(P["qkv_in_psum"], 1)

                    @block.scalar
                    def _(e):
                        for u in range(NCH):
                            e.wait_ge(P["qkv_in_psum"], u + 1)
                            e.activation(Y[:, ds(b * L + u * CH, CH)], ps[0][u % 2][:, :], ACT.Copy).then_inc(P["q_out"], 1)
                            e.activation(inside(Vp, u), grid(ps[2][u % 2]), ACT.Copy).then_inc(P["v_out3"], 1)

                    @block.vector
                    def _(e):
                        for u in range(NCH):
                            e.wait_ge(P["qkv_in_psum"], u + 1)
                            e.tensor_copy(inside(Kp, u), grid(ps[1][u % 2])).then_inc(P["k_out3"], 1)

        U = 4
        pool_k, dve_k = [0, 1, 2, 3, 4], [5, 6, 7, 8]
        order = [0, 5, 1, 6, 2, 7, 3, 8, 4]
        prod_pool = [sb(f"c3_pp{i}", [128, CH]) for i in range(2)]
        prod_dve = [sb(f"c3_pd{i}", [128, CH]) for i in range(2)]
        logits = sb("c3_lg", [128, CH])
        mx, sm, ri = (sb(n, [128, TPC, HEADS]) for n in ("c3_mx", "c3_sm", "c3_ri"))
        ex = sb("c3_ex", [128, TPC, KH])
        attn = [sb(f"c3_at{i}", [128, TPC, 128]) for i in range(2)]
        w_sb = [sb(f"c3_w{i}", [128, CH]) for i in range(2)]
        m = [sb(f"c3_m{i}", [128, CH]) for i in range(3)]
        acc = [sb(f"c3_acc{i}", [128, CH]) for i in range(2)]
        psL, psLt, psW, psP = (pb(n, [128, CH]) for n in ("c3_psL", "c3_psLt", "c3_psW", "c3_psP"))
        psB = [pb(f"c3_psB{i}", [128, CH]) for i in range(2)]
        S = Stage(nc, ctx, ["prod_p", "prod_d", "prod_used", "l_copied", "lt_in_psum", "max_done",
                            "sub_done", "exp_done", "sum_done", "ri_done", "ria_done", "attn_done",
                            "w_in_psum", "w_copied", "spread", "m_done", "acc_done", "proj_in_psum3", "x_added"])
        with S.block() as block:
            @block.vector
            def _(e):
                for i in range(2):
                    e.memset(attn[i][:, :, :], 0.0)
        with nc.Fori(0, B) as b, nc.Fori(0, NCH // U) as half:
            with S.block() as block:
                cols = lambda u: ds(b * L + half * (U * CH) + u * CH, CH)
                row0 = lambda u, k: b * PW + half * (8 * U) + (8 * u + k // 3)
                shifted = lambda img, u, k: img[:, ds(row0(u, k), 8), k % 3:k % 3 + W]
                grid = lambda t: t[:, :].rearrange("p (r c) -> p r c", c=W)
                qgrid = lambda u: Y[:, :].rearrange("p (r c) -> p r c", c=W)[:, ds(b * H + half * (8 * U) + 8 * u, 8), :]

                def products(e, u, ks, bufs, sem, used_before):
                    for i, k in enumerate(ks):
                        n = u * len(ks) + i
                        if n >= 2:
                            e.wait_ge(S["prod_used"], used_before(n - 2))
                        e.tensor_tensor(grid(bufs[n % 2]), qgrid(u), shifted(Kp, u, k), ALU.mult).then_inc(sem, 1)

                def used_count(ks):
                    return lambda n: (n // len(ks)) * K2 + order.index(ks[n % len(ks)]) + 1

                @block.gpsimd
                def _(e):
                    products(e, 0, pool_k, prod_pool, S["prod_p"], used_count(pool_k))
                    for u in range(U):
                        if u + 1 < U:
                            products(e, u + 1, pool_k, prod_pool, S["prod_p"], used_count(pool_k))
                        for k in range(1, K2):
                            e.wait_ge(S["m_done"], u * K2 + k + 1)
                            if k == 1:
                                if u >= 2:
                                    e.wait_ge(S["proj_in_psum3"], u - 1)
                                e.tensor_tensor(acc[u % 2][:, :], m[(u * K2) % 3][:, :], m[(u * K2 + 1) % 3][:, :],
                                                ALU.add).then_inc(S["acc_done"], 1)
                            else:
                                e.wait_ge(S["acc_done"], u * (K2 - 1) + k - 1)
                                e.tensor_tensor(acc[u % 2][:, :], acc[u % 2][:, :], m[(u * K2 + k) % 3][:, :],
                                                ALU.add).then_inc(S["acc_done"], 1)

                @block.tensor
                def _(e):
                    def score(u):
                        if u >= 1:
                            e.wait_ge(S["l_copied"], u)
                        for i, k in enumerate(order):
                            if k in pool_k:
                                n = u * len(pool_k) + pool_k.index(k)
                                e.wait_ge(S["prod_p"], n + 1)
                                buf = prod_pool[n % 2]
                            else:
                                n = u * len(dve_k) + dve_k.index(k)
                                e.wait_ge(S["prod_d"], n + 1)
                                buf = prod_dve[n % 2]
                            mm = e.matmul(psL[:, :], hsum[:, k, :], buf[:, :], start=(i == 0), stop=(i == K2 - 1))
                            mm.then_inc(S["prod_used"], 1)
                        e.wait_ge(S["prod_used"], K2 * (u + 1))

                    def turn(u):
                        e.wait_ge(S["l_copied"], u + 1)
                        if u >= 1:
                            e.wait_ge(S["sub_done"], u)
                        for j in range(TPC):
                            tr = e.transpose(psLt[:, j * 128:(j + 1) * 128], logits[:, j * 128:(j + 1) * 128], T["ident"][:, :])
                        tr.then_inc(S["lt_in_psum"], 1)

                    def weights(u):
                        if u >= 1:
                            e.wait_ge(S["w_copied"], u)
                        rhs = [Y[:, cols(u)], shifted(Kp, u, 4), shifted(Vp, u, 4)]
                        for p in range(3):
                            e.matmul(psW[:, :], wker[:, p, :], rhs[p], start=(p == 0), stop=False)
                        e.wait_ge(S["attn_done"], u + 1)
                        for j in range(TPC):
                            mm = e.matmul(psW[:, j * 128:(j + 1) * 128], attn[u % 2][:, j, :], T["ident"][:, :],
                                          start=False, stop=(j == TPC - 1))
                        mm.then_inc(S["w_in_psum"], 1)

                    def spread(u):
                        e.wait_ge(S["w_copied"], u + 1)
                        for k in range(K2):
                            n = u * K2 + k
                            if n >= 2:
                                e.wait_ge(S["m_done"], n - 1)
                            e.matmul(psB[n % 2][:, :], hspread[:, k, :], w_sb[u % 2][:, :], start=True, stop=True)\
                                .then_inc(S["spread"], 1)

                    def project(u):
                        e.wait_ge(S["acc_done"], (K2 - 1) * (u + 1))
                        if u >= 1:
                            e.wait_ge(S["x_added"], u)
                        e.matmul(psP[:, :], wproj[:, :], acc[u % 2][:, :], start=True, stop=True)\
                            .then_inc(S["proj_in_psum3"], 1)

                    score(0)
                    turn(0)
                    for u in range(U):
                        if u + 1 < U:
                            score(u + 1)
                        weights(u)
                        if u + 1 < U:
                            turn(u + 1)
                        spread(u)
                        if u >= 1:
                            project(u - 1)
                    project(U - 1)

                @block.vector
                def _(e):
                    def soften(u):
                        e.wait_ge(S["lt_in_psum"], u + 1)
                        lt = psLt[:, :].rearrange("p (s w) -> p s w", s=TPC)[:, :, 0:KH]
                        if u >= 1:
                            e.wait_ge(S["attn_done"], u)
                        e.tensor_reduce(mx[:, :, :], lt.rearrange("p s (k h) -> p s h k", h=HEADS), AX.X, ALU.max)\
                            .then_inc(S["max_done"], 1)
                        e.wait_ge(S["max_done"], u + 1)
                        e.tensor_tensor(ex[:, :, :].rearrange("p s (k h) -> p s k h", h=HEADS),
                                        lt.rearrange("p s (k h) -> p s k h", h=HEADS),
                                        mx[:, :, :].unsqueeze(2).to_broadcast([128, TPC, K2, HEADS]), ALU.subtract)\
                            .then_inc(S["sub_done"], 1)
                        e.wait_ge(S["exp_done"], u + 1)
                        e.tensor_reduce(sm[:, :, :], ex[:, :, :].rearrange("p s (k h) -> p s h k", h=HEADS), AX.X, ALU.add)\
                            .then_inc(S["sum_done"], 1)
                        e.wait_ge(S["sum_done"], u + 1)
                        e.reciprocal(ri[:, :, :], sm[:, :, :]).then_inc(S["ri_done"], 1)
                        e.wait_ge(S["ri_done"], u + 1)
                        e.tensor_scalar(ri[:, :, :], ri[:, :, :], alpha[:, 0:1], None, ALU.mult).then_inc(S["ria_done"], 1)
                        e.wait_ge(S["ria_done"], u + 1)
                        if u >= 2:
                            e.wait_ge(S["w_in_psum"], u - 1)
                        e.tensor_tensor(attn[u % 2][:, :, 0:KH].rearrange("p s (k h) -> p s k h", h=HEADS),
                                        ex[:, :, :].rearrange("p s (k h) -> p s k h", h=HEADS),
                                        ri[:, :, :].unsqueeze(2).to_broadcast([128, TPC, K2, HEADS]), ALU.mult)\
                            .then_inc(S["attn_done"], 1)

                    def weigh(u):
                        for k in range(K2):
                            n = u * K2 + k
                            e.wait_ge(S["spread"], n + 1)
                            if n >= 3:
                                up, kp = divmod(n - 3, K2)
                                e.wait_ge(S["acc_done"], up * (K2 - 1) + max(kp, 1))
                            e.tensor_tensor(grid(m[n % 3]), grid(psB[n % 2]), shifted(Vp, u, k), ALU.mult)\
                                .then_inc(S["m_done"], 1)

                    def add(u):
                        e.wait_ge(S["proj_in_psum3"], u + 1)
                        e.tensor_tensor(X[:, cols(u)], psP[:, :], X[:, cols(u)], ALU.add).then_inc(S["x_added"], 1)

                    products(e, 0, dve_k, prod_dve, S["prod_d"], used_count(dve_k))
                    soften(0)
                    for u in range(U):
                        if u + 1 < U:
                            products(e, u + 1, dve_k, prod_dve, S["prod_d"], used_count(dve_k))
                            soften(u + 1)
                        weigh(u)
                        if u >= 1:
                            add(u - 1)
                    add(U - 1)

                @block.scalar
                def _(e):
                    def copy_logits(u):
                        e.wait_ge(S["prod_used"], K2 * (u + 1))
                        if u >= 1:
                            e.wait_ge(S["lt_in_psum"], u)
                        e.activation(logits[:, :], psL[:, :], ACT.Copy).then_inc(S["l_copied"], 1)

                    def exponentials(u):
                        e.wait_ge(S["sub_done"], u + 1)
                        e.activation(ex[:, :, :], ex[:, :, :], ACT.Exp).then_inc(S["exp_done"], 1)

                    def copy_weights(u):
                        e.wait_ge(S["w_in_psum"], u + 1)
                        if u >= 2:
                            e.wait_ge(S["spread"], K2 * (u - 1))
                        e.activation(w_sb[u % 2][:, :], psW[:, :], ACT.Identity, bias=bker[:, 0:1]).then_inc(S["w_copied"], 1)

                    copy_logits(0)
                    exponentials(0)
                    for u in range(U):
                        if u + 1 < U:
                            copy_logits(u + 1)
                        copy_weights(u)
                        if u + 1 < U:
                            exponentials(u + 1)


def linear_attention(nc, T):
    X, Y = T["X"], T["Y"]
    with ExitStack() as ctx:
        sb, pb = allocator(nc, ctx, "_la")
        w, bias = sb("la_w", [128, 3, 128]), sb("la_b", [128, 3])
        k_sb = [sb(f"la_k{i}", [128, CH]) for i in range(2)]
        kv_all = sb("la_kvall", [128, CH])
        t_sb = [sb(f"la_t{i}", [128, CH]) for i in range(2)]
        kvp, kv, bqkv = sb("la_kvp", [128, NCH]), sb("la_kv", [128, 1]), sb("la_bqkv", [128, 1])
        psK = [pb(f"la_psK{i}", [128, CH]) for i in range(2)]
        psV = [pb(f"la_psV{i}", [128, CH]) for i in range(2)]
        psQ = [pb(f"la_psQ{i}", [128, CH]) for i in range(2)]
        S0 = Stage(nc, ctx, ["la_loaded"])
        with S0.block() as block:
            @block.sync
            def _(e):
                e.dma_start(w[:, :, :], T["la_w"]).then_inc(S0["la_loaded"], 16)
                e.dma_start(bias[:, :], T["la_b"]).then_inc(S0["la_loaded"], 16)
                e.wait_ge(S0["la_loaded"], 32)
        S = Stage(nc, ctx, ["k_in_psum_l", "v_in_psum_l", "k_copied", "kv_done", "kv_summed", "bqkv_done",
                            "q_in_psum_l", "q_scaled", "q_added"])
        with nc.Fori(0, B) as b:
            cols = lambda c: ds(b * L + c * CH, CH)
            with S.block() as block:
                @block.tensor
                def _(e):
                    for c in range(NCH):
                        if c >= 2:
                            e.wait_ge(S["k_copied"], c - 1)
                            e.wait_ge(S["kv_done"], c - 1)
                        e.matmul(psK[c % 2][:, :], w[:, 1, :], Y[:, cols(c)], start=True, stop=True).then_inc(S["k_in_psum_l"], 1)
                        e.matmul(psV[c % 2][:, :], w[:, 2, :], Y[:, cols(c)], start=True, stop=True).then_inc(S["v_in_psum_l"], 1)
                    for c in range(NCH):
                        if c >= 2:
                            e.wait_ge(S["q_scaled"], c - 1)
                        e.matmul(psQ[c % 2][:, :], w[:, 0, :], Y[:, cols(c)], start=True, stop=True).then_inc(S["q_in_psum_l"], 1)

                @block.scalar
                def _(e):
                    for c in range(NCH):
                        e.wait_ge(S["k_in_psum_l"], c + 1)
                        if c >= 2:
                            e.wait_ge(S["kv_done"], c - 1)
                        e.activation(k_sb[c % 2][:, :], psK[c % 2][:, :], ACT.Identity, bias=bias[:, 1:2]).then_inc(S["k_copied"], 1)
                    e.wait_ge(S["bqkv_done"], 1)
                    for c in range(NCH):
                        e.wait_ge(S["q_in_psum_l"], c + 1)
                        if c >= 2:
                            e.wait_ge(S["q_added"], c - 1)
                        e.activation(t_sb[c % 2][:, :], psQ[c % 2][:, :], ACT.Identity, bias=bqkv[:, 0:1],
                                     scale=kv[:, 0:1]).then_inc(S["q_scaled"], 1)

                @block.vector
                def _(e):
                    for c in range(NCH):
                        e.wait_ge(S["v_in_psum_l"], c + 1)
                        e.wait_ge(S["k_copied"], c + 1)
                        if c >= 1:
                            e.wait_ge(S["kv_done"], c)
                        e.scalar_tensor_tensor(kv_all[:, :], psV[c % 2][:, :], bias[:, 2:3], k_sb[c % 2][:, :],
                                               ALU.add, ALU.mult, accum_out=kvp[:, c:c + 1]).then_inc(S["kv_done"], 1)
                    e.wait_ge(S["kv_done"], NCH)
                    e.tensor_reduce(kv[:, :], kvp[:, :], AX.X, ALU.add).then_inc(S["kv_summed"], 1)
                    e.wait_ge(S["kv_summed"], 1)
                    e.tensor_tensor(bqkv[:, :], kv[:, :], bias[:, 0:1], ALU.mult).then_inc(S["bqkv_done"], 1)

                @block.gpsimd
                def _(e):
                    for c in range(NCH):
                        e.wait_ge(S["q_scaled"], c + 1)
                        e.tensor_tensor(X[:, cols(c)], X[:, cols(c)], t_sb[c % 2][:, :], ALU.add).then_inc(S["q_added"], 1)


UPAD = 4
UL = L + UPAD


def mixing_weights(nc, T, G):
    with ExitStack() as ctx:
        sb, _ = allocator(nc, ctx, "_mix")
        z, g, e1, y, oh, wt = (sb("mx_" + n, [128, 4]) for n in ("z", "g", "e", "y", "oh", "w"))
        m1, s1, r1, free = (sb("mx_" + n, [128, 1]) for n in ("m", "s", "r", "free"))
        sig, quarter = sb("mx_sig", [128, NF]), sb("mx_quarter", [128, NF])
        raw = [sb(f"mx_raw{i}", [128, 4, NF // 2 * 128]) for i in range(2)]
        raw_u = sb("mx_rawu", [128, 4, 3 * 128])
        mixed = [sb(f"mx_mixed{i}", [128, NF // 2, 128]) for i in range(2)]
        S = Stage(nc, ctx, ["small_loaded", ("mat_loaded", 4), "mu_loaded", "chain", "sig_done", "acc_step",
                            "high_done", "split_done"])
        with S.block() as block:
            @block.sync
            def _(e):
                row = lambda n: T[n][0, :].partition_broadcast(128)
                loads = [(z, row("log_weights")), (g, row("gumbel")), (sig, row("sigma")),
                         (quarter, T["c_quarter"]), (G["sign"], T["c_sign"])]
                for dst, src in loads:
                    e.dma_start(dst[:, :], src).then_inc(S["small_loaded"], 16)
                e.dma_start(raw_u[:, :, :], T["m_u"].rearrange("d i t e -> d i (t e)")).then_inc(S["mu_loaded"], 16)
                for n, name in enumerate(("m_plus", "m_minus")):
                    for part in range(2):
                        i = 2 * n + part
                        if i >= 2:
                            e.wait_ge(S["acc_step"], 5 * (i - 1))
                        k0 = part * NF // 2
                        e.dma_start(raw[i % 2][:, :, :], T[name][:, :, k0:k0 + NF // 2, :].rearrange("d i k e -> d i (k e)"))\
                            .then_inc(S["mat_loaded"][i], 16)
                e.wait_ge(S["mat_loaded"][3], 16)

            @block.gpsimd
            def _(e):
                e.wait_ge(S["small_loaded"], 80)
                e.tensor_tensor(sig[:, :], sig[:, :], quarter[:, :], ALU.pow).then_inc(S["sig_done"], 1)
                e.memset(G["U"][:, 0, 0:UPAD], 0.0)
                e.memset(G["U"][:, 1, 0:UPAD], 0.0)

            @block.scalar
            def _(e):
                e.wait_ge(S["chain"], 3)
                e.activation(e1[:, :], z[:, :], ACT.Exp).then_inc(S["chain"], 1)
                for i in range(4):
                    e.wait_ge(S["acc_step"], 5 * (i + 1))
                    n, k0 = i // 2, i % 2 * (NF // 2)
                    e.activation(G["Mh"][n][:, k0:k0 + NF // 2, :], mixed[i % 2][:, :, :], ACT.Copy).then_inc(S["high_done"], 1)

            @block.vector
            def _(e):
                count = [0]

                def link(op):
                    count[0] += 1
                    op.then_inc(S["chain"], 1)
                    e.wait_ge(S["chain"], count[0])

                e.wait_ge(S["small_loaded"], 80)
                link(e.tensor_tensor(z[:, :], z[:, :], g[:, :], ALU.add))
                link(e.tensor_reduce(m1[:, :], z[:, :], AX.X, ALU.max))
                link(e.tensor_scalar(z[:, :], z[:, :], m1[:, 0:1], None, ALU.subtract))
                count[0] += 1
                e.wait_ge(S["chain"], 4)
                link(e.tensor_reduce(s1[:, :], e1[:, :], AX.X, ALU.add))
                link(e.reciprocal(r1[:, :], s1[:, :]))
                link(e.tensor_scalar(y[:, :], e1[:, :], r1[:, 0:1], None, ALU.mult))
                link(e.tensor_reduce(m1[:, :], y[:, :], AX.X, ALU.max))
                link(e.tensor_scalar(oh[:, :], y[:, :], m1[:, 0:1], None, ALU.is_ge))
                for i in range(1, 4):
                    link(e.tensor_reduce(s1[:, :], oh[:, 0:i], AX.X, ALU.add))
                    link(e.tensor_scalar(free[:, :], s1[:, :], -1.0, 1.0, ALU.mult, ALU.add))
                    link(e.tensor_tensor(oh[:, i:i + 1], oh[:, i:i + 1], free[:, :], ALU.mult))
                link(e.tensor_tensor(wt[:, :], oh[:, :], y[:, :], ALU.subtract))
                link(e.tensor_tensor(wt[:, :], wt[:, :], y[:, :], ALU.add))
                for c in range(NCH):
                    n = sum(c < NCH >> i for i in range(4))
                    op = e.tensor_reduce(G["keep"][:, c:c + 1], oh[:, 0:n], AX.X, ALU.add)
                link(op)
                steps = [0]

                def mix(dst, src):
                    for i in range(4):
                        if i == 0:
                            op = e.tensor_scalar(dst, src(i), wt[:, 0:1], None, ALU.mult)
                        else:
                            op = e.scalar_tensor_tensor(dst, src(i), wt[:, i:i + 1], dst, ALU.mult, ALU.add)
                        steps[0] += 1
                        op.then_inc(S["acc_step"], 1)
                        e.wait_ge(S["acc_step"], steps[0])

                e.wait_ge(S["sig_done"], 1)
                for n in range(2):
                    for part in range(2):
                        i, k0 = 2 * n + part, part * NF // 2
                        e.wait_ge(S["mat_loaded"][i], 16)
                        dst = mixed[i % 2][:, :, :]
                        if i >= 2:
                            e.wait_ge(S["split_done"], i - 1)
                        mix(dst.rearrange("d k e -> d (k e)"), lambda x, i=i: raw[i % 2][:, x, :])
                        steps[0] += 1
                        e.tensor_tensor(dst, dst, sig[:, k0:k0 + NF // 2].unsqueeze(2).to_broadcast([128, NF // 2, 128]),
                                        ALU.mult).then_inc(S["acc_step"], 1)
                        e.wait_ge(S["high_done"], i + 1)
                        e.tensor_tensor(G["Ml"][n][:, k0:k0 + NF // 2, :], dst, G["Mh"][n][:, k0:k0 + NF // 2, :],
                                        ALU.subtract).then_inc(S["split_done"], 1)
                e.wait_ge(S["mu_loaded"], 16)
                mix(G["Mu"][:, :, :].rearrange("d t e -> d (t e)"), lambda x: raw_u[:, x, :])


def spectral_inputs(nc, T, G):
    PC = 2048
    with ExitStack() as ctx:
        sb, pb = allocator(nc, ctx, "_fwd")
        u_blk = sb("fw_u", [128, 128 * R])
        fwd = sb("fw_m", [128, B, 128])
        out = [sb(f"fw_o{i}", [128, PC]) for i in range(2)]
        phi, flt = sb("fw_phi", [128, NF, 2 * R]), sb("fw_flt", [128, 2, 128])
        fo = sb("fw_fo", [128, 2, NF, 2 * R])
        ps = [pb(f"fw_ps{i}", [128, CH]) for i in range(4)]
        NP = B * 128 * R // PC
        S = Stage(nc, ctx, ["u_stored", ("u_loaded", 4), "fwd_loaded", "phi_loaded", "f_in_psum", "f_copied",
                            ("piece_stored", NP), "filt_stored"])
        with S.block() as block:
            @block.sync
            def _(e):
                for b in range(B):
                    e.dma_start(T["u_blocks"][b].rearrange("j d s -> d j s"),
                                G["U"][:, b, UPAD:].rearrange("d (j s) -> d j s", s=R)).then_inc(S["u_stored"], 16)
                e.wait_ge(S["u_stored"], 32)
                for p in range(4):
                    q = 128 * R // 4
                    e.dma_start(u_blk[:, p * q:(p + 1) * q],
                                T["u_blocks"].rearrange("b j d s -> (b j) (d s)")[:, p * q:(p + 1) * q])\
                        .then_inc(S["u_loaded"][p], 16)
                for p in range(NP):
                    e.wait_ge(S["f_copied"], 8 + 4 * (p + 1))
                    e.dma_start(T["u_hat"][:, p * PC:(p + 1) * PC], out[p % 2][:, :]).then_inc(S["piece_stored"][p], 16)
                for p in range(NP - 2, NP):
                    e.wait_ge(S["piece_stored"][p], 16)

            @block.scalar
            def _(e):
                e.dma_start(phi[:, :, :], T["phi_blocks"]).then_inc(S["phi_loaded"], 16)
                e.dma_start(flt[:, :, :], T["c_flt"]).then_inc(S["phi_loaded"], 16)
                e.dma_start(fwd[:, :, :], T["c_fwd"]).then_inc(S["fwd_loaded"], 16)
                e.wait_ge(S["fwd_loaded"], 16)
                e.wait_ge(S["f_copied"], 8)
                for part in range(2):
                    e.dma_start(T["filt_hat"][0:2 * SLOTS, :, part, :], fo[:, part, :, :]).then_inc(S["filt_stored"], 16)
                e.wait_ge(S["filt_stored"], 32)

            @block.tensor
            def _(e):
                e.wait_ge(S["phi_loaded"], 32)
                for n in range(8 + NP * 4):
                    if n >= 4:
                        e.wait_ge(S["f_copied"], n - 3)
                    if n < 8:
                        part, k0 = n // 4, (n % 4) * 4
                        e.matmul(ps[n % 4][:, :], flt[:, part, :], phi[:, k0:k0 + 4, :].rearrange("a k m -> a (k m)"),
                                 start=True, stop=True).then_inc(S["f_in_psum"], 1)
                    else:
                        b, c = divmod(n - 8, NP * 2)
                        if n == 8:
                            e.wait_ge(S["fwd_loaded"], 16)
                        if b == 0 and c % 4 == 0:
                            e.wait_ge(S["u_loaded"][c // 4], 16)
                        e.matmul(ps[n % 4][:, :], fwd[:, b, :], u_blk[:, c * CH:(c + 1) * CH], start=True, stop=True)\
                            .then_inc(S["f_in_psum"], 1)

            @block.vector
            def _(e):
                for n in range(8 + NP * 4):
                    e.wait_ge(S["f_in_psum"], n + 1)
                    if n < 8:
                        part, k0 = n // 4, (n % 4) * 4
                        dst = fo[:, part, k0:k0 + 4, :].rearrange("a k m -> a (k m)")
                    else:
                        p, c = divmod(n - 8, 4)
                        if p >= 2 and c == 0:
                            e.wait_ge(S["piece_stored"][p - 2], 16)
                        dst = out[p % 2][:, c * CH:(c + 1) * CH].rearrange("c (d s) -> c d s", s=R)[:, :, ::-1]
                    src = ps[n % 4][:, :] if n < 8 else ps[n % 4][:, :].rearrange("c (d s) -> c d s", s=R)
                    e.tensor_copy(dst, src).then_inc(S["f_copied"], 1)


def spectral_slots(nc, T, G):
    NE = 4 * 4
    NPV = 6
    AHEAD = 2
    with ExitStack() as ctx:
        sb, pb = allocator(nc, ctx, "_slot")
        u_raw = [sb(f"sl_u{i}", [128, B, 2, R]) for i in range(AHEAD)]
        f_raw = [sb(f"sl_f{i}", [128, NF, 2, R]) for i in range(AHEAD)]
        u_in = [[sb(f"sl_u{p}{i}", [128, B, 2, R], F32R) for p in "hl"] for i in range(2)]
        f_in = [sb(f"sl_f{p}", [128, NF, 2, R], F32R) for p in "hl"]
        v = [sb(f"sl_v{p}", [128, NF, 2, B, 128], F32R) for p in "hl"]
        t_sb = [sb(f"sl_t{i}", [128, B * 128]) for i in range(2)]
        y_sb = [sb(f"sl_y{i}", [128, B * 128]) for i in range(2)]
        psV = [pb(f"sl_psV{i}", [128, CH]) for i in range(NPV)]
        psY = [pb(f"sl_psY{i}", [128, CH]) for i in range(2)]
        S = Stage(nc, ctx, [("slot_loaded", SPB + AHEAD), "u_high", "u_split", "f_high", "f_split", "f_used", "v_high", "v_split",
                            "v_in_psum_s", "y_minus", "y_sum", ("y_stored", SPB)])
        signs = G["sign"][:, 0:1]

        def load(e, u, slot):
            uh = T["u_hat"].rearrange("(g i) (b d s) -> g i b d s", i=2, b=B, s=R)
            for b in range(B):
                src = uh[ds(slot, 1), :, b, :, :].rearrange("g i d s -> d (g i) s")
                e.dma_start(u_raw[u % AHEAD][:, b, :, :], src).then_inc(S["slot_loaded"][u], 16)
            for part in range(2):
                row = T["filt_hat"][ds(slot * 2 + part, 1), :, :, :]
                src = bass.AP(row.tensor, row.offset, [[1, R], [2 * R, NF * 2], [1, R]])
                e.dma_start(f_raw[u % AHEAD][part * R:(part + 1) * R, :, :, :].rearrange("p k o r -> p (k o) r"), src)\
                    .then_inc(S["slot_loaded"][u], 16)

        with S.block() as block:
            @block.sync
            def _(e):
                for u in range(AHEAD):
                    load(e, u, u)
                for u in range(AHEAD):
                    e.wait_ge(S["slot_loaded"][u], 64)

        def body(slot0, last):
            with S.block() as block:
                @block.sync
                def _(e):
                    loads = SPB if last else SPB + AHEAD
                    for u in range(SPB):
                        if u + AHEAD < loads:
                            e.wait_ge(S["f_split"], 2 * (u + 1))
                            load(e, u + AHEAD, slot0 + (u + AHEAD))
                        e.wait_ge(S["y_sum"], u + 1)
                        e.dma_start(T["y_hat"][ds(slot0 * 128 + u * 128, 128), :], y_sb[u % 2][:, :])\
                            .then_inc(S["y_stored"][u], 16)
                    for u in range(SPB, loads):
                        e.wait_ge(S["slot_loaded"][u], 64)
                    for u in range(SPB):
                        e.wait_ge(S["y_stored"][u], 16)

                @block.gpsimd
                def _(e):
                    for u in range(SPB):
                        if u >= AHEAD:
                            e.wait_ge(S["slot_loaded"][u], 64)
                        if u >= 2:
                            e.wait_ge(S["v_in_psum_s"], NE * (u - 1))
                        flat = lambda t: t.rearrange("p a b c -> p (a b c)")
                        uh, ul, raw = (flat(t[:, :, :, :]) for t in (*u_in[u % 2], u_raw[u % AHEAD]))
                        e.tensor_copy(uh, raw).then_inc(S["u_high"], 1)
                        e.wait_ge(S["u_high"], u + 1)
                        e.tensor_tensor(ul, raw, uh, ALU.subtract).then_inc(S["u_split"], 1)
                        for part in range(2):
                            n = 2 * u + part
                            if u >= 1:
                                e.wait_ge(S["f_used"], n - 1)
                            fh, fl, raw = (flat(t[:, part * NF // 2:(part + 1) * NF // 2, :, :]) for t in (*f_in, f_raw[u % AHEAD]))
                            e.tensor_copy(fh, raw).then_inc(S["f_high"], 1)
                            e.wait_ge(S["f_high"], n + 1)
                            e.tensor_tensor(fl, raw, fh, ALU.subtract).then_inc(S["f_split"], 1)

                @block.tensor
                def _(e):
                    for u in range(SPB):
                        e.wait_ge(S["u_split"], u + 1)
                        for kc in range(4):
                            for q in range(4):
                                b, pm = divmod(q, 2)
                                n = u * NE + kc * 4 + q
                                if n >= NPV:
                                    e.wait_ge(S["v_split"], n - NPV + 1)
                                product(e, psV[n % NPV][:, :], [t[:, b, :, :].rearrange("d i s -> d (i s)") for t in u_in[u % 2]],
                                        [G[m][pm][:, kc * 4:kc * 4 + 4, :].rearrange("d k e -> d (k e)") for m in ("Mh", "Ml")],
                                        True, True).then_inc(S["v_in_psum_s"], 1)
                        if u >= 2:
                            e.wait_ge(S["y_sum"], u - 1)
                        for k in range(NF):
                            if k % (NF // 2) == 0:
                                e.wait_ge(S["f_split"], 2 * u + k // (NF // 2) + 1)
                            if k % 4 == 0:
                                e.wait_ge(S["v_split"], u * NE + k + 4)
                            mm = product(e, psY[u % 2][:, :], [t[:, k, :, :].rearrange("p o r -> p (o r)") for t in f_in],
                                         [t[:, k, :, :, :].rearrange("p m b e -> p (m b e)") for t in v], k == 0, k == NF - 1)
                            if k % (NF // 2) == NF // 2 - 1:
                                mm.then_inc(S["f_used"], 1)

                def v_part(part, n):
                    kc, q = divmod(n % NE, 4)
                    b, pm = divmod(q, 2)
                    return v[part][:, kc * 4:kc * 4 + 4, pm, b, :]

                bank = lambda n: psV[n % NPV][:, :].rearrange("p (k e) -> p k e", k=4)

                @block.scalar
                def _(e):
                    for u in range(SPB):
                        for n in range(u * NE, (u + 1) * NE):
                            e.wait_ge(S["v_in_psum_s"], n + 1)
                            if u >= 1 and n == u * NE:
                                e.wait_ge(S["f_used"], 2 * u)
                            e.activation(v_part(0, n), bank(n), ACT.Copy, scale=signs if n % 2 else 1.0)\
                                .then_inc(S["v_high"], 1)
                        e.wait_ge(S["f_used"], 2 * (u + 1))
                        if u >= 2:
                            e.wait_ge(S["y_sum"], u - 1)
                        e.activation(t_sb[u % 2][:, :], psY[u % 2][:, B * 128:], ACT.Copy, scale=signs).then_inc(S["y_minus"], 1)

                @block.vector
                def _(e):
                    for u in range(SPB):
                        for n in range(u * NE, (u + 1) * NE):
                            e.wait_ge(S["v_high"], n + 1)
                            if n % 2:
                                e.scalar_tensor_tensor(v_part(1, n), bank(n), signs, v_part(0, n), ALU.mult, ALU.subtract)\
                                    .then_inc(S["v_split"], 1)
                            else:
                                e.tensor_tensor(v_part(1, n), bank(n), v_part(0, n), ALU.subtract).then_inc(S["v_split"], 1)
                        e.wait_ge(S["y_minus"], u + 1)
                        if u >= 2:
                            e.wait_ge(S["y_stored"][u - 2], 16)
                        e.tensor_tensor(y_sb[u % 2][:, :], psY[u % 2][:, 0:B * 128], t_sb[u % 2][:, :], ALU.subtract)\
                            .then_inc(S["y_sum"], 1)

        with nc.Fori(0, SLOTS // SPB - 1) as it:
            body(it * SPB, False)
        body(SLOTS - SPB, True)


def spectral_inverse(nc, T):
    PC, NP = 2048, 8
    with ExitStack() as ctx:
        sb, pb = allocator(nc, ctx, "_inv")
        y_in = sb("iv_y", [128, NP, PC])
        inv = sb("iv_m", [128, NB])
        out = [sb(f"iv_o{i}", [NB, PC]) for i in range(2)]
        ps = [pb(f"iv_ps{i}", [128, CH]) for i in range(4)]
        S = Stage(nc, ctx, ["inv_loaded", ("yh_loaded", NP), "i_in_psum", "i_act", "i_dve", ("o_stored", NP)])
        with S.block() as block:
            @block.sync
            def _(e):
                for p in range(NP):
                    e.dma_start(y_in[:, p, :], T["y_hat"].rearrange("(c r) w -> c (r w)", r=R)[:, p * PC:(p + 1) * PC])\
                        .then_inc(S["yh_loaded"][p], 16)
                for p in range(NP):
                    e.wait_ge(S["i_act"], 2 * (p + 1))
                    e.wait_ge(S["i_dve"], 2 * (p + 1))
                    e.dma_start(T["y_seq"].rearrange("(i r) w -> i (r w)", r=R)[:, p * PC:(p + 1) * PC], out[p % 2][:, :])\
                        .then_inc(S["o_stored"][p], 16)
                for p in range(NP):
                    e.wait_ge(S["o_stored"][p], 16)

            @block.scalar
            def _(e):
                e.dma_start(inv[:, :], T["c_inv"]).then_inc(S["inv_loaded"], 16)
                for n in range(0, 4 * NP, 2):
                    e.wait_ge(S["i_in_psum"], n + 1)
                    p, c = divmod(n, 4)
                    if p >= 2 and c == 0:
                        e.wait_ge(S["o_stored"][p - 2], 16)
                    e.activation(out[p % 2][:, c * CH:(c + 1) * CH], ps[n % 4][0:NB, :], ACT.Copy).then_inc(S["i_act"], 1)

            @block.vector
            def _(e):
                for n in range(1, 4 * NP, 2):
                    e.wait_ge(S["i_in_psum"], n + 1)
                    p, c = divmod(n, 4)
                    if p >= 2 and c == 1:
                        e.wait_ge(S["o_stored"][p - 2], 16)
                    e.tensor_copy(out[p % 2][:, c * CH:(c + 1) * CH], ps[n % 4][0:NB, :]).then_inc(S["i_dve"], 1)

            @block.tensor
            def _(e):
                e.wait_ge(S["inv_loaded"], 16)
                for n in range(4 * NP):
                    p, c = divmod(n, 4)
                    if c == 0:
                        e.wait_ge(S["yh_loaded"][p], 16)
                    if n >= 4:
                        e.wait_ge(S["i_act"] if n % 2 == 0 else S["i_dve"], (n - 4) // 2 + 1)
                    e.matmul(ps[n % 4][0:NB, :], inv[:, :], y_in[:, p, c * CH:(c + 1) * CH], start=True, stop=True)\
                        .then_inc(S["i_in_psum"], 1)


def autoregressive(nc, T, G):
    X = T["X"]
    with ExitStack() as ctx:
        _, pb = allocator(nc, ctx, "_ar")
        ps = [pb(f"ar_ps{i}", [128, CH]) for i in range(2)]
        S = Stage(nc, ctx, ["ar_in_psum", "ar_added"])
        with nc.Fori(0, B) as b:
            with S.block() as block:
                @block.tensor
                def _(e):
                    for c in range(NCH):
                        if c >= 2:
                            e.wait_ge(S["ar_added"], c - 1)
                        for i in range(3):
                            mm = e.matmul(ps[c % 2][:, :], G["Mu"][:, i, :],
                                          G["U"][:, :, :].rearrange("p b c -> p (b c)")[:, ds(b * UL + UPAD + c * CH - i, CH)],
                                          start=(i == 0), stop=(i == 2))
                        mm.then_inc(S["ar_in_psum"], 1)

                @block.vector
                def _(e):
                    for c in range(NCH):
                        e.wait_ge(S["ar_in_psum"], c + 1)
                        x = X[:, ds(b * L + c * CH, CH)]
                        e.scalar_tensor_tensor(x, ps[c % 2][:, :], G["keep"][:, c:c + 1], x, ALU.mult, ALU.add)\
                            .then_inc(S["ar_added"], 1)


def spectral_output(nc, T, G):
    X = T["X"]
    with ExitStack() as ctx:
        sb, pb = allocator(nc, ctx, "_so")
        o_in = [sb(f"so_o{i}", [128, TPC, 128]) for i in range(NCH)]
        ps = [pb(f"so_ps{i}", [128, CH]) for i in range(2)]
        S = Stage(nc, ctx, [("seq_loaded", NCH), "so_in_psum", "so_added"])
        with nc.Fori(0, B) as b:
            with S.block() as block:
                @block.sync
                def _(e):
                    seq = T["y_seq"].rearrange("t (b c) -> t b c", b=B)
                    for c in range(NCH):
                        src = seq[c * CH:(c + 1) * CH, ds(b, 1), :].rearrange("(j p) b c -> p (j b) c", p=128)
                        e.dma_start(o_in[c][:, :, :], src).then_inc(S["seq_loaded"][c], 16)
                    for c in range(NCH):
                        e.wait_ge(S["seq_loaded"][c], 16)

                @block.tensor
                def _(e):
                    for c in range(NCH):
                        if c >= 2:
                            e.wait_ge(S["so_added"], c - 1)
                        e.wait_ge(S["seq_loaded"][c], 16)
                        for j in range(TPC):
                            tr = e.transpose(ps[c % 2][:, j * 128:(j + 1) * 128], o_in[c][:, j, :], T["ident"][:, :])
                        tr.then_inc(S["so_in_psum"], 1)

                @block.vector
                def _(e):
                    for c in range(NCH):
                        e.wait_ge(S["so_in_psum"], c + 1)
                        x = X[:, ds(b * L + c * CH, CH)]
                        e.scalar_tensor_tensor(x, ps[c % 2][:, :], G["keep"][:, c:c + 1], x, ALU.mult, ALU.add)\
                            .then_inc(S["so_added"], 1)


def spectral_bank(nc, T):
    with ExitStack() as ctx:
        sb, _ = allocator(nc, ctx, "_sp")
        G = {"sign": sb("sp_sign", [128, 1]), "keep": sb("sp_keep", [128, NCH])}
        for part in "hl":
            G["M" + part] = [sb(f"sp_M{part}{n}", [128, NF, 128], F32R) for n in range(2)]
        with ExitStack() as inner:
            sbi, _ = allocator(nc, inner, "_sp")
            G["U"], G["Mu"] = sbi("sp_U", [128, B, UL]), sbi("sp_Mu", [128, 3, 128])
            flat = G["U"][:, :, :].rearrange("p b c -> p (b c)")
            mixing_weights(nc, T, G)
            layer_norm_tokens(nc, T, T["X"], lambda b, half, u: flat[:, ds(b * UL + half * (4 * CH) + (UPAD + u * CH), CH)],
                              "sp")
            spectral_inputs(nc, T, G)
            autoregressive(nc, T, G)
        spectral_slots(nc, T, G)
        spectral_inverse(nc, T)
        spectral_output(nc, T, G)


def causal_attention(nc, T):
    X, Y = T["X"], T["Y"]
    NT = L // 128
    scale = float(C) ** -0.5
    with ExitStack() as ctx:
        sb, pb = allocator(nc, ctx, "_ca")
        w, causal = sb("ca_w", [128, 3, 128]), sb("ca_mask", [128, CH])
        q_all, k_all, v_all = sb("ca_q", [128, L]), sb("ca_k", [128, L]), sb("ca_v", [128, NT, 128])
        with ExitStack() as inner:
            sbi, pbi = allocator(nc, inner, "_cai")
            S = Stage(nc, inner, ["ca_loaded"])
            with S.block() as block:
                @block.sync
                def _(e):
                    e.dma_start(w[:, :, :], T["ca_w"]).then_inc(S["ca_loaded"], 16)
                    e.dma_start(causal[:, :], T["c_causal"]).then_inc(S["ca_loaded"], 16)
                    e.wait_ge(S["ca_loaded"], 32)
        s_sb = [sb(f"ca_s{i}", [128, L]) for i in range(2)]
        pt_sb = [sb(f"ca_pt{i}", [128, TPC, 128]) for i in range(3)]
        z_in = [sb(f"ca_z{i}", [128, CH]) for i in range(2)]
        mx, nm, rs, ri = sb("ca_mx", [128, NT, NCH]), sb("ca_nm", [128, NT]), sb("ca_rs", [128, NT]), sb("ca_ri", [128, NT])
        o_sb = [sb(f"ca_o{i}", [128, 128]) for i in range(2)]
        ps = [pb(f"ca_ps{i}", [128, CH]) for i in range(8)]
        psS, psT, psO, psX = ps[0:3], ps[3:5], ps[5:7], ps[7]
        width = lambda i, c: min(CH, (i + 1) * 128 - c * CH)
        pieces = [(i, c) for i in range(NT) for c in range(i // TPC + 1)]
        P = Stage(nc, ctx, ["z_staged", "q_in_psum_c", "k_in_psum_c", "v_in_psum_c", "q_out_c", "k_out_c", "v_out_c"])
        S = Stage(nc, ctx, ["s_in_psum_c", "s_copied", "nmax_done", "p_done_c", "pt_in_psum_c", "pt_act", "pt_dve", "pv_piece",
                            "pv_done", "ri_done_c", "o_scaled_c", "ox_in_psum", "x_added_c"])
        with nc.Fori(0, B) as b:
            with P.block() as block:
                @block.gpsimd
                def _(e):
                    for c in range(NCH):
                        if c >= 2:
                            e.wait_ge(P["v_in_psum_c"], c - 1)
                        e.tensor_copy(z_in[c % 2][:, :], Y[:, ds(b * L + c * CH, CH)]).then_inc(P["z_staged"], 1)

                @block.tensor
                def _(e):
                    for c in range(NCH):
                        e.wait_ge(P["z_staged"], c + 1)
                        if c >= 2:
                            e.wait_ge(P["q_out_c"], c - 1)
                            e.wait_ge(P["k_out_c"], c - 1)
                            e.wait_ge(P["v_out_c"], c - 1)
                        e.matmul(ps[c % 2][:, :], w[:, 0, :], z_in[c % 2][:, :], start=True, stop=True).then_inc(P["q_in_psum_c"], 1)
                        e.matmul(ps[2 + c % 2][:, :], w[:, 1, :], z_in[c % 2][:, :], start=True, stop=True).then_inc(P["k_in_psum_c"], 1)
                        for j in range(TPC):
                            mm = e.matmul(ps[4 + c % 2][:, j * 128:(j + 1) * 128], z_in[c % 2][:, j * 128:(j + 1) * 128],
                                          w[:, 2, :], start=True, stop=True)
                        mm.then_inc(P["v_in_psum_c"], 1)

                @block.scalar
                def _(e):
                    for c in range(NCH):
                        e.wait_ge(P["q_in_psum_c"], c + 1)
                        e.activation(q_all[:, c * CH:(c + 1) * CH], ps[c % 2][:, :], ACT.Copy, scale=scale).then_inc(P["q_out_c"], 1)
                        e.wait_ge(P["v_in_psum_c"], c + 1)
                        e.activation(v_all[:, c * TPC:(c + 1) * TPC, :].rearrange("p j d -> p (j d)"), ps[4 + c % 2][:, :],
                                     ACT.Copy).then_inc(P["v_out_c"], 1)

                @block.vector
                def _(e):
                    for c in range(NCH):
                        e.wait_ge(P["k_in_psum_c"], c + 1)
                        e.tensor_copy(k_all[:, c * CH:(c + 1) * CH], ps[2 + c % 2][:, :]).then_inc(P["k_out_c"], 1)

            with S.block() as block:
                first = {}
                for n, (i, c) in enumerate(pieces):
                    first.setdefault(i, n)
                last = {i: n for n, (i, c) in enumerate(pieces)}
                on_act = lambda n: n % 2 == 0
                copied_by = lambda n: (n // 2 + 1)

                @block.tensor
                def _(e):
                    def scores(i):
                        for c in range(i // TPC + 1):
                            n = first[i] + c
                            if n >= 3:
                                e.wait_ge(S["s_copied"], n - 2)
                            e.matmul(psS[n % 3][:, 0:width(i, c)], q_all[:, i * 128:(i + 1) * 128],
                                     k_all[:, c * CH:c * CH + width(i, c)], start=True, stop=True).then_inc(S["s_in_psum_c"], 1)

                    def turn(n):
                        i, c = pieces[n]
                        if c == 0:
                            e.wait_ge(S["p_done_c"], i + 1)
                        if n >= 2:
                            e.wait_ge(S["pt_act"] if on_act(n - 2) else S["pt_dve"], copied_by(n - 2))
                        for j in range(width(i, c) // 128):
                            at = c * CH + j * 128
                            tr = e.transpose(psT[n % 2][:, j * 128:(j + 1) * 128], s_sb[i % 2][:, at:at + 128], T["ident"][:, :])
                        tr.then_inc(S["pt_in_psum_c"], 1)

                    def values(n):
                        i, c = pieces[n]
                        e.wait_ge(S["pt_act"] if on_act(n) else S["pt_dve"], copied_by(n))
                        if c == 0 and i >= 2:
                            e.wait_ge(S["o_scaled_c"], i - 1)
                        for j in range(width(i, c) // 128):
                            k = c * TPC + j
                            mm = e.matmul(psO[i % 2][:, 0:128], pt_sb[n % 3][:, j, :], v_all[:, k, :],
                                          start=(k == 0), stop=(k == i))
                        mm.then_inc(S["pv_piece"], 1)

                    def output(i):
                        e.wait_ge(S["o_scaled_c"], i + 1)
                        if i >= 1:
                            e.wait_ge(S["x_added_c"], i)
                        e.transpose(psX[:, 0:128], o_sb[i % 2][:, :], T["ident"][:, :]).then_inc(S["ox_in_psum"], 1)

                    scores(0)
                    for i in range(NT):
                        if i + 1 < NT:
                            scores(i + 1)
                        for n in range(first[i], last[i] + 1):
                            turn(n)
                            if n > first[i]:
                                values(n - 1)
                        values(last[i])
                        if i >= 1:
                            output(i - 1)
                    output(NT - 1)

                @block.vector
                def _(e):
                    def copy_scores(i):
                        for c in range(i // TPC + 1):
                            n = first[i] + c
                            e.wait_ge(S["s_in_psum_c"], n + 1)
                            if c == 0 and i >= 2:
                                e.wait_ge(S["pt_in_psum_c"], last[i - 2] + 1)
                            k = width(i, c)
                            dst, m = s_sb[i % 2][:, c * CH:c * CH + k], mx[:, i, c:c + 1]
                            if c == i // TPC:
                                e.tensor_tensor_reduce(out=dst, in0=psS[n % 3][:, 0:k], in1=causal[:, CH - k:], scale=1.0,
                                                       scalar=-2 * BIG, op0=ALU.add, op1=ALU.max, accum_out=m).then_inc(S["s_copied"], 1)
                            else:
                                e.tensor_scalar(dst, psS[n % 3][:, 0:k], 1.0, None, ALU.mult, ALU.max, accum_out=m)\
                                    .then_inc(S["s_copied"], 1)
                        e.wait_ge(S["s_copied"], last[i] + 1)
                        e.tensor_reduce(nm[:, i:i + 1], mx[:, i, 0:i // TPC + 1], AX.X, ALU.max, negate=True).then_inc(S["nmax_done"], 1)

                    def normalise(i):
                        e.wait_ge(S["p_done_c"], i + 1)
                        e.reciprocal(ri[:, i:i + 1], rs[:, i:i + 1]).then_inc(S["ri_done_c"], 1)
                        e.wait_ge(S["ri_done_c"], i + 1)
                        e.wait_ge(S["pv_piece"], last[i] + 1)
                        if i >= 2:
                            e.wait_ge(S["ox_in_psum"], i - 1)
                        e.tensor_scalar(o_sb[i % 2][:, :], psO[i % 2][:, 0:128], ri[:, i:i + 1], None, ALU.mult).then_inc(S["o_scaled_c"], 1)

                    def add(i):
                        e.wait_ge(S["ox_in_psum"], i + 1)
                        x = X[:, ds(b * L + i * 128, 128)]
                        e.tensor_tensor(x, psX[:, 0:128], x, ALU.add).then_inc(S["x_added_c"], 1)

                    copy_scores(0)
                    for i in range(NT):
                        if i + 1 < NT:
                            copy_scores(i + 1)
                        for n in range(first[i], last[i] + 1):
                            if not on_act(n):
                                e.wait_ge(S["pt_in_psum_c"], n + 1)
                                if n >= 3:
                                    e.wait_ge(S["pv_piece"], n - 2)
                                k = width(*pieces[n]) // 128
                                e.tensor_copy(pt_sb[n % 3][:, 0:k, :].rearrange("p j q -> p (j q)"), psT[n % 2][:, 0:k * 128])\
                                    .then_inc(S["pt_dve"], 1)
                        if i >= 1:
                            add(i - 1)
                        normalise(i)
                    add(NT - 1)

                @block.scalar
                def _(e):
                    def exponentials(i):
                        e.wait_ge(S["nmax_done"], i + 1)
                        row = s_sb[i % 2][:, 0:(i + 1) * 128]
                        e.activation(row, row, ACT.Exp, bias=nm[:, i:i + 1], accum_out=rs[:, i:i + 1]).then_inc(S["p_done_c"], 1)

                    exponentials(0)
                    for i in range(NT):
                        for n in range(first[i], last[i] + 1):
                            if on_act(n):
                                e.wait_ge(S["pt_in_psum_c"], n + 1)
                                if n >= 3:
                                    e.wait_ge(S["pv_piece"], n - 2)
                                k = width(*pieces[n]) // 128
                                e.activation(pt_sb[n % 3][:, 0:k, :].rearrange("p j q -> p (j q)"), psT[n % 2][:, 0:k * 128],
                                             ACT.Copy).then_inc(S["pt_act"], 1)
                        if i + 1 < NT:
                            exponentials(i + 1)


def experts(nc, T):
    X, Y = T["X"], T["Y"]
    NT = 8
    DV = 4
    with ExitStack() as ctx:
        sb, pb = allocator(nc, ctx, "_ex")
        rw, rb, rank = sb("ex_rw", [128, MOE]), sb("ex_rb", [128, MOE]), sb("ex_rank", [128, MOE])
        ew, eb = sb("ex_ew", [128, MOE, 128]), sb("ex_eb", [128, 128])
        z_in = sb("ex_z", [128, NT, 128])
        lg, t1, oh1, oh2, gates = (sb("ex_" + n, [128, NT, MOE]) for n in ("lg", "t1", "oh1", "oh2", "g"))
        m1, m2 = sb("ex_m1", [128, NT]), sb("ex_m2", [128, NT])
        gate_pad = sb("ex_gp", [128, NT, 128])
        gate_t = [sb(f"ex_gt{i}", [128, 128]) for i in range(2)]
        acc = [sb(f"ex_acc{i}", [128, 128]) for i in range(2)]
        wtd = [sb(f"ex_w{i}", [128, MOE - DV, 128]) for i in range(2)]
        out = [sb(f"ex_out{i}", [128, CH]) for i in range(2)]
        psL = pb("ex_psL", [128, CH])
        psE = [pb(f"ex_psE{i}", [128, CH]) for i in range(4)]
        psG = pb("ex_psG", [128, CH])
        psO = [pb(f"ex_psO{i}", [128, CH]) for i in range(2)]
        S0 = Stage(nc, ctx, ["ex_loaded", "gp_zeroed"])
        with S0.block() as block:
            @block.sync
            def _(e):
                loads = [(rw[:, :], T["router_w"]), (rb[:, :], T["router_b"][0, :].partition_broadcast(128)),
                         (rank[:, :], T["c_rank"]), (ew[:, :, :], T["expert_w"]), (eb[:, :], T["expert_b"])]
                for dst, src in loads:
                    e.dma_start(dst, src).then_inc(S0["ex_loaded"], 16)
                e.wait_ge(S0["ex_loaded"], 16 * len(loads))

            @block.vector
            def _(e):
                e.memset(gate_pad[:, :, :], 0.0)
        S = Stage(nc, ctx, ["z_staged_e", "l_in_psum_e", "gate_chain", "exp_done_e", "g_ready", "gt_in_psum", "gt_copied",
                            "e_in_psum", "weighed_dve", "weighed_act", "acc_step_e", "out_in_psum", "out_done",
                            ("out_stored", NT * 128 // CH)])
        with nc.Fori(0, B) as b, nc.Fori(0, L // (NT * 128)) as part:
            base = b * L + part * (NT * 128)
            with S.block() as block:
                @block.gpsimd
                def _(e):
                    for h in range(2):
                        e.tensor_copy(z_in[:, h * TPC:(h + 1) * TPC, :].rearrange("p j t -> p (j t)"),
                                      Y[:, ds(base + h * CH, CH)]).then_inc(S["z_staged_e"], 1)

                @block.tensor
                def _(e):
                    for t in range(NT):
                        if t % TPC == 0:
                            e.wait_ge(S["z_staged_e"], t // TPC + 1)
                        mm = e.matmul(psL[:, t * MOE:(t + 1) * MOE], z_in[:, t, :], rw[:, :], start=True, stop=True)
                    mm.then_inc(S["l_in_psum_e"], 1)

                    def expert_outputs(t):
                        if t >= 2:
                            e.wait_ge(S["weighed_dve"], t - 1)
                            e.wait_ge(S["weighed_act"], t - 1)
                        for h in range(2):
                            mm = e.matmul(psE[2 * (t % 2) + h][:, :], z_in[:, t, :],
                                          ew[:, 4 * h:4 * h + 4, :].rearrange("d e c -> d (e c)"), start=True, stop=True)
                        mm.then_inc(S["e_in_psum"], 1)

                    def gates_turned(t):
                        if t == 0:
                            e.wait_ge(S["g_ready"], 1)
                        if t >= 1:
                            e.wait_ge(S["gt_copied"], t)
                        e.transpose(psG[:, 0:128], gate_pad[:, t, :], T["ident"][:, :]).then_inc(S["gt_in_psum"], 1)

                    def combine(t):
                        h, j = divmod(t, TPC)
                        dst = psO[h][:, j * 128:(j + 1) * 128]
                        e.wait_ge(S["gt_copied"], t + 1)
                        e.matmul(dst, eb[:, :], gate_t[t % 2][:, :], start=True, stop=False)
                        e.wait_ge(S["weighed_dve"], t + 1)
                        e.wait_ge(S["weighed_act"], t + 1)
                        e.matmul(dst, acc[t % 2][:, :], T["ident"][:, :], start=False, stop=False)
                        for x in range(MOE - DV):
                            mm = e.matmul(dst, wtd[t % 2][:, x, :], T["ident"][:, :], start=False, stop=(x == MOE - DV - 1))
                        mm.then_inc(S["out_in_psum"], 1)

                    expert_outputs(0)
                    for t in range(NT):
                        if t + 1 < NT:
                            expert_outputs(t + 1)
                        gates_turned(t)
                        combine(t)

                @block.scalar
                def _(e):
                    e.wait_ge(S["gate_chain"], 4)
                    e.activation(lg[:, :, :], lg[:, :, :], ACT.Exp).then_inc(S["exp_done_e"], 1)
                    e.wait_ge(S["g_ready"], 1)
                    for t in range(NT):
                        e.wait_ge(S["e_in_psum"], t + 1)
                        if t >= 2:
                            e.wait_ge(S["out_in_psum"], t - 1)
                        for x in range(DV, MOE):
                            op = e.activation(wtd[t % 2][:, x - DV, :], psE[2 * (t % 2) + 1][:, (x - 4) * 128:(x - 3) * 128],
                                              ACT.Copy, scale=gates[:, t, x:x + 1])
                        op.then_inc(S["weighed_act"], 1)
                        e.wait_ge(S["gt_in_psum"], t + 1)
                        if t >= 2:
                            e.wait_ge(S["out_in_psum"], t - 1)
                        e.activation(gate_t[t % 2][:, :], psG[:, 0:128], ACT.Copy).then_inc(S["gt_copied"], 1)

                @block.vector
                def _(e):
                    count = [0]

                    def link(op):
                        count[0] += 1
                        op.then_inc(S["gate_chain"], 1)
                        e.wait_ge(S["gate_chain"], count[0])

                    wide = lambda v: v.to_broadcast([128, NT, MOE])
                    e.wait_ge(S["l_in_psum_e"], 1)
                    link(e.tensor_tensor(lg[:, :, :], psL[:, 0:NT * MOE].rearrange("p (t x) -> p t x", x=MOE),
                                         wide(rb[:, :].unsqueeze(1)), ALU.add))
                    link(e.tensor_reduce(m1[:, :], lg[:, :, :], AX.X, ALU.max))

                    def first_max(oh, src, m):
                        link(e.tensor_tensor(t1[:, :, :], src, wide(m[:, :].unsqueeze(2)), ALU.is_equal))
                        link(e.tensor_tensor(t1[:, :, :], t1[:, :, :], wide(rank[:, :].unsqueeze(1)), ALU.mult))
                        link(e.tensor_reduce(m2[:, :], t1[:, :, :], AX.X, ALU.max))
                        link(e.tensor_tensor(oh[:, :, :], t1[:, :, :], wide(m2[:, :].unsqueeze(2)), ALU.is_equal))

                    link(e.tensor_copy(gates[:, :, :], lg[:, :, :]))
                    link(e.tensor_tensor(lg[:, :, :], lg[:, :, :], wide(m1[:, :].unsqueeze(2)), ALU.subtract))
                    first_max(oh1, gates[:, :, :], m1)
                    link(e.tensor_scalar(t1[:, :, :], oh1[:, :, :], -BIG, None, ALU.mult))
                    link(e.tensor_tensor(gates[:, :, :], gates[:, :, :], t1[:, :, :], ALU.add))
                    link(e.tensor_reduce(m1[:, :], gates[:, :, :], AX.X, ALU.max))
                    first_max(oh2, gates[:, :, :], m1)
                    link(e.tensor_tensor(oh1[:, :, :], oh1[:, :, :], oh2[:, :, :], ALU.add))
                    e.wait_ge(S["exp_done_e"], 1)
                    link(e.tensor_tensor(oh1[:, :, :], oh1[:, :, :], lg[:, :, :], ALU.mult))
                    link(e.tensor_reduce(m1[:, :], oh1[:, :, :], AX.X, ALU.add))
                    link(e.reciprocal(m2[:, :], m1[:, :]))
                    link(e.tensor_tensor(gates[:, :, :], oh1[:, :, :], wide(m2[:, :].unsqueeze(2)), ALU.mult))
                    e.tensor_copy(gate_pad[:, :, 0:MOE], gates[:, :, :]).then_inc(S["g_ready"], 1)
                    steps = [0]
                    for t in range(NT):
                        e.wait_ge(S["e_in_psum"], t + 1)
                        if t >= 2:
                            e.wait_ge(S["out_in_psum"], t - 1)
                        for x in range(DV):
                            src = psE[2 * (t % 2) + x // 4][:, (x % 4) * 128:(x % 4 + 1) * 128]
                            g = gates[:, t, x:x + 1]
                            if x == 0:
                                op = e.tensor_scalar(acc[t % 2][:, :], src, g, None, ALU.mult)
                            else:
                                op = e.scalar_tensor_tensor(acc[t % 2][:, :], src, g, acc[t % 2][:, :], ALU.mult, ALU.add)
                            if x < DV - 1:
                                steps[0] += 1
                                op.then_inc(S["acc_step_e"], 1)
                                e.wait_ge(S["acc_step_e"], steps[0])
                        op.then_inc(S["weighed_dve"], 1)
                        if t % TPC == TPC - 1:
                            h = t // TPC
                            e.wait_ge(S["out_in_psum"], t + 1)
                            e.tensor_tensor(out[h][:, :], psO[h][:, :], X[:, ds(base + h * CH, CH)], ALU.add).then_inc(S["out_done"], 1)

                @block.sync
                def _(e):
                    for h in range(2):
                        e.wait_ge(S["out_done"], h + 1)
                        e.dma_start(T["out"].rearrange("b c t -> c b t")[:, ds(b, 1), ds(part * (NT * 128) + h * CH, CH)],
                                    out[h][:, :].unsqueeze(1)).then_inc(S["out_stored"][h], 16)
                    for h in range(2):
                        e.wait_ge(S["out_stored"][h], 16)


def build_program(nc, T):
    dram = lambda n, s: nc.dram_tensor(n, s, F32, kind="Internal").ap()
    T["v_dram"] = dram("na_values", (N, C))
    T["u_blocks"] = dram("u_blocks", (B, NB, C, R))
    T["u_hat"] = dram("u_hat", (2 * SLOTS, B * C * R))
    T["filt_hat"] = dram("filt_hat", (2 * SLOTS, NF, 2, 2 * R))
    T["y_hat"] = dram("y_hat", (SLOTS * 2 * R, B * C))
    T["y_seq"] = dram("y_seq", (L, B * C))
    with ExitStack() as ctx:
        sb = lambda n, s: ctx.enter_context(nc.sbuf_tensor(n, s, F32))
        X = T["X"] = sb("X", [128, N])
        T["ident"], T["gmat"], T["eps"] = sb("ident", [128, 128]), sb("gmat", [128, 128]), sb("eps", [128, 1])
        into = lambda img: lambda b, half, u: img[:, ds(b * L + half * (4 * CH) + u * CH, CH)]
        with nc.sbuf_tensor("Y", [128, N], F32) as Y:
            T["Y"] = Y
            load_and_group_norm(nc, T, True)
            neighbourhood_attention(nc, T)
            norm_into_residual(nc, T)
            load_and_group_norm(nc, T, False)
            conv_attention(nc, T)
            layer_norm_tokens(nc, T, X, into(Y), "la")
            linear_attention(nc, T)
        spectral_bank(nc, T)
        with nc.sbuf_tensor("Y2", [128, N], F32) as Y:
            T["Y"] = Y
            layer_norm_tokens(nc, T, X, into(Y), "ca")
            causal_attention(nc, T)
            layer_norm_tokens(nc, T, X, into(Y), "ex")
            experts(nc, T)


def _window_tables():
    row_rel = [0, KW // 2, (H - QR) - (H - RR)]
    col_rel = [0, KW // 2, (W - QC) - (W - RC)]
    at = np.zeros((9, 128, NKEY), np.int64)
    mask = np.zeros((9, 128, NKEY), np.float32)

    def axis(n_q, n_k, rel, kind, size):
        q, k = np.arange(n_q)[:, None] + rel, np.arange(n_k)[None, :]
        start = q - KW // 2
        if kind == 0:
            start = np.maximum(start, 0)
        if kind == 2:
            start = np.minimum(start, n_k - KW)
        inside = (k >= start) & (k < start + KW)
        return np.clip(k - q + KW - 1, 0, 2 * KW - 2), inside

    for rk in range(3):
        ri, rin = axis(QR, RR, row_rel[rk], rk, H)
        for ck in range(3):
            ci, cin = axis(QC, RC, col_rel[ck], ck, W)
            idx = ri[:, None, :, None] * (2 * KW - 1) + ci[None, :, None, :]
            ok = rin[:, None, :, None] & cin[None, :, None, :]
            at[rk * 3 + ck] = idx.reshape(128, NKEY)
            mask[rk * 3 + ck] = np.where(ok, 0.0, BIG).reshape(128, NKEY)
    return at, mask


def _constants():
    f = np.float32
    p = np.arange(128)
    at, mask = _window_tables()
    c = {
        "c_ident": np.eye(128, dtype=f),
        "c_gmat": (p[:, None] // GN_GROUP == p[None, :] // GN_GROUP).astype(f) / GN_GROUP,
        "c_eps": np.full((128, 1), 1e-5, f),
        "c_headmask": (p[:, None] // HD == np.arange(HEADS)[None, :]).astype(f),
        "c_namask": np.ascontiguousarray(mask.transpose(1, 0, 2)),
    }
    hsum = np.zeros((K2, 128, 128), f)
    for k in range(K2):
        hsum[k, p, k * HEADS + p // HD] = 1.0
    c["c_hsum"] = np.ascontiguousarray(hsum.transpose(1, 0, 2))
    c["c_hspread"] = np.ascontiguousarray(hsum.transpose(2, 0, 1))
    j = np.arange(NB)
    g = np.arange(SLOTS)
    ang = 2 * np.pi * np.outer(j, g) / (2 * NB)
    fwd = np.zeros((NB, SLOTS, 2))
    fwd[:, :, 0], fwd[:, :, 1] = np.cos(ang), -np.sin(ang)
    fwd[:, 0, 1] = (-1.0) ** j
    both = np.zeros((B, B, NB, 2 * SLOTS))
    for b in range(B):
        both[b, b] = fwd.reshape(NB, 2 * SLOTS)
    c["c_fwd"] = np.ascontiguousarray(both.reshape(B, B * NB, 2 * SLOTS).transpose(1, 0, 2)).astype(f)
    inv = np.zeros((SLOTS, 2, NB))
    inv[:, 0], inv[:, 1] = 2 * np.cos(ang.T), -2 * np.sin(ang.T)
    inv[0, 0], inv[0, 1] = 1.0, (-1.0) ** j
    c["c_inv"] = (inv.reshape(2 * SLOTS, NB) / (2 * NB)).astype(f)
    flt = np.zeros((2, 128, SLOTS, 2))
    flt[0, :NB, :, 0] = fwd[:, :, 0]
    flt[0, :NB, :, 1] = -fwd[:, :, 1]
    flt[1, :NB, :, 0] = fwd[:, :, 1]
    flt[1, :NB, :, 1] = fwd[:, :, 0]
    flt[0, :NB, 0, 1] = 0.0
    flt[1, :NB, 0, 0] = 0.0
    flt[1, :NB, 0, 1] = fwd[:, 0, 1]
    c["c_flt"] = np.ascontiguousarray(flt.reshape(2, 128, 2 * SLOTS).transpose(1, 0, 2)).astype(f)
    c["c_sign"] = ((-1.0) ** p).astype(f)[:, None].copy()
    c["c_quarter"] = np.full((128, NF), 0.25, f)
    tri = np.zeros((128, CH), f)
    tri[:, CH - 128:] = np.where(p[None, :] <= p[:, None], 0.0, -BIG)
    c["c_causal"] = tri
    c["c_rank"] = np.broadcast_to(MOE - np.arange(MOE), (128, MOE)).astype(f).copy()
    return c, at


def _lay_out(i):
    f = lambda n: np.asarray(i[n])
    t = np.ascontiguousarray
    c, at = _constants()
    a = dict(c)
    a["x"] = t(f("x").reshape(B, C, L))
    qkv, proj = f("L0_conv_qkv_w"), f("L0_conv_proj_w")
    a["na_w"] = t(np.concatenate([qkv.reshape(2, 3, C, C), proj[:, None]], 1).transpose(0, 1, 3, 2))
    a["na_b"] = t(np.concatenate([f("L0_conv_qkv_b").reshape(2, 3, C), f("L0_conv_proj_b")[:, None]], 1))
    rpb = f("L0_conv_rpb").reshape(2, HEADS, (2 * KW - 1) ** 2)
    a["na_bias"] = t(rpb[:, :, at].transpose(0, 2, 3, 1, 4))
    a["ln_g"], a["ln_b"] = f("L0_conv_ln_g"), f("L0_conv_ln_b")
    a["c3_wqkv"] = t(f("L1_conv_w_qkv").reshape(3, C, C).transpose(2, 0, 1))
    wk = f("L1_conv_w_kernel").reshape(HEADS, K2, 3 * C // HEADS)
    col = np.zeros((3 * C, 128), np.float32)
    ch = np.arange(3 * C)
    for k in range(K2):
        col[ch, k * HEADS + ch // 96] = wk[ch // 96, k, ch % 96]
    a["c3_wker"] = t(col.reshape(3, C, 128).transpose(1, 0, 2))
    bk = np.zeros((128, 1), np.float32)
    bk[:K2 * HEADS, 0] = f("L1_conv_b_kernel").reshape(HEADS, K2).T.reshape(-1)
    a["c3_bker"] = bk
    a["c3_wproj"] = t(f("L1_conv_w_proj").T)
    a["alpha"], a["beta"] = f("L1_conv_alpha").reshape(1, 1), f("L1_conv_beta").reshape(1, 1)
    a["la_w"] = t(np.stack([f("L2_attn_Wq"), f("L2_attn_Wk"), f("L2_attn_Wv")], 1))
    a["la_b"] = t(np.stack([f("L2_attn_bq"), f("L2_attn_bk"), f("L2_attn_bv")], 1))
    a["sigma"] = f("L2_ffn_sigma").reshape(1, NF)
    phi = np.zeros((NF, R + L + 2 * R), np.float32)
    phi[:, R:R + L] = f("L2_ffn_phi").T
    rows = np.zeros((128, NF, 2 * R), np.float32)
    for blk in range(NB):
        rows[blk] = phi[:, blk * R + 1:blk * R + 1 + 2 * R]
    a["phi_blocks"] = rows
    a["m_u"] = t(f("L2_ffn_M_u").transpose(2, 0, 1, 3))
    a["m_plus"] = t(f("L2_ffn_M_phi_plus").transpose(2, 0, 1, 3))
    a["m_minus"] = t(f("L2_ffn_M_phi_minus").transpose(2, 0, 1, 3))
    a["log_weights"], a["gumbel"] = f("L2_ffn_log_weights").reshape(1, 4), f("L2_ffn_gumbel").reshape(1, 4)
    a["ca_w"] = t(np.stack([f("L3_attn_Wq").T, f("L3_attn_Wk").T, f("L3_attn_Wv").T], 1))
    a["router_w"], a["router_b"] = f("L3_ffn_router_w"), f("L3_ffn_router_b").reshape(1, MOE)
    a["expert_w"] = t(f("L3_ffn_expert_w").transpose(1, 0, 2))
    eb = np.zeros((128, C), np.float32)
    eb[:MOE] = f("L3_ffn_expert_b")
    a["expert_b"] = eb
    return a


def kernel(**inputs):
    import concourse.bacc as _bacc
    from concourse import mybir as _mybir
    from concourse.bass_utils import run_bass_kernel_spmd as _run

    nc = _bacc.Bacc("TRN2", target_bir_lowering=False, num_devices=1)
    arrays = {f"in_{n}": np.ascontiguousarray(v) for n, v in _lay_out(inputs).items()}
    T = {n[3:]: nc.dram_tensor(n, v.shape, _mybir.dt.from_np(v.dtype), kind="ExternalInput").ap()
         for n, v in arrays.items()}
    T["out"] = nc.dram_tensor("out_0", (B, C, L), _mybir.dt.float32, kind="ExternalOutput").ap()
    build_program(nc, T)
    r = _run(nc, [arrays], core_ids=[0])
    return np.asarray(r.results[0]["out_0"]).reshape(B, C, H, W)
```

```python
from contextlib import ExitStack, contextmanager

import numpy as np
import concourse.bass as bass
from concourse import mybir

F32 = mybir.dt.float32
F32R = mybir.dt.float32r
ALU = mybir.AluOpType
ACT = mybir.ActivationFunctionType
AX = mybir.AxisListType
ds = bass.ds

B, C, H, W = 2, 128, 64, 64
L = H * W
N = B * L
CH = 512
NCH = L // CH
TPC = CH // 128
HEADS, HD = 4, 32
GN_GROUP = 4
KW = 7
QR, QC = 8, 16
RR, RC = QR + KW - 1, QC + KW - 1
NKEY = RR * RC
KROWS = (5, 5, 4)
KOFF = (0, 5 * RC, 10 * RC)
CT = W // QC
COLSTART = [min(max(c * QC - KW // 2, 0), W - RC) for c in range(CT)]
K2, PW = 9, W + 2
NF = 16
R = 64
NB = L // R
SLOTS = NB
SPB = 8
MOE = 8
BIG = 1.0e30


class Stage:

    def __init__(self, nc, stack, names):
        self.nc, self.sems, numbers = nc, {}, []
        for name in names:
            name, n = name if isinstance(name, tuple) else (name, 1)
            made = [stack.enter_context(nc.semaphore(f"{name}{k}" if n > 1 else name)) for k in range(n)]
            self.sems[name] = made if n > 1 else made[0]
            numbers += [sem.num for sem in made]
        self.own = range(min(numbers), max(numbers) + 1)

    def __getitem__(self, name):
        return self.sems[name]

    @contextmanager
    def block(self):
        with self.nc.Block() as block:
            yield block
        self.nc.all_engine_barrier(sems_to_clear=self.own)


def allocator(nc, ctx, tag):
    sb = lambda n, s, dtype=F32: ctx.enter_context(nc.sbuf_tensor(n + tag, s, dtype))
    pb = lambda n, s: ctx.enter_context(nc.psum_tensor(n + tag, s, F32))
    return sb, pb


def product(e, out, left, right, start, stop):
    (lh, ll), (rh, rl) = left, right
    e.matmul(out, lh, rl, start=start, stop=False)
    e.matmul(out, ll, rh, start=False, stop=False)
    return e.matmul(out, lh, rh, start=False, stop=stop)


def load_and_group_norm(nc, T, first):
    X, Y = T["X"], T["Y"]
    with ExitStack() as ctx:
        sb, pb = allocator(nc, ctx, "_0" if first else "_1")
        stats = sb("gn_stats", [128, B, NCH, 6])
        mv = sb("gn_mv", [128, B, 2])
        mom = sb("gn_mom", [128, B, 2])
        grp = sb("gn_grp", [128, B, 2])
        var = sb("gn_var", [128, B])
        rstd = sb("gn_rstd", [128, B])
        ps = pb("gn_ps", [128, CH])
        S = Stage(nc, ctx, [("x_loaded", B * NCH // 2), "const_loaded", "stats_done", "aggr_done", "sq_done", "mom_done",
                            "grp_in_psum", "grp_done", "gvar_a", "gvar_b", "sd_done", "rstd_done"])
        with S.block() as block:
            @block.sync
            def _(e):
                if first:
                    for b in range(B):
                        for c in range(NCH // 2):
                            e.dma_start(X[:, b * L + c * 1024:b * L + (c + 1) * 1024],
                                        T["x"][b, :, c * 1024:(c + 1) * 1024]).then_inc(S["x_loaded"][b * NCH // 2 + c], 16)
                    for piece in S["x_loaded"]:
                        e.wait_ge(piece, 16)

            @block.scalar
            def _(e):
                if first:
                    loads = [(T["ident"], T["c_ident"]), (T["gmat"], T["c_gmat"]), (T["eps"], T["c_eps"])]
                    for dst, src in loads:
                        e.dma_start(dst[:, :], src).then_inc(S["const_loaded"], 16)
                    e.wait_ge(S["const_loaded"], 16 * len(loads))
                e.wait_ge(S["gvar_b"], 1)
                e.activation(var[:, :], var[:, :], ACT.Sqrt, bias=T["eps"][:, 0:1]).then_inc(S["sd_done"], 1)

            @block.tensor
            def _(e):
                if first:
                    e.wait_ge(S["const_loaded"], 48)
                e.wait_ge(S["mom_done"], 1)
                e.matmul(ps[:, 0:2 * B], T["gmat"][:, :], mom[:, :, :].rearrange("p b m -> p (b m)"),
                         start=True, stop=True).then_inc(S["grp_in_psum"], 1)

            @block.vector
            def _(e):
                for b in range(B):
                    for c in range(NCH):
                        if first and c % 2 == 0:
                            e.wait_ge(S["x_loaded"][(b * NCH + c) // 2], 16)
                        at = b * L + c * CH
                        e.bn_stats(stats[:, b, c, :], X[:, at:at + CH]).then_inc(S["stats_done"], 1)
                e.wait_ge(S["stats_done"], B * NCH)
                for b in range(B):
                    e.bn_aggr(mv[:, b, :], stats[:, b, :, :].rearrange("p c s -> p (c s)")).then_inc(S["aggr_done"], 1)
                e.wait_ge(S["aggr_done"], B)
                e.tensor_tensor(mom[:, :, 1], mv[:, :, 0], mv[:, :, 0], ALU.mult).then_inc(S["sq_done"], 1)
                e.wait_ge(S["sq_done"], 1)
                e.tensor_tensor(mom[:, :, 1], mom[:, :, 1], mv[:, :, 1], ALU.add)
                e.tensor_copy(mom[:, :, 0], mv[:, :, 0]).then_inc(S["mom_done"], 1)
                e.wait_ge(S["grp_in_psum"], 1)
                e.tensor_copy(grp[:, :, :].rearrange("p b m -> p (b m)"), ps[:, 0:2 * B]).then_inc(S["grp_done"], 1)
                e.wait_ge(S["grp_done"], 1)
                e.tensor_tensor(var[:, :], grp[:, :, 0], grp[:, :, 0], ALU.mult).then_inc(S["gvar_a"], 1)
                e.wait_ge(S["gvar_a"], 1)
                e.tensor_tensor(var[:, :], grp[:, :, 1], var[:, :], ALU.subtract).then_inc(S["gvar_b"], 1)
                e.wait_ge(S["sd_done"], 1)
                e.reciprocal(rstd[:, :], var[:, :]).then_inc(S["rstd_done"], 1)
                e.wait_ge(S["rstd_done"], 1)
                for b in range(B):
                    e.tensor_scalar(Y[:, b * L:(b + 1) * L], X[:, b * L:(b + 1) * L], grp[:, b, 0:1],
                                    rstd[:, b:b + 1], ALU.subtract, ALU.mult)


def na_keys_values(nc, T, K_img, w, layer, b):
    Y = T["Y"]
    with ExitStack() as ctx:
        sb, pb = allocator(nc, ctx, f"_{layer}")
        y_in = [sb(f"nkv_y{u}", [128, CH]) for u in range(3)]
        v_out = [sb(f"nkv_v{u}", [128, TPC, 128]) for u in range(2)]
        psK = [pb(f"nkv_pk{i}", [128, CH]) for i in range(4)]
        psV = [pb(f"nkv_pv{i}", [128, TPC, 128]) for i in range(2)]
        S = Stage(nc, ctx, ["y_staged", "k_in_psum", "v_in_psum", "k_high", "k_split", "v_out", ("v_stored", NCH)])
        with S.block() as block:
            @block.tensor
            def _(e):
                for u in range(NCH):
                    e.wait_ge(S["y_staged"], u + 1)
                    for g in range(2):
                        n = 2 * u + g
                        if n >= 4:
                            e.wait_ge(S["k_split"], n - 3)
                        e.matmul(psK[n % 4][:, :], w["k"][g][:, :], y_in[u % 3][:, :], start=True, stop=True)\
                            .then_inc(S["k_in_psum"], 1)
                    if u >= 2:
                        e.wait_ge(S["v_out"], u - 1)
                    for j in range(TPC):
                        mm = e.matmul(psV[u % 2][:, j, :], y_in[u % 3][:, j * 128:(j + 1) * 128], w["v"][:, :],
                                      start=True, stop=True)
                    mm.then_inc(S["v_in_psum"], 1)

            @block.scalar
            def _(e):
                for n in range(2 * NCH):
                    u, g = divmod(n, 2)
                    e.wait_ge(S["k_in_psum"], n + 1)
                    e.activation(K_img[g][:, u * CH:(u + 1) * CH], psK[n % 4][:, :], ACT.Identity,
                                 bias=w["bk"][:, g:g + 1]).then_inc(S["k_high"], 1)

            @block.vector
            def _(e):
                def stage(u):
                    if u >= 3:
                        e.wait_ge(S["v_in_psum"], u - 2)
                    e.tensor_copy(y_in[u % 3][:, :], Y[:, ds(b * L + u * CH, CH)]).then_inc(S["y_staged"], 1)

                stage(0)
                stage(1)
                for u in range(NCH):
                    if u + 2 < NCH:
                        stage(u + 2)
                    for g in range(2):
                        n = 2 * u + g
                        e.wait_ge(S["k_high"], n + 1)
                        low = K_img[g][64:128, u * CH:(u + 1) * CH]
                        e.scalar_tensor_tensor(low, psK[n % 4][64:128, :], w["bk"][64:128, g:g + 1], low, ALU.add,
                                               ALU.subtract).then_inc(S["k_split"], 1)
                    e.wait_ge(S["v_in_psum"], u + 1)
                    if u >= 2:
                        e.wait_ge(S["v_stored"][u - 2], 16)
                    e.tensor_tensor(v_out[u % 2][:, :, :], psV[u % 2][:, :, :],
                                    w["bv"][:, :].unsqueeze(1).to_broadcast([128, TPC, 128]), ALU.add)\
                        .then_inc(S["v_out"], 1)

            @block.sync
            def _(e):
                for u in range(NCH):
                    e.wait_ge(S["v_out"], u + 1)
                    e.dma_start(T["v_dram"][ds(b * L + u * CH, CH), :].rearrange("(j p) c -> p j c", p=128),
                                v_out[u % 2][:, :, :]).then_inc(S["v_stored"][u], 16)
                for u in range(NCH):
                    e.wait_ge(S["v_stored"][u], 16)


def na_attend(nc, T, K_img, w, bias, layer, b):
    Y = T["Y"]
    Yrows = Y[:, :].rearrange("p (r c) -> p r c", c=W)
    Krows = [K[:, :].rearrange("p (r c) -> p r c", c=W) for K in K_img]
    Vrows = T["v_dram"].rearrange("(r c) d -> r c d", c=W)
    NT = 2 * CT
    NU = NT * HEADS
    scale = -float(HD) ** -0.5
    with ExitStack() as ctx:
        sb, pb = allocator(nc, ctx, f"_{layer}")
        v_in = sb("na_v", [128, NT, 3, 128])
        q_sb = [sb(f"na_q{i}", [128, 2, 128]) for i in range(2)]
        q_masked = sb("na_qm", [128, HEADS, 128])
        q_high, q_low = ([sb(f"na_q{p}{i}", [128, HEADS, 128], F32R) for i in range(2)] for p in "hl")
        s_sb = [sb(f"na_s{i}", [128, NKEY]) for i in range(2)]
        p_sb = [sb(f"na_p{i}", [128, NKEY]) for i in range(2)]
        pt_sb = [sb(f"na_pt{i}", [128, 3 * 128]) for i in range(2)]
        nmax = sb("na_nmax", [128, 2])
        rsum = sb("na_rsum", [128, NT, HEADS])
        rinv = sb("na_rinv", [128, NT, HEADS])
        o_sb = [sb(f"na_o{i}", [128, 128]) for i in range(2)]
        ot_sb = [sb(f"na_ot{i}", [128, 128]) for i in range(2)]
        psQ = pb("na_psQ", [128, CH])
        psS = [pb(f"na_psS{i}", [128, CH]) for i in range(2)]
        psT = [pb(f"na_psT{i}", [128, CH]) for i in range(2)]
        psO = [pb(f"na_psO{i}", [128, CH]) for i in range(2)]
        psF = pb("na_psF", [128, CH])
        S = Stage(nc, ctx, [("v_loaded", 2 * CT), "q_in_psum", "q_copied", "q_rounded", "q_masked",
                            "q_split", "s_in_psum", "s_biased",
                            "p_done", "pt_in_psum", "pt_copied", "o_in_psum", "rinv_done", "o_scaled",
                            "ot_in_psum", "ot_copied", "proj_in_psum", "y_written"])
        with S.block() as block:
            @block.vector
            def _(e):
                for i in range(2):
                    e.memset(psT[i][:, :], 0.0)

        def body(rows):
            with S.block() as block:
                @block.sync
                def _(e):
                    for t in range(NT):
                        _, k0, _ = rows[t // CT]
                        c0 = COLSTART[t % CT]
                        for j, (n, off) in enumerate(zip(KROWS, (0, 5, 10))):
                            e.dma_start(v_in[0:n * RC, t, j, :], Vrows[ds(b * H + (k0 + off), n), c0:c0 + RC, :])\
                                .then_inc(S["v_loaded"][t], 16)
                    for t in range(NT):
                        e.wait_ge(S["v_loaded"][t], 16 * 3)

                @block.tensor
                def _(e):
                    def queries(t):
                        q0 = b * H + rows[t // CT][0]
                        if t >= 1:
                            e.wait_ge(S["q_copied"], t)
                        for g in range(2):
                            mm = e.matmul(psQ[:, g * 128:(g + 1) * 128], w["q"][g][:, :],
                                          Yrows[:, ds(q0, QR), (t % CT) * QC:(t % CT + 1) * QC], start=True, stop=True)
                        mm.then_inc(S["q_in_psum"], 1)

                    def scores(n):
                        t, h = divmod(n, HEADS)
                        k0, c0 = rows[t // CT][1], COLSTART[t % CT]
                        e.wait_ge(S["q_split"], t + 1)
                        if n >= 2:
                            e.wait_ge(S["s_biased"], n - 1)
                        keys = Krows[h // 2][:, ds(k0, RR), c0:c0 + RC]
                        e.matmul(psS[n % 2][:, 0:NKEY], q_low[t % 2][:, h, :], keys, start=True, stop=False)
                        e.matmul(psS[n % 2][:, 0:NKEY], q_high[t % 2][:, h, :], keys, start=False, stop=True)\
                            .then_inc(S["s_in_psum"], 1)

                    def transposes(n):
                        e.wait_ge(S["p_done"], n + 1)
                        if n >= 2:
                            e.wait_ge(S["pt_copied"], n - 1)
                        for j in range(3):
                            k = KROWS[j] * RC
                            tr = e.transpose(psT[n % 2][0:k, j * 128:(j + 1) * 128],
                                             p_sb[n % 2][:, KOFF[j]:KOFF[j] + k], T["ident"][:, :])
                        tr.then_inc(S["pt_in_psum"], 1)

                    def values(n):
                        t, h = divmod(n, HEADS)
                        e.wait_ge(S["pt_copied"], n + 1)
                        if h == 0:
                            e.wait_ge(S["v_loaded"][t], 16 * 3)
                            if t >= 2:
                                e.wait_ge(S["o_scaled"], t - 1)
                        for j in range(3):
                            k = KROWS[j] * RC
                            mm = e.matmul(psO[t % 2][:, h * 128:(h + 1) * 128],
                                          pt_sb[n % 2][0:k, j * 128:(j + 1) * 128], v_in[0:k, t, j, :],
                                          start=(j == 0), stop=(j == 2))
                        mm.then_inc(S["o_in_psum"], 1)

                    def turn_output(t):
                        e.wait_ge(S["o_scaled"], t + 1)
                        if t >= 1:
                            e.wait_ge(S["y_written"], t)
                        e.transpose(psF[:, 0:128], o_sb[t % 2][:, :], T["ident"][:, :]).then_inc(S["ot_in_psum"], 1)

                    def project(t):
                        e.wait_ge(S["ot_copied"], t + 1)
                        e.matmul(psF[:, 128:256], w["p"][:, :], ot_sb[t % 2][:, :], start=True, stop=True)\
                            .then_inc(S["proj_in_psum"], 1)

                    for t in range(2):
                        queries(t)
                    for n in range(2):
                        scores(n)
                    for n in range(NU):
                        t, h = divmod(n, HEADS)
                        transposes(n)
                        if n + 2 < NU:
                            scores(n + 2)
                        if n >= 1:
                            values(n - 1)
                        if h == 1 and t >= 2:
                            project(t - 2)
                        if h == 2 and t + 2 < NT:
                            queries(t + 2)
                        if h == 3 and t >= 1:
                            turn_output(t - 1)
                    values(NU - 1)
                    project(NT - 2)
                    turn_output(NT - 1)
                    project(NT - 1)

                per_head = lambda q: q[:, :, :].rearrange("p (g h) q -> p g h q", g=2)
                spread_out = lambda q: q[:, :, :].unsqueeze(2).to_broadcast([128, 2, 2, 128])
                mask = T["headmask"][:, :].rearrange("p (g h) -> p g h", g=2).unsqueeze(3).to_broadcast([128, 2, 2, 128])

                @block.gpsimd
                def _(e):
                    for t in range(NT):
                        e.wait_ge(S["q_copied"], t + 1)
                        if t >= 2:
                            e.wait_ge(S["s_in_psum"], HEADS * (t - 1))
                        e.tensor_tensor(per_head(q_high[t % 2]), spread_out(q_sb[t % 2]), mask, ALU.mult)\
                            .then_inc(S["q_rounded"], 1)
                        e.wait_ge(S["q_rounded"], t + 1)
                        e.wait_ge(S["q_masked"], t + 1)
                        e.tensor_tensor(q_low[t % 2][:, :, :], q_masked[:, :, :], q_high[t % 2][:, :, :], ALU.subtract)\
                            .then_inc(S["q_split"], 1)

                @block.vector
                def _(e):
                    def normalise(t):
                        e.wait_ge(S["p_done"], HEADS * (t + 1))
                        e.reciprocal(rinv[:, t, :], rsum[:, t, :]).then_inc(S["rinv_done"], 1)
                        e.wait_ge(S["rinv_done"], t + 1)
                        e.wait_ge(S["o_in_psum"], HEADS * (t + 1))
                        if t >= 2:
                            e.wait_ge(S["ot_in_psum"], t - 1)
                        own = bass.AP(psO[t % 2], 0, [[CH, 128], [128 + HD, HEADS], [1, HD]])
                        e.tensor_tensor(o_sb[t % 2][:, :].rearrange("p (h d) -> p h d", h=HEADS), own,
                                        rinv[:, t, :].unsqueeze(2).to_broadcast([128, HEADS, HD]), ALU.mult)\
                            .then_inc(S["o_scaled"], 1)

                    def mask_queries(t):
                        e.wait_ge(S["q_copied"], t + 1)
                        if t >= 1:
                            e.wait_ge(S["q_split"], t)
                        e.tensor_tensor(per_head(q_masked), spread_out(q_sb[t % 2]), mask, ALU.mult)\
                            .then_inc(S["q_masked"], 1)

                    for t in range(2):
                        mask_queries(t)
                    for n in range(NU):
                        t, h = divmod(n, HEADS)
                        if h == 1 and t >= 1 and t + 1 < NT:
                            mask_queries(t + 1)
                        kind = 3 * rows[t // CT][2] + (0 if t % CT == 0 else 2 if t % CT == CT - 1 else 1)
                        e.wait_ge(S["s_in_psum"], n + 1)
                        if n >= 2:
                            e.wait_ge(S["p_done"], n - 1)
                        e.tensor_tensor_reduce(out=s_sb[n % 2][:, :], in0=psS[n % 2][:, 0:NKEY],
                                               in1=bias[:, kind, h, :], scale=1.0, scalar=2 * BIG, op0=ALU.add,
                                               op1=ALU.min, accum_out=nmax[:, n % 2:n % 2 + 1]).then_inc(S["s_biased"], 1)
                        if h == 3 and t >= 1:
                            normalise(t - 1)
                    normalise(NT - 1)

                @block.scalar
                def _(e):
                    def queries(t):
                        e.wait_ge(S["q_in_psum"], t + 1)
                        if t >= 2:
                            e.wait_ge(S["q_split"], t - 1)
                        for g in range(2):
                            op = e.activation(q_sb[t % 2][:, g, :], psQ[:, g * 128:(g + 1) * 128], ACT.Identity,
                                              bias=w["bq"][:, g:g + 1], scale=scale)
                        op.then_inc(S["q_copied"], 1)

                    def copy_turned(n):
                        e.wait_ge(S["pt_in_psum"], n + 1)
                        if n >= 2:
                            e.wait_ge(S["o_in_psum"], n - 1)
                        e.activation(pt_sb[n % 2][:, :], psT[n % 2][:, 0:3 * 128], ACT.Copy).then_inc(S["pt_copied"], 1)

                    def copy_output(t):
                        e.wait_ge(S["ot_in_psum"], t + 1)
                        if t >= 2:
                            e.wait_ge(S["proj_in_psum"], t - 1)
                        e.activation(ot_sb[t % 2][:, :], psF[:, 0:128], ACT.Copy).then_inc(S["ot_copied"], 1)

                    def write(t):
                        e.wait_ge(S["proj_in_psum"], t + 1)
                        q0 = b * H + rows[t // CT][0]
                        e.activation(Yrows[:, ds(q0, QR), (t % CT) * QC:(t % CT + 1) * QC],
                                     psF[:, 128:256].rearrange("p (r c) -> p r c", r=QR), ACT.Identity,
                                     bias=w["bp"][:, 0:1]).then_inc(S["y_written"], 1)

                    def exponentials(n):
                        t, h = divmod(n, HEADS)
                        e.wait_ge(S["s_biased"], n + 1)
                        if n >= 2:
                            e.wait_ge(S["pt_in_psum"], n - 1)
                        e.activation(p_sb[n % 2][:, :], s_sb[n % 2][:, :], ACT.Exp, scale=-1.0,
                                     bias=nmax[:, n % 2:n % 2 + 1], accum_out=rsum[:, t, h:h + 1]).then_inc(S["p_done"], 1)

                    for t in range(2):
                        queries(t)
                    exponentials(0)
                    for n in range(NU):
                        t, h = divmod(n, HEADS)
                        if n + 1 < NU:
                            exponentials(n + 1)
                        if h == 0 and t >= 2:
                            copy_output(t - 2)
                        copy_turned(n)
                        if h == 2 and t >= 2:
                            write(t - 2)
                        if h == 3 and t + 2 < NT:
                            queries(t + 2)
                    copy_output(NT - 2)
                    write(NT - 2)
                    copy_output(NT - 1)
                    write(NT - 1)

        body([(0, 0, 0), (H - QR, H - RR, 2)])
        with nc.Fori(0, (H // QR - 2) // 2) as r:
            q0 = r * (2 * QR) + QR
            body([(q0, q0 - KW // 2, 1), (q0 + QR, q0 + (QR - KW // 2), 1)])


def neighbourhood_attention(nc, T):
    for layer in range(2):
        with ExitStack() as ctx:
            sb, _ = allocator(nc, ctx, f"_{layer}")
            K_img = [sb(f"na_K{g}", [128, L], F32R) for g in range(2)]
            bias = sb("na_bias", [128, 9, HEADS, NKEY])
            w = {k: sb("na_w" + k, [128, 128]) for k in "vp"}
            for k in "qk":
                w[k] = [sb(f"na_w{k}{g}", [128, 128]) for g in range(2)]
            w["bv"] = sb("na_bv", [128, 128])
            for k, n in (("bq", 2), ("bk", 2), ("bp", 1)):
                w[k] = sb("na_" + k, [128, n])
            T["headmask"] = sb("na_headmask", [128, HEADS])
            msk = sb("na_msk", [128, 9, NKEY])
            S = Stage(nc, ctx, ["w_loaded", "bias_loaded", "bq_done"])
            with S.block() as block:
                @block.sync
                def _(e):
                    loads = [(w[k][:, :], T["na_w"][layer, 2 + i, :, :]) for i, k in enumerate("vp")]
                    loads += [(w[k][g][:, :], T["na_wqk"][layer, i, g, :, :]) for i, k in enumerate("qk") for g in range(2)]
                    loads += [(w[k][:, :], T["na_bqk"][layer, i, :, :]) for i, k in enumerate(("bq", "bk"))]
                    loads += [(w["bv"][:, :], T["na_b"][layer, 2, :].partition_broadcast(128)),
                              (w["bp"][:, :], T["na_b"][layer, 3, :].unsqueeze(1)),
                              (T["headmask"][:, :], T["c_headmask"])]
                    for dst, src in loads:
                        e.dma_start(dst, src).then_inc(S["w_loaded"], 16)
                    e.wait_ge(S["w_loaded"], 16 * len(loads))

                @block.scalar
                def _(e):
                    e.dma_start(msk[:, :, :], T["c_namask"]).then_inc(S["bias_loaded"], 16)
                    for k in range(9):
                        e.dma_start(bias[:, k, :, :], T["na_bias"][layer, k, :, :, :]).then_inc(S["bias_loaded"], 16)
                    e.wait_ge(S["bias_loaded"], 160)

                @block.vector
                def _(e):
                    e.wait_ge(S["w_loaded"], 176)
                    e.tensor_scalar(w["bq"][:, :], w["bq"][:, :], -float(HD) ** -0.5, None, ALU.mult)
                    e.wait_ge(S["bias_loaded"], 160)
                    for h in range(HEADS):
                        e.tensor_tensor(bias[:, :, h, :], msk[:, :, :], bias[:, :, h, :], ALU.subtract)
            with nc.Fori(0, B) as b:
                na_keys_values(nc, T, K_img, w, layer, b)
                na_attend(nc, T, K_img, w, bias, layer, b)


def layer_norm_tokens(nc, T, src, dst, tag, affine=None):
    X, U = T["X"], 4
    with ExitStack() as ctx:
        sb, pb = allocator(nc, ctx, "_" + tag)
        x_in = [sb(f"ln_x{u}", [128, CH]) for u in range(U)]
        stats = sb("ln_stats", [128, U, TPC, 6])
        mv = sb("ln_mv", [128, U, TPC, 2])
        sd = sb("ln_sd", [128, U, TPC])
        rstd = sb("ln_rstd", [128, U, TPC])
        z = [sb(f"ln_z{i}", [128, TPC, 128]) for i in range(2)]
        zg = [sb(f"ln_zg{i}", [128, CH]) for i in range(2)] if affine else None
        psA = [pb(f"ln_psA{i}", [128, TPC, 128]) for i in range(3)]
        psB = [pb(f"ln_psB{i}", [128, CH]) for i in range(2)]
        S = Stage(nc, ctx, ["x_staged", "xt_in_psum", "stats_done", "aggr_done", "sd_done", "rstd_done",
                            "z_done", "zt_in_psum", "z_out", "added"])

        def skewed(first, second):
            first(0)
            for u in range(U):
                if u + 1 < U:
                    first(u + 1)
                second(u)

        with nc.Fori(0, B) as b, nc.Fori(0, NCH // U) as half:
            at = lambda u: ds(b * L + half * (U * CH) + u * CH, CH)
            with S.block() as block:
                if affine:
                    @block.gpsimd
                    def _(e):
                        for u in range(U):
                            e.wait_ge(S["z_out"], u + 1)
                            e.tensor_tensor(X[:, at(u)], X[:, at(u)], zg[u % 2][:, :], ALU.add).then_inc(S["added"], 1)

                @block.tensor
                def _(e):
                    def to_tokens(u):
                        e.wait_ge(S["x_staged"], u + 1)
                        if u >= 3:
                            e.wait_ge(S["z_done"], u - 2)
                        for j in range(TPC):
                            tr = e.transpose(psA[u % 3][:, j, :], x_in[u][:, j * 128:(j + 1) * 128], T["ident"][:, :])
                        tr.then_inc(S["xt_in_psum"], 1)

                    def back(u):
                        e.wait_ge(S["z_done"], u + 1)
                        if u >= 2:
                            e.wait_ge(S["z_out"], u - 1)
                        for j in range(TPC):
                            tr = e.transpose(psB[u % 2][:, j * 128:(j + 1) * 128], z[u % 2][:, j, :], T["ident"][:, :])
                        tr.then_inc(S["zt_in_psum"], 1)

                    skewed(to_tokens, back)

                @block.vector
                def _(e):
                    def statistics(u):
                        e.wait_ge(S["xt_in_psum"], u + 1)
                        for j in range(TPC):
                            e.bn_stats(stats[:, u, j, :], psA[u % 3][:, j, :]).then_inc(S["stats_done"], 1)
                        for j in range(TPC):
                            e.wait_ge(S["stats_done"], u * TPC + j + 1)
                            e.bn_aggr(mv[:, u, j, :], stats[:, u, j, :]).then_inc(S["aggr_done"], 1)

                    def normalise(u):
                        e.wait_ge(S["sd_done"], u + 1)
                        e.reciprocal(rstd[:, u, :], sd[:, u, :]).then_inc(S["rstd_done"], 1)
                        e.wait_ge(S["rstd_done"], u + 1)
                        if u >= 2:
                            e.wait_ge(S["zt_in_psum"], u - 1)
                        for j in range(TPC):
                            op = e.tensor_scalar(z[u % 2][:, j, :], psA[u % 3][:, j, :], mv[:, u, j, 0:1],
                                                 rstd[:, u, j:j + 1], ALU.subtract, ALU.mult)
                        op.then_inc(S["z_done"], 1)

                    skewed(statistics, normalise)

                @block.scalar
                def _(e):
                    for u in range(U):
                        e.activation(x_in[u][:, :], src[:, at(u)], ACT.Copy).then_inc(S["x_staged"], 1)

                    def deviation(u):
                        e.wait_ge(S["aggr_done"], TPC * (u + 1))
                        e.activation(sd[:, u, :], mv[:, u, :, 1], ACT.Sqrt, bias=T["eps"][:, 0:1]).then_inc(S["sd_done"], 1)

                    def out(u):
                        e.wait_ge(S["zt_in_psum"], u + 1)
                        if affine:
                            if u >= 2:
                                e.wait_ge(S["added"], u - 1)
                            e.activation(zg[u % 2][:, :], psB[u % 2][:, :], ACT.Identity, bias=affine[1][:, 0:1],
                                         scale=affine[0][:, 0:1]).then_inc(S["z_out"], 1)
                        else:
                            e.activation(dst(b, half, u), psB[u % 2][:, :], ACT.Copy).then_inc(S["z_out"], 1)

                    skewed(deviation, out)


def norm_into_residual(nc, T):
    with ExitStack() as ctx:
        sb, _ = allocator(nc, ctx, "_l0")
        gain, bias = sb("ln_g", [128, 1]), sb("ln_b", [128, 1])
        S = Stage(nc, ctx, ["ln_loaded"])
        with S.block() as block:
            @block.sync
            def _(e):
                e.dma_start(gain[:, :], T["ln_g"].unsqueeze(1)).then_inc(S["ln_loaded"], 16)
                e.dma_start(bias[:, :], T["ln_b"].unsqueeze(1)).then_inc(S["ln_loaded"], 16)
                e.wait_ge(S["ln_loaded"], 32)
        layer_norm_tokens(nc, T, T["Y"], None, "l0", affine=(gain, bias))


def conv_attention(nc, T):
    X, Y = T["X"], T["Y"]
    KH = K2 * HEADS
    with ExitStack() as ctx:
        sb, pb = allocator(nc, ctx, "_c3")
        Kp, Vp = sb("c3_K", [128, B * PW, PW]), sb("c3_V", [128, B * PW, PW])
        wqkv, wker = sb("c3_wqkv", [128, 3, 128]), sb("c3_wker", [128, 3, 128])
        wproj = sb("c3_wproj", [128, 128])
        hsum, hspread = sb("c3_hsum", [128, K2, 128]), sb("c3_hspread", [128, K2, 128])
        spreads = sb("c3_spreads", [128, K2, 128], F32R)
        bker, alpha, beta = sb("c3_bker", [128, 1]), sb("c3_alpha", [128, 1]), sb("c3_beta", [128, 1])
        with ExitStack() as inner:
            _, pbi = allocator(nc, inner, "_c3p")
            S = Stage(nc, inner, ["c3_loaded", "borders_zeroed"])
            with S.block() as block:
                @block.sync
                def _(e):
                    loads = [(wqkv[:, :, :], T["c3_wqkv"]), (wker[:, :, :], T["c3_wker"]),
                             (wproj[:, :], T["c3_wproj"]), (hsum[:, :, :], T["c_hsum"]),
                             (hspread[:, :, :], T["c_hspread"]), (bker[:, :], T["c3_bker"]),
                             (alpha[:, :], T["alpha"][0, :].partition_broadcast(128)),
                             (beta[:, :], T["beta"][0, :].partition_broadcast(128))]
                    for dst, src in loads:
                        e.dma_start(dst, src).then_inc(S["c3_loaded"], 16)
                    e.wait_ge(S["c3_loaded"], 16 * len(loads))

                @block.vector
                def _(e):
                    e.memset(Vp[:, :, :], 0.0)
                    e.wait_ge(S["c3_loaded"], 128)
                    e.tensor_scalar(wker[:, :, :], wker[:, :, :], beta[:, 0:1], None, ALU.mult)
                    e.tensor_scalar(bker[:, :], bker[:, :], beta[:, 0:1], None, ALU.mult)
                    e.tensor_copy(spreads[:, :, :], hspread[:, :, :])

                @block.gpsimd
                def _(e):
                    e.memset(Kp[:, :, :], 0.0)

            P = Stage(nc, inner, ["qkv_in_psum", "q_out", "k_out3", "v_out3"])
            ps = [[pbi(f"c3_ps{p}{i}", [128, CH]) for i in range(2)] for p in range(3)]
            with nc.Fori(0, B) as b:
                with P.block() as block:
                    inside = lambda img, u: img[:, ds(b * PW + (1 + 8 * u), 8), 1:1 + W]
                    grid = lambda p: p[:, :].rearrange("p (r c) -> p r c", c=W)

                    @block.tensor
                    def _(e):
                        for u in range(NCH):
                            if u >= 2:
                                e.wait_ge(P["q_out"], u - 1)
                                e.wait_ge(P["k_out3"], u - 1)
                                e.wait_ge(P["v_out3"], u - 1)
                            for p in range(3):
                                mm = e.matmul(ps[p][u % 2][:, :], wqkv[:, p, :], Y[:, ds(b * L + u * CH, CH)],
                                              start=True, stop=True)
                            mm.then_inc(P["qkv_in_psum"], 1)

                    @block.scalar
                    def _(e):
                        for u in range(NCH):
                            e.wait_ge(P["qkv_in_psum"], u + 1)
                            e.activation(Y[:, ds(b * L + u * CH, CH)], ps[0][u % 2][:, :], ACT.Copy).then_inc(P["q_out"], 1)
                            e.activation(inside(Vp, u), grid(ps[2][u % 2]), ACT.Copy).then_inc(P["v_out3"], 1)

                    @block.vector
                    def _(e):
                        for u in range(NCH):
                            e.wait_ge(P["qkv_in_psum"], u + 1)
                            e.tensor_copy(inside(Kp, u), grid(ps[1][u % 2])).then_inc(P["k_out3"], 1)

        U = 4
        pool_k, dve_k = [0, 1, 2, 3], [4, 5, 6, 7, 8]
        order = [4, 0, 5, 1, 6, 2, 7, 3, 8]
        EARLY = 2
        prod_pool = [sb(f"c3_pp{i}", [128, CH]) for i in range(2)]
        prod_dve = [sb(f"c3_pd{i}", [128, CH]) for i in range(2)]
        logits = sb("c3_lg", [128, CH])
        mx, sm, ri = (sb(n, [128, TPC, HEADS]) for n in ("c3_mx", "c3_sm", "c3_ri"))
        ex = sb("c3_ex", [128, TPC, KH])
        attn = [sb(f"c3_at{i}", [128, TPC, 128]) for i in range(2)]
        w_sb = [sb(f"c3_w{i}", [128, CH]) for i in range(2)]
        w_high, w_low = ([sb(f"c3_w{p}{i}", [128, CH], F32R) for i in range(2)] for p in "hl")
        m = [sb(f"c3_m{i}", [128, CH]) for i in range(3)]
        acc = [sb(f"c3_acc{i}", [128, CH]) for i in range(2)]
        psL, psLt, psW, psP = (pb(n, [128, CH]) for n in ("c3_psL", "c3_psLt", "c3_psW", "c3_psP"))
        psB = [pb(f"c3_psB{i}", [128, CH]) for i in range(2)]
        S = Stage(nc, ctx, ["prod_p", "prod_d", "prod_used", "l_copied", "lt_in_psum", "max_done",
                            "sub_done", "exp_done", "sum_done", "ri_done", "ria_done", "attn_done",
                            "w_in_psum", "w_copied", "w_rounded", "w_split", "spread", "m_done", "acc_done", "proj_in_psum3", "x_added"])
        with S.block() as block:
            @block.vector
            def _(e):
                for i in range(2):
                    e.memset(attn[i][:, :, :], 0.0)
        with nc.Fori(0, B) as b, nc.Fori(0, NCH // U) as half:
            with S.block() as block:
                cols = lambda u: ds(b * L + half * (U * CH) + u * CH, CH)
                row0 = lambda u, k: b * PW + half * (8 * U) + (8 * u + k // 3)
                shifted = lambda img, u, k: img[:, ds(row0(u, k), 8), k % 3:k % 3 + W]
                grid = lambda t: t[:, :].rearrange("p (r c) -> p r c", c=W)
                qgrid = lambda u: Y[:, :].rearrange("p (r c) -> p r c", c=W)[:, ds(b * H + half * (8 * U) + 8 * u, 8), :]

                def multiply(e, at, ks, bufs, sem, used_before):
                    u, i = divmod(at, K2)
                    if u < U and order[i] in ks:
                        n = u * len(ks) + ks.index(order[i])
                        if n >= 2:
                            e.wait_ge(S["prod_used"], used_before(n - 2))
                        e.tensor_tensor(grid(bufs[n % 2]), qgrid(u), shifted(Kp, u, order[i]), ALU.mult).then_inc(sem, 1)

                def used_count(ks):
                    return lambda n: (n // len(ks)) * K2 + order.index(ks[n % len(ks)]) + 1

                @block.gpsimd
                def _(e):
                    for i in range(K2 + EARLY):
                        multiply(e, i, pool_k, prod_pool, S["prod_p"], used_count(pool_k))
                    for u in range(U):
                        for k in range(K2):
                            multiply(e, (u + 1) * K2 + k + EARLY, pool_k, prod_pool, S["prod_p"], used_count(pool_k))
                            if k == 0:
                                continue
                            e.wait_ge(S["m_done"], u * K2 + k + 1)
                            if k == 1:
                                if u >= 2:
                                    e.wait_ge(S["proj_in_psum3"], u - 1)
                                e.tensor_tensor(acc[u % 2][:, :], m[(u * K2) % 3][:, :], m[(u * K2 + 1) % 3][:, :],
                                                ALU.add).then_inc(S["acc_done"], 1)
                            else:
                                e.wait_ge(S["acc_done"], u * (K2 - 1) + k - 1)
                                e.tensor_tensor(acc[u % 2][:, :], acc[u % 2][:, :], m[(u * K2 + k) % 3][:, :],
                                                ALU.add).then_inc(S["acc_done"], 1)

                @block.tensor
                def _(e):
                    def score(u, i):
                        if u >= 1 and i == 0:
                            e.wait_ge(S["l_copied"], u)
                        k = order[i]
                        if k in pool_k:
                            n = u * len(pool_k) + pool_k.index(k)
                            e.wait_ge(S["prod_p"], n + 1)
                            buf = prod_pool[n % 2]
                        else:
                            n = u * len(dve_k) + dve_k.index(k)
                            e.wait_ge(S["prod_d"], n + 1)
                            buf = prod_dve[n % 2]
                        e.matmul(psL[:, :], hsum[:, k, :], buf[:, :], start=(i == 0), stop=(i == K2 - 1))\
                            .then_inc(S["prod_used"], 1)

                    def turn(u):
                        e.wait_ge(S["l_copied"], u + 1)
                        if u >= 1:
                            e.wait_ge(S["sub_done"], u)
                        for j in range(TPC):
                            tr = e.transpose(psLt[:, j * 128:(j + 1) * 128], logits[:, j * 128:(j + 1) * 128], T["ident"][:, :])
                        tr.then_inc(S["lt_in_psum"], 1)

                    def weights(u):
                        if u >= 1:
                            e.wait_ge(S["w_copied"], u)
                        rhs = [Y[:, cols(u)], shifted(Kp, u, 4), shifted(Vp, u, 4)]
                        for p in range(3):
                            e.matmul(psW[:, :], wker[:, p, :], rhs[p], start=(p == 0), stop=False)
                        e.wait_ge(S["attn_done"], u + 1)
                        for j in range(TPC):
                            mm = e.matmul(psW[:, j * 128:(j + 1) * 128], attn[u % 2][:, j, :], T["ident"][:, :],
                                          start=False, stop=(j == TPC - 1))
                        mm.then_inc(S["w_in_psum"], 1)

                    def spread(u):
                        e.wait_ge(S["w_split"], u + 1)
                        for k in range(K2):
                            n = u * K2 + k
                            if u + 1 < U:
                                score(u + 1, k)
                            if n >= 2:
                                e.wait_ge(S["m_done"], n - 1)
                            e.matmul(psB[n % 2][:, :], spreads[:, k, :], w_low[u % 2][:, :], start=True, stop=False)
                            e.matmul(psB[n % 2][:, :], spreads[:, k, :], w_high[u % 2][:, :], start=False, stop=True)\
                                .then_inc(S["spread"], 1)

                    def project(u):
                        e.wait_ge(S["acc_done"], (K2 - 1) * (u + 1))
                        if u >= 1:
                            e.wait_ge(S["x_added"], u)
                        e.matmul(psP[:, :], wproj[:, :], acc[u % 2][:, :], start=True, stop=True)\
                            .then_inc(S["proj_in_psum3"], 1)

                    for i in range(K2):
                        score(0, i)
                    turn(0)
                    for u in range(U):
                        weights(u)
                        spread(u)
                        if u + 1 < U:
                            turn(u + 1)
                        project(u)

                @block.vector
                def _(e):
                    def soften(u):
                        e.wait_ge(S["lt_in_psum"], u + 1)
                        lt = psLt[:, :].rearrange("p (s w) -> p s w", s=TPC)[:, :, 0:KH]
                        if u >= 1:
                            e.wait_ge(S["attn_done"], u)
                        e.tensor_reduce(mx[:, :, :], lt.rearrange("p s (k h) -> p s h k", h=HEADS), AX.X, ALU.max)\
                            .then_inc(S["max_done"], 1)
                        e.wait_ge(S["max_done"], u + 1)
                        e.tensor_tensor(ex[:, :, :].rearrange("p s (k h) -> p s k h", h=HEADS),
                                        lt.rearrange("p s (k h) -> p s k h", h=HEADS),
                                        mx[:, :, :].unsqueeze(2).to_broadcast([128, TPC, K2, HEADS]), ALU.subtract)\
                            .then_inc(S["sub_done"], 1)
                        e.wait_ge(S["exp_done"], u + 1)
                        e.tensor_reduce(sm[:, :, :], ex[:, :, :].rearrange("p s (k h) -> p s h k", h=HEADS), AX.X, ALU.add)\
                            .then_inc(S["sum_done"], 1)
                        e.wait_ge(S["sum_done"], u + 1)
                        e.reciprocal(ri[:, :, :], sm[:, :, :]).then_inc(S["ri_done"], 1)
                        e.wait_ge(S["ri_done"], u + 1)
                        e.tensor_scalar(ri[:, :, :], ri[:, :, :], alpha[:, 0:1], None, ALU.mult).then_inc(S["ria_done"], 1)
                        e.wait_ge(S["ria_done"], u + 1)
                        if u >= 2:
                            e.wait_ge(S["w_in_psum"], u - 1)
                        e.tensor_tensor(attn[u % 2][:, :, 0:KH].rearrange("p s (k h) -> p s k h", h=HEADS),
                                        ex[:, :, :].rearrange("p s (k h) -> p s k h", h=HEADS),
                                        ri[:, :, :].unsqueeze(2).to_broadcast([128, TPC, K2, HEADS]), ALU.mult)\
                            .then_inc(S["attn_done"], 1)

                    def split_weights(u):
                        e.wait_ge(S["w_copied"], u + 1)
                        e.wait_ge(S["w_rounded"], u + 1)
                        if u >= 2:
                            e.wait_ge(S["spread"], K2 * (u - 1))
                        e.tensor_tensor(w_low[u % 2][:, :], w_sb[u % 2][:, :], w_high[u % 2][:, :], ALU.subtract)\
                            .then_inc(S["w_split"], 1)

                    def weigh(u):
                        for k in range(K2):
                            multiply(e, (u + 1) * K2 + k + EARLY, dve_k, prod_dve, S["prod_d"], used_count(dve_k))
                            n = u * K2 + k
                            e.wait_ge(S["spread"], n + 1)
                            if n >= 3:
                                up, kp = divmod(n - 3, K2)
                                e.wait_ge(S["acc_done"], up * (K2 - 1) + max(kp, 1))
                            e.tensor_tensor(grid(m[n % 3]), grid(psB[n % 2]), shifted(Vp, u, k), ALU.mult)\
                                .then_inc(S["m_done"], 1)

                    def add(u):
                        e.wait_ge(S["proj_in_psum3"], u + 1)
                        e.tensor_tensor(X[:, cols(u)], psP[:, :], X[:, cols(u)], ALU.add).then_inc(S["x_added"], 1)

                    for i in range(K2 + EARLY):
                        multiply(e, i, dve_k, prod_dve, S["prod_d"], used_count(dve_k))
                    soften(0)
                    for u in range(U):
                        split_weights(u)
                        weigh(u)
                        if u + 1 < U:
                            soften(u + 1)
                        add(u)

                @block.scalar
                def _(e):
                    def copy_logits(u):
                        e.wait_ge(S["prod_used"], K2 * (u + 1))
                        if u >= 1:
                            e.wait_ge(S["lt_in_psum"], u)
                        e.activation(logits[:, :], psL[:, :], ACT.Copy).then_inc(S["l_copied"], 1)

                    def exponentials(u):
                        e.wait_ge(S["sub_done"], u + 1)
                        e.activation(ex[:, :, :], ex[:, :, :], ACT.Exp).then_inc(S["exp_done"], 1)

                    def copy_weights(u):
                        e.wait_ge(S["w_in_psum"], u + 1)
                        if u >= 2:
                            e.wait_ge(S["w_split"], u - 1)
                            e.wait_ge(S["spread"], K2 * (u - 1))
                        e.activation(w_high[u % 2][:, :], psW[:, :], ACT.Identity, bias=bker[:, 0:1]).then_inc(S["w_rounded"], 1)
                        e.activation(w_sb[u % 2][:, :], psW[:, :], ACT.Identity, bias=bker[:, 0:1]).then_inc(S["w_copied"], 1)

                    copy_logits(0)
                    exponentials(0)
                    for u in range(U):
                        copy_weights(u)
                        if u + 1 < U:
                            copy_logits(u + 1)
                        if u + 1 < U:
                            exponentials(u + 1)


def linear_attention(nc, T):
    X, Y = T["X"], T["Y"]
    with ExitStack() as ctx:
        sb, pb = allocator(nc, ctx, "_la")
        w, bias = sb("la_w", [128, 3, 128]), sb("la_b", [128, 3])
        k_sb = [sb(f"la_k{i}", [128, CH]) for i in range(2)]
        kv_all = sb("la_kvall", [128, CH])
        t_sb = [sb(f"la_t{i}", [128, CH]) for i in range(2)]
        kvp, kv, bqkv = sb("la_kvp", [128, NCH]), sb("la_kv", [128, 1]), sb("la_bqkv", [128, 1])
        psK = [pb(f"la_psK{i}", [128, CH]) for i in range(2)]
        psV = [pb(f"la_psV{i}", [128, CH]) for i in range(2)]
        psQ = [pb(f"la_psQ{i}", [128, CH]) for i in range(2)]
        S0 = Stage(nc, ctx, ["la_loaded"])
        with S0.block() as block:
            @block.sync
            def _(e):
                e.dma_start(w[:, :, :], T["la_w"]).then_inc(S0["la_loaded"], 16)
                e.dma_start(bias[:, :], T["la_b"]).then_inc(S0["la_loaded"], 16)
                e.wait_ge(S0["la_loaded"], 32)
        S = Stage(nc, ctx, ["k_in_psum_l", "v_in_psum_l", "k_copied", "kv_done", "kv_summed", "bqkv_done",
                            "q_in_psum_l", "q_scaled", "q_added"])
        with nc.Fori(0, B) as b:
            cols = lambda c: ds(b * L + c * CH, CH)
            with S.block() as block:
                @block.tensor
                def _(e):
                    for c in range(NCH):
                        if c >= 2:
                            e.wait_ge(S["k_copied"], c - 1)
                            e.wait_ge(S["kv_done"], c - 1)
                        e.matmul(psK[c % 2][:, :], w[:, 1, :], Y[:, cols(c)], start=True, stop=True).then_inc(S["k_in_psum_l"], 1)
                        e.matmul(psV[c % 2][:, :], w[:, 2, :], Y[:, cols(c)], start=True, stop=True).then_inc(S["v_in_psum_l"], 1)
                    for c in range(NCH):
                        if c >= 2:
                            e.wait_ge(S["q_scaled"], c - 1)
                        e.matmul(psQ[c % 2][:, :], w[:, 0, :], Y[:, cols(c)], start=True, stop=True).then_inc(S["q_in_psum_l"], 1)

                @block.scalar
                def _(e):
                    for c in range(NCH):
                        e.wait_ge(S["k_in_psum_l"], c + 1)
                        if c >= 2:
                            e.wait_ge(S["kv_done"], c - 1)
                        e.activation(k_sb[c % 2][:, :], psK[c % 2][:, :], ACT.Identity, bias=bias[:, 1:2]).then_inc(S["k_copied"], 1)
                    e.wait_ge(S["bqkv_done"], 1)
                    for c in range(NCH):
                        e.wait_ge(S["q_in_psum_l"], c + 1)
                        if c >= 2:
                            e.wait_ge(S["q_added"], c - 1)
                        e.activation(t_sb[c % 2][:, :], psQ[c % 2][:, :], ACT.Identity, bias=bqkv[:, 0:1],
                                     scale=kv[:, 0:1]).then_inc(S["q_scaled"], 1)

                @block.vector
                def _(e):
                    for c in range(NCH):
                        e.wait_ge(S["v_in_psum_l"], c + 1)
                        e.wait_ge(S["k_copied"], c + 1)
                        if c >= 1:
                            e.wait_ge(S["kv_done"], c)
                        e.scalar_tensor_tensor(kv_all[:, :], psV[c % 2][:, :], bias[:, 2:3], k_sb[c % 2][:, :],
                                               ALU.add, ALU.mult, accum_out=kvp[:, c:c + 1]).then_inc(S["kv_done"], 1)
                    e.wait_ge(S["kv_done"], NCH)
                    e.tensor_reduce(kv[:, :], kvp[:, :], AX.X, ALU.add).then_inc(S["kv_summed"], 1)
                    e.wait_ge(S["kv_summed"], 1)
                    e.tensor_tensor(bqkv[:, :], kv[:, :], bias[:, 0:1], ALU.mult).then_inc(S["bqkv_done"], 1)

                @block.gpsimd
                def _(e):
                    for c in range(NCH):
                        e.wait_ge(S["q_scaled"], c + 1)
                        e.tensor_tensor(X[:, cols(c)], X[:, cols(c)], t_sb[c % 2][:, :], ALU.add).then_inc(S["q_added"], 1)


UPAD = 4
UL = L + UPAD


def mixing_weights(nc, T, G):
    with ExitStack() as ctx:
        sb, _ = allocator(nc, ctx, "_mix")
        z, g, e1, y, oh, wt = (sb("mx_" + n, [128, 4]) for n in ("z", "g", "e", "y", "oh", "w"))
        m1, s1, r1, free = (sb("mx_" + n, [128, 1]) for n in ("m", "s", "r", "free"))
        sig, quarter = sb("mx_sig", [128, NF]), sb("mx_quarter", [128, NF])
        raw = [sb(f"mx_raw{i}", [128, 4, NF // 2 * 128]) for i in range(2)]
        raw_u = sb("mx_rawu", [128, 4, 3 * 128])
        mixed = [sb(f"mx_mixed{i}", [128, NF // 2, 128]) for i in range(2)]
        S = Stage(nc, ctx, ["small_loaded", ("mat_loaded", 4), "mu_loaded", "chain", "sig_done", "acc_step",
                            "high_done", "split_done"])
        with S.block() as block:
            @block.sync
            def _(e):
                row = lambda n: T[n][0, :].partition_broadcast(128)
                loads = [(z, row("log_weights")), (g, row("gumbel")), (sig, row("sigma")),
                         (quarter, T["c_quarter"]), (G["sign"], T["c_sign"])]
                for dst, src in loads:
                    e.dma_start(dst[:, :], src).then_inc(S["small_loaded"], 16)
                e.dma_start(raw_u[:, :, :], T["m_u"].rearrange("d i t e -> d i (t e)")).then_inc(S["mu_loaded"], 16)
                for n, name in enumerate(("m_plus", "m_minus")):
                    for part in range(2):
                        i = 2 * n + part
                        if i >= 2:
                            e.wait_ge(S["acc_step"], 5 * (i - 1))
                        k0 = part * NF // 2
                        e.dma_start(raw[i % 2][:, :, :], T[name][:, :, k0:k0 + NF // 2, :].rearrange("d i k e -> d i (k e)"))\
                            .then_inc(S["mat_loaded"][i], 16)
                e.wait_ge(S["mat_loaded"][3], 16)

            @block.gpsimd
            def _(e):
                e.wait_ge(S["small_loaded"], 80)
                e.tensor_tensor(sig[:, :], sig[:, :], quarter[:, :], ALU.pow).then_inc(S["sig_done"], 1)
                e.memset(G["U"][:, 0, 0:UPAD], 0.0)
                e.memset(G["U"][:, 1, 0:UPAD], 0.0)

            @block.scalar
            def _(e):
                e.wait_ge(S["chain"], 3)
                e.activation(e1[:, :], z[:, :], ACT.Exp).then_inc(S["chain"], 1)
                for i in range(4):
                    e.wait_ge(S["acc_step"], 5 * (i + 1))
                    n, k0 = i // 2, i % 2 * (NF // 2)
                    e.activation(G["Mh"][n][:, k0:k0 + NF // 2, :], mixed[i % 2][:, :, :], ACT.Copy).then_inc(S["high_done"], 1)

            @block.vector
            def _(e):
                count = [0]

                def link(op):
                    count[0] += 1
                    op.then_inc(S["chain"], 1)
                    e.wait_ge(S["chain"], count[0])

                e.wait_ge(S["small_loaded"], 80)
                link(e.tensor_tensor(z[:, :], z[:, :], g[:, :], ALU.add))
                link(e.tensor_reduce(m1[:, :], z[:, :], AX.X, ALU.max))
                link(e.tensor_scalar(z[:, :], z[:, :], m1[:, 0:1], None, ALU.subtract))
                count[0] += 1
                e.wait_ge(S["chain"], 4)
                link(e.tensor_reduce(s1[:, :], e1[:, :], AX.X, ALU.add))
                link(e.reciprocal(r1[:, :], s1[:, :]))
                link(e.tensor_scalar(y[:, :], e1[:, :], r1[:, 0:1], None, ALU.mult))
                link(e.tensor_reduce(m1[:, :], y[:, :], AX.X, ALU.max))
                link(e.tensor_scalar(oh[:, :], y[:, :], m1[:, 0:1], None, ALU.is_ge))
                for i in range(1, 4):
                    link(e.tensor_reduce(s1[:, :], oh[:, 0:i], AX.X, ALU.add))
                    link(e.tensor_scalar(free[:, :], s1[:, :], -1.0, 1.0, ALU.mult, ALU.add))
                    link(e.tensor_tensor(oh[:, i:i + 1], oh[:, i:i + 1], free[:, :], ALU.mult))
                link(e.tensor_tensor(wt[:, :], oh[:, :], y[:, :], ALU.subtract))
                link(e.tensor_tensor(wt[:, :], wt[:, :], y[:, :], ALU.add))
                for c in range(NCH):
                    n = sum(c < NCH >> i for i in range(4))
                    op = e.tensor_reduce(G["keep"][:, c:c + 1], oh[:, 0:n], AX.X, ALU.add)
                link(op)
                steps = [0]

                def mix(dst, src):
                    for i in range(4):
                        if i == 0:
                            op = e.tensor_scalar(dst, src(i), wt[:, 0:1], None, ALU.mult)
                        else:
                            op = e.scalar_tensor_tensor(dst, src(i), wt[:, i:i + 1], dst, ALU.mult, ALU.add)
                        steps[0] += 1
                        op.then_inc(S["acc_step"], 1)
                        e.wait_ge(S["acc_step"], steps[0])

                e.wait_ge(S["sig_done"], 1)
                for n in range(2):
                    for part in range(2):
                        i, k0 = 2 * n + part, part * NF // 2
                        e.wait_ge(S["mat_loaded"][i], 16)
                        dst = mixed[i % 2][:, :, :]
                        if i >= 2:
                            e.wait_ge(S["split_done"], i - 1)
                        mix(dst.rearrange("d k e -> d (k e)"), lambda x, i=i: raw[i % 2][:, x, :])
                        steps[0] += 1
                        e.tensor_tensor(dst, dst, sig[:, k0:k0 + NF // 2].unsqueeze(2).to_broadcast([128, NF // 2, 128]),
                                        ALU.mult).then_inc(S["acc_step"], 1)
                        e.wait_ge(S["high_done"], i + 1)
                        e.tensor_tensor(G["Ml"][n][:, k0:k0 + NF // 2, :], dst, G["Mh"][n][:, k0:k0 + NF // 2, :],
                                        ALU.subtract).then_inc(S["split_done"], 1)
                e.wait_ge(S["mu_loaded"], 16)
                mix(G["Mu"][:, :, :].rearrange("d t e -> d (t e)"), lambda x: raw_u[:, x, :])


def spectral_inputs(nc, T, G):
    PC = 2048
    with ExitStack() as ctx:
        sb, pb = allocator(nc, ctx, "_fwd")
        u_blk = sb("fw_u", [128, 128 * R])
        fwd = sb("fw_m", [128, B, 128])
        out = [sb(f"fw_o{i}", [128, PC]) for i in range(2)]
        phi, flt = sb("fw_phi", [128, NF, 2 * R]), sb("fw_flt", [128, 2, 128])
        fo = sb("fw_fo", [128, 2, NF, 2 * R])
        ps = [pb(f"fw_ps{i}", [128, CH]) for i in range(4)]
        NP = B * 128 * R // PC
        S = Stage(nc, ctx, ["u_stored", ("u_loaded", 4), "fwd_loaded", "phi_loaded", "f_in_psum", "f_copied",
                            ("piece_stored", NP), "filt_stored"])
        with S.block() as block:
            @block.sync
            def _(e):
                for b in range(B):
                    e.dma_start(T["u_blocks"][b].rearrange("j d s -> d j s"),
                                G["U"][:, b, UPAD:].rearrange("d (j s) -> d j s", s=R)).then_inc(S["u_stored"], 16)
                e.wait_ge(S["u_stored"], 32)
                for p in range(4):
                    q = 128 * R // 4
                    e.dma_start(u_blk[:, p * q:(p + 1) * q],
                                T["u_blocks"].rearrange("b j d s -> (b j) (d s)")[:, p * q:(p + 1) * q])\
                        .then_inc(S["u_loaded"][p], 16)
                for p in range(NP):
                    e.wait_ge(S["f_copied"], 8 + 4 * (p + 1))
                    e.dma_start(T["u_hat"][:, p * PC:(p + 1) * PC], out[p % 2][:, :]).then_inc(S["piece_stored"][p], 16)
                for p in range(NP - 2, NP):
                    e.wait_ge(S["piece_stored"][p], 16)

            @block.scalar
            def _(e):
                e.dma_start(phi[:, :, :], T["phi_blocks"]).then_inc(S["phi_loaded"], 16)
                e.dma_start(flt[:, :, :], T["c_flt"]).then_inc(S["phi_loaded"], 16)
                e.dma_start(fwd[:, :, :], T["c_fwd"]).then_inc(S["fwd_loaded"], 16)
                e.wait_ge(S["fwd_loaded"], 16)
                e.wait_ge(S["f_copied"], 8)
                for part in range(2):
                    e.dma_start(T["filt_hat"][0:2 * SLOTS, :, part, :], fo[:, part, :, :]).then_inc(S["filt_stored"], 16)
                e.wait_ge(S["filt_stored"], 32)

            @block.tensor
            def _(e):
                e.wait_ge(S["phi_loaded"], 32)
                for n in range(8 + NP * 4):
                    if n >= 4:
                        e.wait_ge(S["f_copied"], n - 3)
                    if n < 8:
                        part, k0 = n // 4, (n % 4) * 4
                        e.matmul(ps[n % 4][:, :], flt[:, part, :], phi[:, k0:k0 + 4, :].rearrange("a k m -> a (k m)"),
                                 start=True, stop=True).then_inc(S["f_in_psum"], 1)
                    else:
                        b, c = divmod(n - 8, NP * 2)
                        if n == 8:
                            e.wait_ge(S["fwd_loaded"], 16)
                        if b == 0 and c % 4 == 0:
                            e.wait_ge(S["u_loaded"][c // 4], 16)
                        e.matmul(ps[n % 4][:, :], fwd[:, b, :], u_blk[:, c * CH:(c + 1) * CH], start=True, stop=True)\
                            .then_inc(S["f_in_psum"], 1)

            @block.vector
            def _(e):
                for n in range(8 + NP * 4):
                    e.wait_ge(S["f_in_psum"], n + 1)
                    if n < 8:
                        part, k0 = n // 4, (n % 4) * 4
                        dst = fo[:, part, k0:k0 + 4, :].rearrange("a k m -> a (k m)")
                    else:
                        p, c = divmod(n - 8, 4)
                        if p >= 2 and c == 0:
                            e.wait_ge(S["piece_stored"][p - 2], 16)
                        dst = out[p % 2][:, c * CH:(c + 1) * CH].rearrange("c (d s) -> c d s", s=R)[:, :, ::-1]
                    src = ps[n % 4][:, :] if n < 8 else ps[n % 4][:, :].rearrange("c (d s) -> c d s", s=R)
                    e.tensor_copy(dst, src).then_inc(S["f_copied"], 1)


def spectral_slots(nc, T, G):
    NE = 4 * 4
    NPV = 6
    AHEAD = 2
    with ExitStack() as ctx:
        sb, pb = allocator(nc, ctx, "_slot")
        u_raw = [sb(f"sl_u{i}", [128, B, 2, R]) for i in range(AHEAD)]
        f_raw = [sb(f"sl_f{i}", [128, NF, 2, R]) for i in range(AHEAD)]
        u_in = [[sb(f"sl_u{p}{i}", [128, B, 2, R], F32R) for p in "hl"] for i in range(2)]
        f_in = [sb(f"sl_f{p}", [128, NF, 2, R], F32R) for p in "hl"]
        v = [sb(f"sl_v{p}", [128, NF, 2, B, 128], F32R) for p in "hl"]
        t_sb = [sb(f"sl_t{i}", [128, B * 128]) for i in range(2)]
        y_sb = [sb(f"sl_y{i}", [128, B * 128]) for i in range(2)]
        psV = [pb(f"sl_psV{i}", [128, CH]) for i in range(NPV)]
        psY = [pb(f"sl_psY{i}", [128, CH]) for i in range(2)]
        S = Stage(nc, ctx, [("slot_loaded", SPB + AHEAD), "u_high", "u_split", "f_high", "f_split", "f_used", "v_high", "v_split",
                            "v_in_psum_s", "y_minus", "y_sum", ("y_stored", SPB)])
        signs = G["sign"][:, 0:1]

        def load(e, u, slot):
            uh = T["u_hat"].rearrange("(g i) (b d s) -> g i b d s", i=2, b=B, s=R)
            for b in range(B):
                src = uh[ds(slot, 1), :, b, :, :].rearrange("g i d s -> d (g i) s")
                e.dma_start(u_raw[u % AHEAD][:, b, :, :], src).then_inc(S["slot_loaded"][u], 16)
            for part in range(2):
                row = T["filt_hat"][ds(slot * 2 + part, 1), :, :, :]
                src = bass.AP(row.tensor, row.offset, [[1, R], [2 * R, NF * 2], [1, R]])
                e.dma_start(f_raw[u % AHEAD][part * R:(part + 1) * R, :, :, :].rearrange("p k o r -> p (k o) r"), src)\
                    .then_inc(S["slot_loaded"][u], 16)

        with S.block() as block:
            @block.sync
            def _(e):
                for u in range(AHEAD):
                    load(e, u, u)
                for u in range(AHEAD):
                    e.wait_ge(S["slot_loaded"][u], 64)

        def body(slot0, last):
            with S.block() as block:
                @block.sync
                def _(e):
                    loads = SPB if last else SPB + AHEAD
                    for u in range(SPB):
                        if u + AHEAD < loads:
                            e.wait_ge(S["f_split"], 2 * (u + 1))
                            load(e, u + AHEAD, slot0 + (u + AHEAD))
                        e.wait_ge(S["y_sum"], u + 1)
                        e.dma_start(T["y_hat"][ds(slot0 * 128 + u * 128, 128), :], y_sb[u % 2][:, :])\
                            .then_inc(S["y_stored"][u], 16)
                    for u in range(SPB, loads):
                        e.wait_ge(S["slot_loaded"][u], 64)
                    for u in range(SPB):
                        e.wait_ge(S["y_stored"][u], 16)

                @block.gpsimd
                def _(e):
                    for u in range(SPB):
                        if u >= AHEAD:
                            e.wait_ge(S["slot_loaded"][u], 64)
                        if u >= 2:
                            e.wait_ge(S["v_in_psum_s"], NE * (u - 1))
                        flat = lambda t: t.rearrange("p a b c -> p (a b c)")
                        uh, ul, raw = (flat(t[:, :, :, :]) for t in (*u_in[u % 2], u_raw[u % AHEAD]))
                        e.tensor_copy(uh, raw).then_inc(S["u_high"], 1)
                        e.wait_ge(S["u_high"], u + 1)
                        e.tensor_tensor(ul, raw, uh, ALU.subtract).then_inc(S["u_split"], 1)
                        for part in range(2):
                            n = 2 * u + part
                            if u >= 1:
                                e.wait_ge(S["f_used"], n - 1)
                            fh, fl, raw = (flat(t[:, part * NF // 2:(part + 1) * NF // 2, :, :]) for t in (*f_in, f_raw[u % AHEAD]))
                            e.tensor_copy(fh, raw).then_inc(S["f_high"], 1)
                            e.wait_ge(S["f_high"], n + 1)
                            e.tensor_tensor(fl, raw, fh, ALU.subtract).then_inc(S["f_split"], 1)

                @block.tensor
                def _(e):
                    for u in range(SPB):
                        e.wait_ge(S["u_split"], u + 1)
                        for kc in range(4):
                            for q in range(4):
                                b, pm = divmod(q, 2)
                                n = u * NE + kc * 4 + q
                                if n >= NPV:
                                    e.wait_ge(S["v_split"], n - NPV + 1)
                                product(e, psV[n % NPV][:, :], [t[:, b, :, :].rearrange("d i s -> d (i s)") for t in u_in[u % 2]],
                                        [G[m][pm][:, kc * 4:kc * 4 + 4, :].rearrange("d k e -> d (k e)") for m in ("Mh", "Ml")],
                                        True, True).then_inc(S["v_in_psum_s"], 1)
                        if u >= 2:
                            e.wait_ge(S["y_sum"], u - 1)
                        for k in range(NF):
                            if k % (NF // 2) == 0:
                                e.wait_ge(S["f_split"], 2 * u + k // (NF // 2) + 1)
                            if k % 4 == 0:
                                e.wait_ge(S["v_split"], u * NE + k + 4)
                            mm = product(e, psY[u % 2][:, :], [t[:, k, :, :].rearrange("p o r -> p (o r)") for t in f_in],
                                         [t[:, k, :, :, :].rearrange("p m b e -> p (m b e)") for t in v], k == 0, k == NF - 1)
                            if k % (NF // 2) == NF // 2 - 1:
                                mm.then_inc(S["f_used"], 1)

                def v_part(part, n):
                    kc, q = divmod(n % NE, 4)
                    b, pm = divmod(q, 2)
                    return v[part][:, kc * 4:kc * 4 + 4, pm, b, :]

                bank = lambda n: psV[n % NPV][:, :].rearrange("p (k e) -> p k e", k=4)

                @block.scalar
                def _(e):
                    for u in range(SPB):
                        for n in range(u * NE, (u + 1) * NE):
                            e.wait_ge(S["v_in_psum_s"], n + 1)
                            if u >= 1 and n == u * NE:
                                e.wait_ge(S["f_used"], 2 * u)
                            e.activation(v_part(0, n), bank(n), ACT.Copy, scale=signs if n % 2 else 1.0)\
                                .then_inc(S["v_high"], 1)
                        e.wait_ge(S["f_used"], 2 * (u + 1))
                        if u >= 2:
                            e.wait_ge(S["y_sum"], u - 1)
                        e.activation(t_sb[u % 2][:, :], psY[u % 2][:, B * 128:], ACT.Copy, scale=signs).then_inc(S["y_minus"], 1)

                @block.vector
                def _(e):
                    for u in range(SPB):
                        for n in range(u * NE, (u + 1) * NE):
                            e.wait_ge(S["v_high"], n + 1)
                            if n % 2:
                                e.scalar_tensor_tensor(v_part(1, n), bank(n), signs, v_part(0, n), ALU.mult, ALU.subtract)\
                                    .then_inc(S["v_split"], 1)
                            else:
                                e.tensor_tensor(v_part(1, n), bank(n), v_part(0, n), ALU.subtract).then_inc(S["v_split"], 1)
                        e.wait_ge(S["y_minus"], u + 1)
                        if u >= 2:
                            e.wait_ge(S["y_stored"][u - 2], 16)
                        e.tensor_tensor(y_sb[u % 2][:, :], psY[u % 2][:, 0:B * 128], t_sb[u % 2][:, :], ALU.subtract)\
                            .then_inc(S["y_sum"], 1)

        with nc.Fori(0, SLOTS // SPB - 1) as it:
            body(it * SPB, False)
        body(SLOTS - SPB, True)


def spectral_inverse(nc, T):
    PC, NP = 2048, 8
    with ExitStack() as ctx:
        sb, pb = allocator(nc, ctx, "_inv")
        y_in = sb("iv_y", [128, NP, PC])
        inv = sb("iv_m", [128, NB])
        out = [sb(f"iv_o{i}", [NB, PC]) for i in range(2)]
        ps = [pb(f"iv_ps{i}", [128, CH]) for i in range(4)]
        S = Stage(nc, ctx, ["inv_loaded", ("yh_loaded", NP), "i_in_psum", "i_act", "i_dve", ("o_stored", NP)])
        with S.block() as block:
            @block.sync
            def _(e):
                for p in range(NP):
                    e.dma_start(y_in[:, p, :], T["y_hat"].rearrange("(c r) w -> c (r w)", r=R)[:, p * PC:(p + 1) * PC])\
                        .then_inc(S["yh_loaded"][p], 16)
                for p in range(NP):
                    e.wait_ge(S["i_act"], 2 * (p + 1))
                    e.wait_ge(S["i_dve"], 2 * (p + 1))
                    e.dma_start(T["y_seq"].rearrange("(i r) w -> i (r w)", r=R)[:, p * PC:(p + 1) * PC], out[p % 2][:, :])\
                        .then_inc(S["o_stored"][p], 16)
                for p in range(NP):
                    e.wait_ge(S["o_stored"][p], 16)

            @block.scalar
            def _(e):
                e.dma_start(inv[:, :], T["c_inv"]).then_inc(S["inv_loaded"], 16)
                for n in range(0, 4 * NP, 2):
                    e.wait_ge(S["i_in_psum"], n + 1)
                    p, c = divmod(n, 4)
                    if p >= 2 and c == 0:
                        e.wait_ge(S["o_stored"][p - 2], 16)
                    e.activation(out[p % 2][:, c * CH:(c + 1) * CH], ps[n % 4][0:NB, :], ACT.Copy).then_inc(S["i_act"], 1)

            @block.vector
            def _(e):
                for n in range(1, 4 * NP, 2):
                    e.wait_ge(S["i_in_psum"], n + 1)
                    p, c = divmod(n, 4)
                    if p >= 2 and c == 1:
                        e.wait_ge(S["o_stored"][p - 2], 16)
                    e.tensor_copy(out[p % 2][:, c * CH:(c + 1) * CH], ps[n % 4][0:NB, :]).then_inc(S["i_dve"], 1)

            @block.tensor
            def _(e):
                e.wait_ge(S["inv_loaded"], 16)
                for n in range(4 * NP):
                    p, c = divmod(n, 4)
                    if c == 0:
                        e.wait_ge(S["yh_loaded"][p], 16)
                    if n >= 4:
                        e.wait_ge(S["i_act"] if n % 2 == 0 else S["i_dve"], (n - 4) // 2 + 1)
                    e.matmul(ps[n % 4][0:NB, :], inv[:, :], y_in[:, p, c * CH:(c + 1) * CH], start=True, stop=True)\
                        .then_inc(S["i_in_psum"], 1)


def autoregressive(nc, T, G):
    X = T["X"]
    with ExitStack() as ctx:
        _, pb = allocator(nc, ctx, "_ar")
        ps = [pb(f"ar_ps{i}", [128, CH]) for i in range(2)]
        S = Stage(nc, ctx, ["ar_in_psum", "ar_added"])
        with nc.Fori(0, B) as b:
            with S.block() as block:
                @block.tensor
                def _(e):
                    for c in range(NCH):
                        if c >= 2:
                            e.wait_ge(S["ar_added"], c - 1)
                        for i in range(3):
                            mm = e.matmul(ps[c % 2][:, :], G["Mu"][:, i, :],
                                          G["U"][:, :, :].rearrange("p b c -> p (b c)")[:, ds(b * UL + UPAD + c * CH - i, CH)],
                                          start=(i == 0), stop=(i == 2))
                        mm.then_inc(S["ar_in_psum"], 1)

                @block.vector
                def _(e):
                    for c in range(NCH):
                        e.wait_ge(S["ar_in_psum"], c + 1)
                        x = X[:, ds(b * L + c * CH, CH)]
                        e.scalar_tensor_tensor(x, ps[c % 2][:, :], G["keep"][:, c:c + 1], x, ALU.mult, ALU.add)\
                            .then_inc(S["ar_added"], 1)


def spectral_output(nc, T, G):
    X = T["X"]
    with ExitStack() as ctx:
        sb, pb = allocator(nc, ctx, "_so")
        o_in = [sb(f"so_o{i}", [128, TPC, 128]) for i in range(NCH)]
        ps = [pb(f"so_ps{i}", [128, CH]) for i in range(2)]
        S = Stage(nc, ctx, [("seq_loaded", NCH), "so_in_psum", "so_added"])
        with nc.Fori(0, B) as b:
            with S.block() as block:
                @block.sync
                def _(e):
                    seq = T["y_seq"].rearrange("t (b c) -> t b c", b=B)
                    for c in range(NCH):
                        src = seq[c * CH:(c + 1) * CH, ds(b, 1), :].rearrange("(j p) b c -> p (j b) c", p=128)
                        e.dma_start(o_in[c][:, :, :], src).then_inc(S["seq_loaded"][c], 16)
                    for c in range(NCH):
                        e.wait_ge(S["seq_loaded"][c], 16)

                @block.tensor
                def _(e):
                    for c in range(NCH):
                        if c >= 2:
                            e.wait_ge(S["so_added"], c - 1)
                        e.wait_ge(S["seq_loaded"][c], 16)
                        for j in range(TPC):
                            tr = e.transpose(ps[c % 2][:, j * 128:(j + 1) * 128], o_in[c][:, j, :], T["ident"][:, :])
                        tr.then_inc(S["so_in_psum"], 1)

                @block.vector
                def _(e):
                    for c in range(NCH):
                        e.wait_ge(S["so_in_psum"], c + 1)
                        x = X[:, ds(b * L + c * CH, CH)]
                        e.scalar_tensor_tensor(x, ps[c % 2][:, :], G["keep"][:, c:c + 1], x, ALU.mult, ALU.add)\
                            .then_inc(S["so_added"], 1)


def spectral_bank(nc, T):
    with ExitStack() as ctx:
        sb, _ = allocator(nc, ctx, "_sp")
        G = {"sign": sb("sp_sign", [128, 1]), "keep": sb("sp_keep", [128, NCH])}
        for part in "hl":
            G["M" + part] = [sb(f"sp_M{part}{n}", [128, NF, 128], F32R) for n in range(2)]
        with ExitStack() as inner:
            sbi, _ = allocator(nc, inner, "_sp")
            G["U"], G["Mu"] = sbi("sp_U", [128, B, UL]), sbi("sp_Mu", [128, 3, 128])
            flat = G["U"][:, :, :].rearrange("p b c -> p (b c)")
            mixing_weights(nc, T, G)
            layer_norm_tokens(nc, T, T["X"], lambda b, half, u: flat[:, ds(b * UL + half * (4 * CH) + (UPAD + u * CH), CH)],
                              "sp")
            spectral_inputs(nc, T, G)
            autoregressive(nc, T, G)
        spectral_slots(nc, T, G)
        spectral_inverse(nc, T)
        spectral_output(nc, T, G)


def causal_attention(nc, T):
    X, Y = T["X"], T["Y"]
    NT = L // 128
    scale = float(C) ** -0.5
    with ExitStack() as ctx:
        sb, pb = allocator(nc, ctx, "_ca")
        w, causal = sb("ca_w", [128, 3, 128]), sb("ca_mask", [128, CH])
        q_all, k_all = ([sb(f"ca_{n}{p}", [128, L], F32R) for p in "hl"] for n in "qk")
        v_all = sb("ca_v", [128, NT, 128])
        with ExitStack() as inner:
            sbi, pbi = allocator(nc, inner, "_cai")
            S = Stage(nc, inner, ["ca_loaded"])
            with S.block() as block:
                @block.sync
                def _(e):
                    e.dma_start(w[:, :, :], T["ca_w"]).then_inc(S["ca_loaded"], 16)
                    e.dma_start(causal[:, :], T["c_causal"]).then_inc(S["ca_loaded"], 16)
                    e.wait_ge(S["ca_loaded"], 32)
        s_sb = [sb(f"ca_s{i}", [128, L]) for i in range(2)]
        pt_sb = [sb(f"ca_pt{i}", [128, TPC, 128]) for i in range(3)]
        z_in = [s_sb[i][:, 0:CH] for i in range(2)]
        mx, nm, rs, ri = sb("ca_mx", [128, NT, NCH]), sb("ca_nm", [128, NT]), sb("ca_rs", [128, NT]), sb("ca_ri", [128, NT])
        o_sb = [sb(f"ca_o{i}", [128, 128]) for i in range(2)]
        ps = [pb(f"ca_ps{i}", [128, CH]) for i in range(8)]
        psS, psT, psO, psX = ps[0:3], ps[3:5], ps[5:7], ps[7]
        width = lambda i, c: min(CH, (i + 1) * 128 - c * CH)
        pieces = [(i, c) for i in range(NT) for c in range(i // TPC + 1)]
        P = Stage(nc, ctx, ["z_staged", "q_in_psum_c", "k_in_psum_c", "v_in_psum_c", "q_high_c", "k_high_c",
                            "q_out_c", "k_out_c", "v_out_c"])
        S = Stage(nc, ctx, ["s_in_psum_c", "s_copied", "nmax_done", "p_done_c", "pt_in_psum_c", "pt_act", "pt_dve", "pv_piece",
                            "pv_done", "ri_done_c", "o_scaled_c", "ox_in_psum", "x_added_c"])
        with nc.Fori(0, B) as b:
            with P.block() as block:
                @block.tensor
                def _(e):
                    for c in range(NCH):
                        e.wait_ge(P["z_staged"], c + 1)
                        if c >= 2:
                            e.wait_ge(P["q_out_c"], c - 1)
                            e.wait_ge(P["k_out_c"], c - 1)
                            e.wait_ge(P["v_out_c"], c - 1)
                        e.matmul(ps[c % 2][:, :], w[:, 0, :], z_in[c % 2], start=True, stop=True).then_inc(P["q_in_psum_c"], 1)
                        e.matmul(ps[2 + c % 2][:, :], w[:, 1, :], z_in[c % 2], start=True, stop=True).then_inc(P["k_in_psum_c"], 1)
                        for j in range(TPC):
                            mm = e.matmul(ps[4 + c % 2][:, j * 128:(j + 1) * 128], z_in[c % 2][:, j * 128:(j + 1) * 128],
                                          w[:, 2, :], start=True, stop=True)
                        mm.then_inc(P["v_in_psum_c"], 1)

                @block.scalar
                def _(e):
                    for c in range(NCH):
                        e.wait_ge(P["q_in_psum_c"], c + 1)
                        e.activation(q_all[0][:, c * CH:(c + 1) * CH], ps[c % 2][:, :], ACT.Copy, scale=scale)\
                            .then_inc(P["q_high_c"], 1)
                        e.wait_ge(P["k_in_psum_c"], c + 1)
                        e.activation(k_all[0][:, c * CH:(c + 1) * CH], ps[2 + c % 2][:, :], ACT.Copy).then_inc(P["k_high_c"], 1)
                        e.wait_ge(P["v_in_psum_c"], c + 1)
                        e.activation(v_all[:, c * TPC:(c + 1) * TPC, :].rearrange("p j d -> p (j d)"), ps[4 + c % 2][:, :],
                                     ACT.Copy).then_inc(P["v_out_c"], 1)

                @block.vector
                def _(e):
                    def stage(c):
                        if c >= 2:
                            e.wait_ge(P["v_in_psum_c"], c - 1)
                        e.tensor_copy(z_in[c % 2], Y[:, ds(b * L + c * CH, CH)]).then_inc(P["z_staged"], 1)

                    stage(0)
                    for c in range(NCH):
                        if c + 1 < NCH:
                            stage(c + 1)
                        q_high, q_low, k_high, k_low = (t[:, c * CH:(c + 1) * CH] for t in (*q_all, *k_all))
                        e.wait_ge(P["q_high_c"], c + 1)
                        e.scalar_tensor_tensor(q_low, ps[c % 2][:, :], scale, q_high, ALU.mult, ALU.subtract)\
                            .then_inc(P["q_out_c"], 1)
                        e.wait_ge(P["k_high_c"], c + 1)
                        e.tensor_tensor(k_low, ps[2 + c % 2][:, :], k_high, ALU.subtract).then_inc(P["k_out_c"], 1)

            with S.block() as block:
                first = {}
                for n, (i, c) in enumerate(pieces):
                    first.setdefault(i, n)
                last = {i: n for n, (i, c) in enumerate(pieces)}
                on_act = lambda n: n % 2 == 0
                copied_by = lambda n: (n // 2 + 1)

                @block.tensor
                def _(e):
                    def scores(i):
                        for c in range(i // TPC + 1):
                            n = first[i] + c
                            if n >= 3:
                                e.wait_ge(S["s_copied"], n - 2)
                            product(e, psS[n % 3][:, 0:width(i, c)], [q[:, i * 128:(i + 1) * 128] for q in q_all],
                                    [k[:, c * CH:c * CH + width(i, c)] for k in k_all], True, True).then_inc(S["s_in_psum_c"], 1)

                    def turn(n):
                        i, c = pieces[n]
                        if c == 0:
                            e.wait_ge(S["p_done_c"], i + 1)
                        if n >= 2:
                            e.wait_ge(S["pt_act"] if on_act(n - 2) else S["pt_dve"], copied_by(n - 2))
                        for j in range(width(i, c) // 128):
                            at = c * CH + j * 128
                            tr = e.transpose(psT[n % 2][:, j * 128:(j + 1) * 128], s_sb[i % 2][:, at:at + 128], T["ident"][:, :])
                        tr.then_inc(S["pt_in_psum_c"], 1)

                    def values(n):
                        i, c = pieces[n]
                        e.wait_ge(S["pt_act"] if on_act(n) else S["pt_dve"], copied_by(n))
                        if c == 0 and i >= 2:
                            e.wait_ge(S["o_scaled_c"], i - 1)
                        for j in range(width(i, c) // 128):
                            k = c * TPC + j
                            mm = e.matmul(psO[i % 2][:, 0:128], pt_sb[n % 3][:, j, :], v_all[:, k, :],
                                          start=(k == 0), stop=(k == i))
                        mm.then_inc(S["pv_piece"], 1)

                    def output(i):
                        e.wait_ge(S["o_scaled_c"], i + 1)
                        if i >= 1:
                            e.wait_ge(S["x_added_c"], i)
                        e.transpose(psX[:, 0:128], o_sb[i % 2][:, :], T["ident"][:, :]).then_inc(S["ox_in_psum"], 1)

                    scores(0)
                    for i in range(NT):
                        if i + 1 < NT:
                            scores(i + 1)
                        for n in range(first[i], last[i] + 1):
                            turn(n)
                            if n > first[i]:
                                values(n - 1)
                        values(last[i])
                        if i >= 1:
                            output(i - 1)
                    output(NT - 1)

                @block.vector
                def _(e):
                    def copy_scores(i):
                        for c in range(i // TPC + 1):
                            n = first[i] + c
                            e.wait_ge(S["s_in_psum_c"], n + 1)
                            if c == 0 and i >= 2:
                                e.wait_ge(S["pt_in_psum_c"], last[i - 2] + 1)
                            k = width(i, c)
                            dst, m = s_sb[i % 2][:, c * CH:c * CH + k], mx[:, i, c:c + 1]
                            if c == i // TPC:
                                e.tensor_tensor_reduce(out=dst, in0=psS[n % 3][:, 0:k], in1=causal[:, CH - k:], scale=1.0,
                                                       scalar=-2 * BIG, op0=ALU.add, op1=ALU.max, accum_out=m).then_inc(S["s_copied"], 1)
                            else:
                                e.tensor_scalar(dst, psS[n % 3][:, 0:k], 1.0, None, ALU.mult, ALU.max, accum_out=m)\
                                    .then_inc(S["s_copied"], 1)
                        e.wait_ge(S["s_copied"], last[i] + 1)
                        e.tensor_reduce(nm[:, i:i + 1], mx[:, i, 0:i // TPC + 1], AX.X, ALU.max, negate=True).then_inc(S["nmax_done"], 1)

                    def normalise(i):
                        e.wait_ge(S["p_done_c"], i + 1)
                        e.reciprocal(ri[:, i:i + 1], rs[:, i:i + 1]).then_inc(S["ri_done_c"], 1)
                        e.wait_ge(S["ri_done_c"], i + 1)
                        e.wait_ge(S["pv_piece"], last[i] + 1)
                        if i >= 2:
                            e.wait_ge(S["ox_in_psum"], i - 1)
                        e.tensor_scalar(o_sb[i % 2][:, :], psO[i % 2][:, 0:128], ri[:, i:i + 1], None, ALU.mult).then_inc(S["o_scaled_c"], 1)

                    def add(i):
                        e.wait_ge(S["ox_in_psum"], i + 1)
                        x = X[:, ds(b * L + i * 128, 128)]
                        e.tensor_tensor(x, psX[:, 0:128], x, ALU.add).then_inc(S["x_added_c"], 1)

                    copy_scores(0)
                    for i in range(NT):
                        if i + 1 < NT:
                            copy_scores(i + 1)
                        for n in range(first[i], last[i] + 1):
                            if not on_act(n):
                                e.wait_ge(S["pt_in_psum_c"], n + 1)
                                if n >= 3:
                                    e.wait_ge(S["pv_piece"], n - 2)
                                k = width(*pieces[n]) // 128
                                e.tensor_copy(pt_sb[n % 3][:, 0:k, :].rearrange("p j q -> p (j q)"), psT[n % 2][:, 0:k * 128])\
                                    .then_inc(S["pt_dve"], 1)
                        if i >= 1:
                            add(i - 1)
                        normalise(i)
                    add(NT - 1)

                @block.scalar
                def _(e):
                    def exponentials(i):
                        e.wait_ge(S["nmax_done"], i + 1)
                        row = s_sb[i % 2][:, 0:(i + 1) * 128]
                        e.activation(row, row, ACT.Exp, bias=nm[:, i:i + 1], accum_out=rs[:, i:i + 1]).then_inc(S["p_done_c"], 1)

                    exponentials(0)
                    for i in range(NT):
                        for n in range(first[i], last[i] + 1):
                            if on_act(n):
                                e.wait_ge(S["pt_in_psum_c"], n + 1)
                                if n >= 3:
                                    e.wait_ge(S["pv_piece"], n - 2)
                                k = width(*pieces[n]) // 128
                                e.activation(pt_sb[n % 3][:, 0:k, :].rearrange("p j q -> p (j q)"), psT[n % 2][:, 0:k * 128],
                                             ACT.Copy).then_inc(S["pt_act"], 1)
                        if i + 1 < NT:
                            exponentials(i + 1)


def experts(nc, T):
    X, Y = T["X"], T["Y"]
    NT = 16
    NH = NT // TPC
    DV = 4
    with ExitStack() as ctx:
        sb, pb = allocator(nc, ctx, "_ex")
        rw, rb, rank = sb("ex_rw", [128, MOE]), sb("ex_rb", [128, MOE]), sb("ex_rank", [128, MOE])
        ew, eb = sb("ex_ew", [128, MOE, 128]), sb("ex_eb", [128, 128])
        ew_parts = [sb(f"ex_ew{p}", [128, MOE, 128], F32R) for p in "hl"]
        z_in = sb("ex_z", [128, NT, 128])
        z_parts = [sb(f"ex_z{p}", [128, NT, 128], F32R) for p in "hl"]
        lg, t1, oh1, oh2, gates = (sb("ex_" + n, [128, NT, MOE]) for n in ("lg", "t1", "oh1", "oh2", "g"))
        m1, m2 = sb("ex_m1", [128, NT]), sb("ex_m2", [128, NT])
        gate_pad = sb("ex_gp", [128, NT, 128])
        gate_t = [sb(f"ex_gt{i}", [128, 128]) for i in range(2)]
        acc = [sb(f"ex_acc{i}", [128, 128]) for i in range(2)]
        wtd = [sb(f"ex_w{i}", [128, MOE - DV, 128]) for i in range(2)]
        out = [sb(f"ex_out{i}", [128, CH]) for i in range(2)]
        psL = pb("ex_psL", [128, CH])
        psE = [pb(f"ex_psE{i}", [128, CH]) for i in range(4)]
        psG = pb("ex_psG", [128, CH])
        psO = [pb(f"ex_psO{i}", [128, CH]) for i in range(2)]
        S0 = Stage(nc, ctx, ["ex_loaded", "ew_high"])
        with S0.block() as block:
            @block.sync
            def _(e):
                loads = [(rw[:, :], T["router_w"]), (rb[:, :], T["router_b"][0, :].partition_broadcast(128)),
                         (rank[:, :], T["c_rank"]), (ew[:, :, :], T["expert_w"]), (eb[:, :], T["expert_b"])]
                for dst, src in loads:
                    e.dma_start(dst, src).then_inc(S0["ex_loaded"], 16)
                e.wait_ge(S0["ex_loaded"], 16 * len(loads))

            @block.vector
            def _(e):
                e.memset(gate_pad[:, :, :], 0.0)
                e.wait_ge(S0["ex_loaded"], 80)
                e.tensor_copy(ew_parts[0][:, :, :], ew[:, :, :]).then_inc(S0["ew_high"], 1)
                e.wait_ge(S0["ew_high"], 1)
                e.tensor_tensor(ew_parts[1][:, :, :], ew[:, :, :], ew_parts[0][:, :, :], ALU.subtract)
        S = Stage(nc, ctx, ["z_staged_e", "z_high", "z_split", "l_in_psum_e", "gate_chain", "exp_done_e", "g_ready", "gt_in_psum", "gt_copied",
                            "e_in_psum", "weighed_dve", "weighed_act", "acc_step_e", "out_in_psum", "out_done",
                            ("out_stored", NH)])
        with nc.Fori(0, B) as b, nc.Fori(0, L // (NT * 128)) as part:
            base = b * L + part * (NT * 128)
            with S.block() as block:
                @block.tensor
                def _(e):
                    for t in range(NT):
                        if t % TPC == 0:
                            e.wait_ge(S["z_staged_e"], t // TPC + 1)
                        mm = e.matmul(psL[:, t * MOE:(t + 1) * MOE], z_in[:, t, :], rw[:, :], start=True, stop=True)
                    mm.then_inc(S["l_in_psum_e"], 1)

                    def expert_outputs(t):
                        if t >= 2:
                            e.wait_ge(S["weighed_dve"], t - 1)
                            e.wait_ge(S["weighed_act"], t - 1)
                        if t % TPC == 0:
                            e.wait_ge(S["z_split"], t // TPC + 1)
                        for h in range(2):
                            mm = product(e, psE[2 * (t % 2) + h][:, :], [z[:, t, :] for z in z_parts],
                                         [m[:, 4 * h:4 * h + 4, :].rearrange("d e c -> d (e c)") for m in ew_parts], True, True)
                        mm.then_inc(S["e_in_psum"], 1)

                    def gates_turned(t):
                        if t == 0:
                            e.wait_ge(S["g_ready"], 1)
                        if t >= 1:
                            e.wait_ge(S["gt_copied"], t)
                        e.transpose(psG[:, 0:128], gate_pad[:, t, :], T["ident"][:, :]).then_inc(S["gt_in_psum"], 1)

                    def combine(t):
                        h, j = divmod(t, TPC)
                        dst = psO[h % 2][:, j * 128:(j + 1) * 128]
                        if h >= 2 and j == 0:
                            e.wait_ge(S["out_done"], h - 1)
                        e.wait_ge(S["gt_copied"], t + 1)
                        e.matmul(dst, eb[:, :], gate_t[t % 2][:, :], start=True, stop=False)
                        e.wait_ge(S["weighed_dve"], t + 1)
                        e.wait_ge(S["weighed_act"], t + 1)
                        e.matmul(dst, acc[t % 2][:, :], T["ident"][:, :], start=False, stop=False)
                        for x in range(MOE - DV):
                            mm = e.matmul(dst, wtd[t % 2][:, x, :], T["ident"][:, :], start=False, stop=(x == MOE - DV - 1))
                        mm.then_inc(S["out_in_psum"], 1)

                    expert_outputs(0)
                    for t in range(NT):
                        if t + 1 < NT:
                            expert_outputs(t + 1)
                        gates_turned(t)
                        combine(t)

                @block.scalar
                def _(e):
                    for h in range(NH):
                        e.activation(z_in[:, h * TPC:(h + 1) * TPC, :].rearrange("p j t -> p (j t)"),
                                     Y[:, ds(base + h * CH, CH)], ACT.Copy).then_inc(S["z_staged_e"], 1)
                        e.activation(z_parts[0][:, h * TPC:(h + 1) * TPC, :].rearrange("p j t -> p (j t)"),
                                     Y[:, ds(base + h * CH, CH)], ACT.Copy).then_inc(S["z_high"], 1)
                    e.wait_ge(S["gate_chain"], 4)
                    e.activation(lg[:, :, :], lg[:, :, :], ACT.Exp).then_inc(S["exp_done_e"], 1)
                    e.wait_ge(S["g_ready"], 1)
                    for t in range(NT):
                        e.wait_ge(S["e_in_psum"], t + 1)
                        if t >= 2:
                            e.wait_ge(S["out_in_psum"], t - 1)
                        for x in range(DV, MOE):
                            op = e.activation(wtd[t % 2][:, x - DV, :], psE[2 * (t % 2) + 1][:, (x - 4) * 128:(x - 3) * 128],
                                              ACT.Copy, scale=gates[:, t, x:x + 1])
                        op.then_inc(S["weighed_act"], 1)
                        e.wait_ge(S["gt_in_psum"], t + 1)
                        if t >= 2:
                            e.wait_ge(S["out_in_psum"], t - 1)
                        e.activation(gate_t[t % 2][:, :], psG[:, 0:128], ACT.Copy).then_inc(S["gt_copied"], 1)

                @block.vector
                def _(e):
                    count = [0]

                    def link(op):
                        count[0] += 1
                        op.then_inc(S["gate_chain"], 1)
                        e.wait_ge(S["gate_chain"], count[0])

                    for h in range(NH):
                        e.wait_ge(S["z_staged_e"], h + 1)
                        e.wait_ge(S["z_high"], h + 1)
                        js = slice(h * TPC, (h + 1) * TPC)
                        e.tensor_tensor(z_parts[1][:, js, :], z_in[:, js, :], z_parts[0][:, js, :], ALU.subtract)\
                            .then_inc(S["z_split"], 1)
                    wide = lambda v: v.to_broadcast([128, NT, MOE])
                    e.wait_ge(S["l_in_psum_e"], 1)
                    link(e.tensor_tensor(lg[:, :, :], psL[:, 0:NT * MOE].rearrange("p (t x) -> p t x", x=MOE),
                                         wide(rb[:, :].unsqueeze(1)), ALU.add))
                    link(e.tensor_reduce(m1[:, :], lg[:, :, :], AX.X, ALU.max))

                    def first_max(oh, src, m):
                        link(e.tensor_tensor(t1[:, :, :], src, wide(m[:, :].unsqueeze(2)), ALU.is_equal))
                        link(e.tensor_tensor(t1[:, :, :], t1[:, :, :], wide(rank[:, :].unsqueeze(1)), ALU.mult))
                        link(e.tensor_reduce(m2[:, :], t1[:, :, :], AX.X, ALU.max))
                        link(e.tensor_tensor(oh[:, :, :], t1[:, :, :], wide(m2[:, :].unsqueeze(2)), ALU.is_equal))

                    link(e.tensor_copy(gates[:, :, :], lg[:, :, :]))
                    link(e.tensor_tensor(lg[:, :, :], lg[:, :, :], wide(m1[:, :].unsqueeze(2)), ALU.subtract))
                    first_max(oh1, gates[:, :, :], m1)
                    link(e.tensor_scalar(t1[:, :, :], oh1[:, :, :], -BIG, None, ALU.mult))
                    link(e.tensor_tensor(gates[:, :, :], gates[:, :, :], t1[:, :, :], ALU.add))
                    link(e.tensor_reduce(m1[:, :], gates[:, :, :], AX.X, ALU.max))
                    first_max(oh2, gates[:, :, :], m1)
                    link(e.tensor_tensor(oh1[:, :, :], oh1[:, :, :], oh2[:, :, :], ALU.add))
                    e.wait_ge(S["exp_done_e"], 1)
                    link(e.tensor_tensor(oh1[:, :, :], oh1[:, :, :], lg[:, :, :], ALU.mult))
                    link(e.tensor_reduce(m1[:, :], oh1[:, :, :], AX.X, ALU.add))
                    link(e.reciprocal(m2[:, :], m1[:, :]))
                    link(e.tensor_tensor(gates[:, :, :], oh1[:, :, :], wide(m2[:, :].unsqueeze(2)), ALU.mult))
                    e.tensor_copy(gate_pad[:, :, 0:MOE], gates[:, :, :]).then_inc(S["g_ready"], 1)
                    steps = [0]
                    for t in range(NT):
                        e.wait_ge(S["e_in_psum"], t + 1)
                        if t >= 2:
                            e.wait_ge(S["out_in_psum"], t - 1)
                        for x in range(DV):
                            src = psE[2 * (t % 2) + x // 4][:, (x % 4) * 128:(x % 4 + 1) * 128]
                            g = gates[:, t, x:x + 1]
                            if x == 0:
                                op = e.tensor_scalar(acc[t % 2][:, :], src, g, None, ALU.mult)
                            else:
                                op = e.scalar_tensor_tensor(acc[t % 2][:, :], src, g, acc[t % 2][:, :], ALU.mult, ALU.add)
                            if x < DV - 1:
                                steps[0] += 1
                                op.then_inc(S["acc_step_e"], 1)
                                e.wait_ge(S["acc_step_e"], steps[0])
                        op.then_inc(S["weighed_dve"], 1)
                        if t % TPC == TPC - 1:
                            h = t // TPC
                            e.wait_ge(S["out_in_psum"], t + 1)
                            if h >= 2:
                                e.wait_ge(S["out_stored"][h - 2], 16)
                            e.tensor_tensor(out[h % 2][:, :], psO[h % 2][:, :], X[:, ds(base + h * CH, CH)], ALU.add).then_inc(S["out_done"], 1)

                @block.sync
                def _(e):
                    for h in range(NH):
                        e.wait_ge(S["out_done"], h + 1)
                        e.dma_start(T["out"].rearrange("b c t -> c b t")[:, ds(b, 1), ds(part * (NT * 128) + h * CH, CH)],
                                    out[h % 2][:, :].unsqueeze(1)).then_inc(S["out_stored"][h], 16)
                    for h in range(NH):
                        e.wait_ge(S["out_stored"][h], 16)


def build_program(nc, T):
    dram = lambda n, s: nc.dram_tensor(n, s, F32, kind="Internal").ap()
    T["v_dram"] = dram("na_values", (N, C))
    T["u_blocks"] = dram("u_blocks", (B, NB, C, R))
    T["u_hat"] = dram("u_hat", (2 * SLOTS, B * C * R))
    T["filt_hat"] = dram("filt_hat", (2 * SLOTS, NF, 2, 2 * R))
    T["y_hat"] = dram("y_hat", (SLOTS * 2 * R, B * C))
    T["y_seq"] = dram("y_seq", (L, B * C))
    with ExitStack() as ctx:
        sb = lambda n, s: ctx.enter_context(nc.sbuf_tensor(n, s, F32))
        X = T["X"] = sb("X", [128, N])
        T["ident"], T["gmat"], T["eps"] = sb("ident", [128, 128]), sb("gmat", [128, 128]), sb("eps", [128, 1])
        into = lambda img: lambda b, half, u: img[:, ds(b * L + half * (4 * CH) + u * CH, CH)]
        with nc.sbuf_tensor("Y", [128, N], F32) as Y:
            T["Y"] = Y
            load_and_group_norm(nc, T, True)
            neighbourhood_attention(nc, T)
            norm_into_residual(nc, T)
            load_and_group_norm(nc, T, False)
            conv_attention(nc, T)
            layer_norm_tokens(nc, T, X, into(Y), "la")
            linear_attention(nc, T)
        spectral_bank(nc, T)
        with nc.sbuf_tensor("Y2", [128, N], F32) as Y:
            T["Y"] = Y
            layer_norm_tokens(nc, T, X, into(Y), "ca")
            causal_attention(nc, T)
            layer_norm_tokens(nc, T, X, into(Y), "ex")
            experts(nc, T)


def _window_tables():
    row_rel = [0, KW // 2, (H - QR) - (H - RR)]
    col_rel = [0, KW // 2, (W - QC) - (W - RC)]
    at = np.zeros((9, 128, NKEY), np.int64)
    mask = np.zeros((9, 128, NKEY), np.float32)

    def axis(n_q, n_k, rel, kind, size):
        q, k = np.arange(n_q)[:, None] + rel, np.arange(n_k)[None, :]
        start = q - KW // 2
        if kind == 0:
            start = np.maximum(start, 0)
        if kind == 2:
            start = np.minimum(start, n_k - KW)
        inside = (k >= start) & (k < start + KW)
        return np.clip(k - q + KW - 1, 0, 2 * KW - 2), inside

    for rk in range(3):
        ri, rin = axis(QR, RR, row_rel[rk], rk, H)
        for ck in range(3):
            ci, cin = axis(QC, RC, col_rel[ck], ck, W)
            idx = ri[:, None, :, None] * (2 * KW - 1) + ci[None, :, None, :]
            ok = rin[:, None, :, None] & cin[None, :, None, :]
            at[rk * 3 + ck] = idx.reshape(128, NKEY)
            mask[rk * 3 + ck] = np.where(ok, 0.0, BIG).reshape(128, NKEY)
    return at, mask


def _constants():
    f = np.float32
    p = np.arange(128)
    at, mask = _window_tables()
    c = {
        "c_ident": np.eye(128, dtype=f),
        "c_gmat": (p[:, None] // GN_GROUP == p[None, :] // GN_GROUP).astype(f) / GN_GROUP,
        "c_eps": np.full((128, 1), 1e-5, f),
        "c_headmask": (p[:, None] // HD % 2 == np.arange(HEADS)[None, :] % 2).astype(f),
        "c_namask": np.ascontiguousarray(mask.transpose(1, 0, 2)),
    }
    hsum = np.zeros((K2, 128, 128), f)
    for k in range(K2):
        hsum[k, p, k * HEADS + p // HD] = 1.0
    c["c_hsum"] = np.ascontiguousarray(hsum.transpose(1, 0, 2))
    c["c_hspread"] = np.ascontiguousarray(hsum.transpose(2, 0, 1))
    j = np.arange(NB)
    g = np.arange(SLOTS)
    ang = 2 * np.pi * np.outer(j, g) / (2 * NB)
    fwd = np.zeros((NB, SLOTS, 2))
    fwd[:, :, 0], fwd[:, :, 1] = np.cos(ang), -np.sin(ang)
    fwd[:, 0, 1] = (-1.0) ** j
    both = np.zeros((B, B, NB, 2 * SLOTS))
    for b in range(B):
        both[b, b] = fwd.reshape(NB, 2 * SLOTS)
    c["c_fwd"] = np.ascontiguousarray(both.reshape(B, B * NB, 2 * SLOTS).transpose(1, 0, 2)).astype(f)
    inv = np.zeros((SLOTS, 2, NB))
    inv[:, 0], inv[:, 1] = 2 * np.cos(ang.T), -2 * np.sin(ang.T)
    inv[0, 0], inv[0, 1] = 1.0, (-1.0) ** j
    c["c_inv"] = (inv.reshape(2 * SLOTS, NB) / (2 * NB)).astype(f)
    flt = np.zeros((2, 128, SLOTS, 2))
    flt[0, :NB, :, 0] = fwd[:, :, 0]
    flt[0, :NB, :, 1] = -fwd[:, :, 1]
    flt[1, :NB, :, 0] = fwd[:, :, 1]
    flt[1, :NB, :, 1] = fwd[:, :, 0]
    flt[0, :NB, 0, 1] = 0.0
    flt[1, :NB, 0, 0] = 0.0
    flt[1, :NB, 0, 1] = fwd[:, 0, 1]
    c["c_flt"] = np.ascontiguousarray(flt.reshape(2, 128, 2 * SLOTS).transpose(1, 0, 2)).astype(f)
    c["c_sign"] = ((-1.0) ** p).astype(f)[:, None].copy()
    c["c_quarter"] = np.full((128, NF), 0.25, f)
    tri = np.zeros((128, CH), f)
    tri[:, CH - 128:] = np.where(p[None, :] <= p[:, None], 0.0, -BIG)
    c["c_causal"] = tri
    c["c_rank"] = np.broadcast_to(MOE - np.arange(MOE), (128, MOE)).astype(f).copy()
    return c, at


def _lay_out(i):
    f = lambda n: np.asarray(i[n])
    t = np.ascontiguousarray
    c, at = _constants()
    a = dict(c)
    a["x"] = t(f("x").reshape(B, C, L))
    qkv, proj = f("L0_conv_qkv_w"), f("L0_conv_proj_w")
    a["na_w"] = t(np.concatenate([qkv.reshape(2, 3, C, C), proj[:, None]], 1).transpose(0, 1, 3, 2))
    a["na_b"] = t(np.concatenate([f("L0_conv_qkv_b").reshape(2, 3, C), f("L0_conv_proj_b")[:, None]], 1))
    a["na_wqk"] = t(np.concatenate([a["na_w"][:, :2].reshape(2, 2, C, 2, 64)] * 2, 4).transpose(0, 1, 3, 2, 4))
    a["na_bqk"] = t(np.concatenate([a["na_b"][:, :2].reshape(2, 2, 2, 64)] * 2, 3).transpose(0, 1, 3, 2))
    rpb = f("L0_conv_rpb").reshape(2, HEADS, (2 * KW - 1) ** 2)
    a["na_bias"] = t(rpb[:, :, at].transpose(0, 2, 3, 1, 4))
    a["ln_g"], a["ln_b"] = f("L0_conv_ln_g"), f("L0_conv_ln_b")
    a["c3_wqkv"] = t(f("L1_conv_w_qkv").reshape(3, C, C).transpose(2, 0, 1))
    wk = f("L1_conv_w_kernel").reshape(HEADS, K2, 3 * C // HEADS)
    col = np.zeros((3 * C, 128), np.float32)
    ch = np.arange(3 * C)
    for k in range(K2):
        col[ch, k * HEADS + ch // 96] = wk[ch // 96, k, ch % 96]
    a["c3_wker"] = t(col.reshape(3, C, 128).transpose(1, 0, 2))
    bk = np.zeros((128, 1), np.float32)
    bk[:K2 * HEADS, 0] = f("L1_conv_b_kernel").reshape(HEADS, K2).T.reshape(-1)
    a["c3_bker"] = bk
    a["c3_wproj"] = t(f("L1_conv_w_proj").T)
    a["alpha"], a["beta"] = f("L1_conv_alpha").reshape(1, 1), f("L1_conv_beta").reshape(1, 1)
    a["la_w"] = t(np.stack([f("L2_attn_Wq"), f("L2_attn_Wk"), f("L2_attn_Wv")], 1))
    a["la_b"] = t(np.stack([f("L2_attn_bq"), f("L2_attn_bk"), f("L2_attn_bv")], 1))
    a["sigma"] = f("L2_ffn_sigma").reshape(1, NF)
    phi = np.zeros((NF, R + L + 2 * R), np.float32)
    phi[:, R:R + L] = f("L2_ffn_phi").T
    rows = np.zeros((128, NF, 2 * R), np.float32)
    for blk in range(NB):
        rows[blk] = phi[:, blk * R + 1:blk * R + 1 + 2 * R]
    a["phi_blocks"] = rows
    a["m_u"] = t(f("L2_ffn_M_u").transpose(2, 0, 1, 3))
    a["m_plus"] = t(f("L2_ffn_M_phi_plus").transpose(2, 0, 1, 3))
    a["m_minus"] = t(f("L2_ffn_M_phi_minus").transpose(2, 0, 1, 3))
    a["log_weights"], a["gumbel"] = f("L2_ffn_log_weights").reshape(1, 4), f("L2_ffn_gumbel").reshape(1, 4)
    a["ca_w"] = t(np.stack([f("L3_attn_Wq").T, f("L3_attn_Wk").T, f("L3_attn_Wv").T], 1))
    a["router_w"], a["router_b"] = f("L3_ffn_router_w"), f("L3_ffn_router_b").reshape(1, MOE)
    a["expert_w"] = t(f("L3_ffn_expert_w").transpose(1, 0, 2))
    eb = np.zeros((128, C), np.float32)
    eb[:MOE] = f("L3_ffn_expert_b")
    a["expert_b"] = eb
    return a


def kernel(**inputs):
    import concourse.bacc as _bacc
    from concourse import mybir as _mybir
    from concourse.bass_utils import run_bass_kernel_spmd as _run

    nc = _bacc.Bacc("TRN2", target_bir_lowering=False, num_devices=1)
    arrays = {f"in_{n}": np.ascontiguousarray(v) for n, v in _lay_out(inputs).items()}
    T = {n[3:]: nc.dram_tensor(n, v.shape, _mybir.dt.from_np(v.dtype), kind="ExternalInput").ap()
         for n, v in arrays.items()}
    T["out"] = nc.dram_tensor("out_0", (B, C, L), _mybir.dt.float32, kind="ExternalOutput").ap()
    build_program(nc, T)
    r = _run(nc, [arrays], core_ids=[0])
    return np.asarray(r.results[0]["out_0"]).reshape(B, C, H, W)
```
